# Optimizing a Trainium2 kernel written in Bass

```python
import numpy as np
import jax
import jax.numpy as jnp

def _softmax(x, axis=-1):
    return jax.nn.softmax(x, axis=axis)

def _gelu(x):
    return jax.nn.gelu(x, approximate=True)

def _silu(x):
    return jax.nn.silu(x)

def _sigmoid(x):
    return jax.nn.sigmoid(x)

def _layernorm(x, axis=-1, eps=1e-05):
    m = jnp.mean(x, axis=axis, keepdims=True)
    v = jnp.var(x, axis=axis, keepdims=True)
    return (x - m) / jnp.sqrt(v + eps)

def _scatter_add(tgt, idx, src, axis=0):
    return tgt.at[idx].add(src)

def _segment_sum(src, seg, n):
    return jax.ops.segment_sum(src, seg, n)
kernel_name = 'mk_gnn_resnorm_d2_gnn_r8_e88338'

def setup_inputs(seed: int=0):
    np.random.seed(seed)
    _w = jnp.asarray

    def _rec_inputs():
        import jax
        import jax.numpy as jnp
        _gk = jax.random.key(seed)
        x = -0.0001126 + 1 * jax.random.normal(jax.random.fold_in(_gk, 1), (1250, 768), jnp.float32)
        src = jax.random.randint(jax.random.fold_in(_gk, 2), (20000,), 0, 1250, jnp.int32)
        dst = jax.random.randint(jax.random.fold_in(_gk, 3), (20000,), 0, 1250, jnp.int32)
        _o = jnp.argsort(dst, stable=True)
        src = src[_o]
        dst = dst[_o]
        return (x, src, dst)
    x, src, dst = _rec_inputs()

    def _L0_gnn_setup():
        import jax, jax.numpy as jnp
        import numpy as np
        N_NODES = 1250
        N_EDGES = 12500
        DIM = 768
        NEG_SLOPE = 0.2

        def gat_conv(x, src, dst, W, att_src, att_dst, bias, num_nodes):
            h = x @ W
            a_s = h @ att_src
            a_d = h @ att_dst
            e = jax.nn.leaky_relu(a_s[src] + a_d[dst], NEG_SLOPE)
            m = jax.ops.segment_max(e, dst, num_segments=num_nodes)
            e = jnp.exp(e - m[dst])
            denom = jax.ops.segment_sum(e, dst, num_segments=num_nodes)
            alpha = e / denom[dst]
            msg = alpha[:, None] * h[src]
            out = jax.ops.segment_sum(msg, dst, num_segments=num_nodes)
            return out + bias
        key = jax.random.key(seed)
        ks = jax.random.split(key, 12)
        s = 1.0 / np.sqrt(DIM)
        inp = {'x': jax.random.normal(ks[0], (N_NODES, DIM), dtype=jnp.float32), 'edge_index': jax.random.randint(ks[1], (2, N_EDGES), 0, N_NODES, dtype=jnp.int64), 'W1': jax.random.normal(ks[2], (DIM, DIM), dtype=jnp.float32) * s, 'att_src1': jax.random.normal(ks[3], (DIM,), dtype=jnp.float32) * s, 'att_dst1': jax.random.normal(ks[4], (DIM,), dtype=jnp.float32) * s, 'b1': jnp.zeros((DIM,), dtype=jnp.float32), 'W2': jax.random.normal(ks[5], (DIM, DIM), dtype=jnp.float32) * s, 'att_src2': jax.random.normal(ks[6], (DIM,), dtype=jnp.float32) * s, 'att_dst2': jax.random.normal(ks[7], (DIM,), dtype=jnp.float32) * s, 'b2': jnp.zeros((DIM,), dtype=jnp.float32)}
        return inp
    _L0_gnn_all = _L0_gnn_setup()
    _L0_gnn_in = {k: v for k, v in _L0_gnn_all.items() if k in ('W1', 'att_src1', 'att_dst1', 'b1', 'W2', 'att_src2', 'att_dst2', 'b2')}
    del _L0_gnn_all

    def _L1_gnn_setup():
        import jax, jax.numpy as jnp
        import numpy as np
        N_NODES = 1250
        N_EDGES = 10000
        IN_DIM, HID, OUT_DIM, HEADS = (768, 512, 768, 4)
        NEG_SLOPE = 0.2

        def _gat_layer(x, src, dst, W, a_src, a_dst, b, heads, d_out, concat):
            N = x.shape[0]
            h = (x @ W).reshape(N, heads, d_out)
            as_n = jnp.einsum('nhd,hd->nh', h, a_src)
            ad_n = jnp.einsum('nhd,hd->nh', h, a_dst)
            e = jax.nn.leaky_relu(as_n[src] + ad_n[dst], NEG_SLOPE)
            e_max = jax.lax.stop_gradient(jax.ops.segment_max(e, dst, num_segments=N))
            ex = jnp.exp(e - e_max[dst])
            denom = jax.ops.segment_sum(ex, dst, num_segments=N)
            alpha = ex / (denom[dst] + 1e-16)
            msg = alpha[:, :, None] * h[src]
            out = jax.ops.segment_sum(msg, dst, num_segments=N)
            out = out.reshape(N, heads * d_out) if concat else out.mean(axis=1)
            return out + b
        key = jax.random.key(seed)
        ks = jax.random.split(key, 10)
        g = 0.05
        return {'x': jax.random.normal(ks[0], (N_NODES, IN_DIM), jnp.float32), 'edge_index': jax.random.randint(ks[1], (2, N_EDGES), 0, N_NODES, jnp.int64), 'W1': jax.random.normal(ks[2], (IN_DIM, HEADS * HID), jnp.float32) * g, 'a1_src': jax.random.normal(ks[3], (HEADS, HID), jnp.float32) * g, 'a1_dst': jax.random.normal(ks[4], (HEADS, HID), jnp.float32) * g, 'b1': jnp.zeros((HEADS * HID,), jnp.float32), 'W2': jax.random.normal(ks[5], (HEADS * HID, OUT_DIM), jnp.float32) * g, 'a2_src': jax.random.normal(ks[6], (1, OUT_DIM), jnp.float32) * g, 'a2_dst': jax.random.normal(ks[7], (1, OUT_DIM), jnp.float32) * g, 'b2': jnp.zeros((OUT_DIM,), jnp.float32)}
    _L1_gnn_all = _L1_gnn_setup()
    _L1_gnn_in = {k: v for k, v in _L1_gnn_all.items() if k in ('W1', 'a1_src', 'a1_dst', 'b1', 'W2', 'a2_src', 'a2_dst', 'b2')}
    del _L1_gnn_all
    return {'x': x, 'src': src, 'dst': dst, 'L0_gnn_W1': _L0_gnn_in['W1'], 'L0_gnn_att_src1': _L0_gnn_in['att_src1'], 'L0_gnn_att_dst1': _L0_gnn_in['att_dst1'], 'L0_gnn_b1': _L0_gnn_in['b1'], 'L0_gnn_W2': _L0_gnn_in['W2'], 'L0_gnn_att_src2': _L0_gnn_in['att_src2'], 'L0_gnn_att_dst2': _L0_gnn_in['att_dst2'], 'L0_gnn_b2': _L0_gnn_in['b2'], 'L1_gnn_W1': _L1_gnn_in['W1'], 'L1_gnn_a1_src': _L1_gnn_in['a1_src'], 'L1_gnn_a1_dst': _L1_gnn_in['a1_dst'], 'L1_gnn_b1': _L1_gnn_in['b1'], 'L1_gnn_W2': _L1_gnn_in['W2'], 'L1_gnn_a2_src': _L1_gnn_in['a2_src'], 'L1_gnn_a2_dst': _L1_gnn_in['a2_dst'], 'L1_gnn_b2': _L1_gnn_in['b2']}

def reference(x, src, dst, L0_gnn_W1, L0_gnn_att_src1, L0_gnn_att_dst1, L0_gnn_b1, L0_gnn_W2, L0_gnn_att_src2, L0_gnn_att_dst2, L0_gnn_b2, L1_gnn_W1, L1_gnn_a1_src, L1_gnn_a1_dst, L1_gnn_b1, L1_gnn_W2, L1_gnn_a2_src, L1_gnn_a2_dst, L1_gnn_b2):
    import jax
    import jax.numpy as jnp

    def _L0_gnn_ref(x, edge_index, W1, att_src1, att_dst1, b1, W2, att_src2, att_dst2, b2):
        import jax, jax.numpy as jnp
        import numpy as np
        N_NODES = 1250
        N_EDGES = 12500
        DIM = 768
        NEG_SLOPE = 0.2

        def gat_conv(x, src, dst, W, att_src, att_dst, bias, num_nodes):
            h = x @ W
            a_s = h @ att_src
            a_d = h @ att_dst
            e = jax.nn.leaky_relu(a_s[src] + a_d[dst], NEG_SLOPE)
            m = jax.ops.segment_max(e, dst, num_segments=num_nodes)
            e = jnp.exp(e - m[dst])
            denom = jax.ops.segment_sum(e, dst, num_segments=num_nodes)
            alpha = e / denom[dst]
            msg = alpha[:, None] * h[src]
            out = jax.ops.segment_sum(msg, dst, num_segments=num_nodes)
            return out + bias
        n = x.shape[0]
        loops = jnp.arange(n, dtype=edge_index.dtype)
        src = jnp.concatenate([edge_index[0], loops])
        dst = jnp.concatenate([edge_index[1], loops])
        h = gat_conv(x, src, dst, W1, att_src1, att_dst1, b1, n)
        h = jax.nn.relu(h)
        out = gat_conv(h, src, dst, W2, att_src2, att_dst2, b2, n)
        return out

    def _L1_gnn_ref(x, edge_index, W1, a1_src, a1_dst, b1, W2, a2_src, a2_dst, b2):
        import jax, jax.numpy as jnp
        import numpy as np
        N_NODES = 1250
        N_EDGES = 10000
        IN_DIM, HID, OUT_DIM, HEADS = (768, 512, 768, 4)
        NEG_SLOPE = 0.2

        def _gat_layer(x, src, dst, W, a_src, a_dst, b, heads, d_out, concat):
            N = x.shape[0]
            h = (x @ W).reshape(N, heads, d_out)
            as_n = jnp.einsum('nhd,hd->nh', h, a_src)
            ad_n = jnp.einsum('nhd,hd->nh', h, a_dst)
            e = jax.nn.leaky_relu(as_n[src] + ad_n[dst], NEG_SLOPE)
            e_max = jax.lax.stop_gradient(jax.ops.segment_max(e, dst, num_segments=N))
            ex = jnp.exp(e - e_max[dst])
            denom = jax.ops.segment_sum(ex, dst, num_segments=N)
            alpha = ex / (denom[dst] + 1e-16)
            msg = alpha[:, :, None] * h[src]
            out = jax.ops.segment_sum(msg, dst, num_segments=N)
            out = out.reshape(N, heads * d_out) if concat else out.mean(axis=1)
            return out + b
        N = x.shape[0]
        loops = jnp.arange(N, dtype=edge_index.dtype)
        src = jnp.concatenate([edge_index[0], loops])
        dst = jnp.concatenate([edge_index[1], loops])
        h = _gat_layer(x, src, dst, W1, a1_src, a1_dst, b1, HEADS, HID, True)
        h = jax.nn.elu(h)
        out = _gat_layer(h, src, dst, W2, a2_src, a2_dst, b2, 1, OUT_DIM, False)
        return out
    edge_index = jnp.stack([src, dst])
    x = _layernorm(x + _L0_gnn_ref(x, edge_index, L0_gnn_W1, L0_gnn_att_src1, L0_gnn_att_dst1, L0_gnn_b1, L0_gnn_W2, L0_gnn_att_src2, L0_gnn_att_dst2, L0_gnn_b2), axis=-1)
    x = _layernorm(x + _L1_gnn_ref(x, edge_index, L1_gnn_W1, L1_gnn_a1_src, L1_gnn_a1_dst, L1_gnn_b1, L1_gnn_W2, L1_gnn_a2_src, L1_gnn_a2_dst, L1_gnn_b2), axis=-1)
    return x

_drawn_inputs = setup_inputs


def setup_inputs(seed=0):
    import zlib

    import numpy as np

    out = dict(_drawn_inputs(seed))
    spreads = {'L0_gnn_b1': (0.0, 0.1),
     'L0_gnn_b2': (0.0, 0.1),
     'L1_gnn_b1': (0.0, 0.1),
     'L1_gnn_b2': (0.0, 0.1)}
    factors = {'L0_gnn_att_dst1': 4.182, 'L0_gnn_att_src2': 4.723, 'L0_gnn_att_dst2': 37.132}
    for name, (base, spread) in spreads.items():
        noise = np.random.default_rng([zlib.crc32(name.encode()), seed]).standard_normal(out[name].shape)
        drawn = base * np.exp(spread * noise) if base else spread * noise
        out[name] = jnp.asarray(drawn.astype(out[name].dtype))
    for name, factor in factors.items():
        out[name] = (out[name] * factor).astype(out[name].dtype)
    return out
```

```python
import concourse.bass as bass
from concourse import mybir
from contextlib import ExitStack

N, E, D, HEADS, HID = 1250, 20000, 768, 4, 512
T = 125
NT = N // T
PAIRS = NT // 2
KD = D // 128
KH = HID // 128
HALF = D // 2
CP = 2 * T
NCP = E // CP
NEG = -3.0e38
SLOPE = 0.2
EPS = 1e-5
HW0, HW1 = D + 2, HID + 2
NATT = 3 + HEADS
LAST = NATT - 1


def gnn(nc, x, src, dst, W1a, s1a, d1a, b1a, W2a, s2a, d2a, b2a, W1b, s1b, d1b, b1b, W2b, s2b, d2b, b2b, out):
    f32, f32r, bf16, f16 = mybir.dt.float32, mybir.dt.float32r, mybir.dt.bfloat16, mybir.dt.float16
    i32, u16 = mybir.dt.int32, mybir.dt.uint16
    ALU, ACT, AX = mybir.AluOpType, mybir.ActivationFunctionType, mybir.AxisListType
    ctx = ExitStack()
    with ctx:
        def sb(name, shape, dt):
            return ctx.enter_context(nc.sbuf_tensor(name, shape, dt))

        def sem(name):
            return ctx.enter_context(nc.semaphore(name))

        def pair(name):
            return [sem(name + "0"), sem(name + "1")]

        mask_dram = nc.dram_tensor("mask_dram", (N, N), bf16).ap()
        h2_dram = nc.dram_tensor("h2_dram", (N, D), f32).ap()
        x1_dram = nc.dram_tensor("x1_dram", (N, D), f32).ap()

        CT = sb("CT", [128, NT * N], u16)
        mask = sb("mask", [128, N], bf16)
        tr_hi = sb("tr_hi", [128, 2, KD, T], f32r)
        tr_lo = sb("tr_lo", [128, 2, KD, T], f32r)
        nat = sb("nat", [128, 2, D], f32)
        hb = sb("hb", [128, 2 * NT * HW0], f32r)
        ring = sb("ring", [128, 2, D], f32)
        P = sb("P", [128, NT, CP], f32)
        p_hi = sb("p_hi", [128, 2, NT, T], f32r)
        p_lo = sb("p_lo", [128, 2, NT, T], f32r)
        r1 = sb("r1", [128, N], f32)
        r2 = sb("r2", [128, N], f32)
        arow = sb("arow", [128, 2 * D], f32)
        wb = sb("wb", [128, 2 * KD * D], f32r)
        stage = sb("stage", [128, 2, D], f32)
        junk = sb("junk", [128, D], f32)
        brow = sb("brow", [128, D], f32)
        ident = sb("ident", [128, 128], f32)
        ones = sb("ones", [128, T], f32)
        wc_raw = sb("wc_raw", [128, 52 + 52], f32)
        wc_hi = sb("wc_hi", [128, 52 + 52], f32r)
        wc_lo = sb("wc_lo", [128, 52 + 52], f32r)
        acol = sb("acol", [128, 3, NT, 2 * HEADS], f32)
        mtile = sb("mtile", [128, 2], f32)
        started = sb("started", [128, 1], f32)
        M = sb("M", [128, NT], f32)
        small = sb("small", [128, 6, NT], f32)
        col = sb("col", [128, 2, 6], f32)
        rstd = sb("rstd", [128, 2], f32)
        expo = sb("expo", [128, 1], f32)
        tab = sb("tab", [1, 3 * NT], i32)

        h0_hi = hb[:, 0:NT * HW0].rearrange("p (s f) -> p s f", f=HW0)
        h0_lo = hb[:, NT * HW0:2 * NT * HW0].rearrange("p (s f) -> p s f", f=HW0)
        h1_hi = hb[:, 0:NT * HW1].rearrange("p (s f) -> p s f", f=HW1)
        h1_lo = hb[:, NT * HW1:2 * NT * HW1].rearrange("p (s f) -> p s f", f=HW1)
        TAIL = 2 * NT * HW1
        w0_hi = wb[:, 0:KD * D].rearrange("p (k f) -> p k f", f=D)
        w0_lo = wb[:, KD * D:2 * KD * D].rearrange("p (k f) -> p k f", f=D)
        WH = KD * HID
        w1_hi = wb[:, 0:WH].rearrange("p (k f) -> p k f", f=HID)
        w1_lo = wb[:, WH:2 * WH].rearrange("p (k f) -> p k f", f=HID)
        w2_hi = wb[:, 2 * WH:3 * WH].rearrange("p (k f) -> p k f", f=D)
        w2_lo = hb[:, TAIL:TAIL + WH].rearrange("p (k f) -> p k f", f=D)
        CT3 = CT[:, :].rearrange("p (s d) -> p s d", d=N)
        flatP = P[:, :, :].rearrange("p s d -> p (s d)")
        iota = flatP[:, 0:625].bitcast(f16)
        oh_src = [flatP[:, 625:1250].bitcast(f16), flatP[:, 1250:1875].bitcast(f16), r2[:, 0:625].bitcast(f16)]
        oh_dst = [flatP[:, 1875:1938].bitcast(f16), flatP[:, 1938:2001].bitcast(f16), r2[:, 625:688].bitcast(f16)]
        zeros = flatP[:, 2001:2064].bitcast(f16)
        ecol = ring[:, 0, 0:4 * NCP].rearrange("p (q c) -> p q c", q=4)
        edge = ring[:, 1, 0:64]
        selfcol = ring[:, 1, 64:64 + NT]
        C = r1[:, :]
        CTw = CT[:, :].bitcast(i32)
        CTf = CT[:, :].bitcast(f32)
        dst_i, src_i = CTw[0:NCP, 0:CP], CTw[0:NCP, CP:2 * CP]
        dst_f, src_f = CTf[0:NCP, 2 * CP:3 * CP], CTf[0:NCP, 3 * CP:4 * CP]

        ps_o = ctx.enter_context(nc.psum_tensor("ps_o", [128, 4, 512], f32))
        ps_h2 = ctx.enter_context(nc.psum_tensor("ps_h2", [128, 2, 512], f32))
        ps_t = ctx.enter_context(nc.psum_tensor("ps_t", [128, 512], f32))
        ps_a = ctx.enter_context(nc.psum_tensor("ps_a", [128, 512], f32))
        ps_c = ps_o[:, 0:3, :].rearrange("p b f -> p (b f)")

        s_edges, s_x_const, s_conv, s_const = sem("s_edges"), sem("s_x_const"), sem("s_conv"), sem("s_const")
        s_etr, s_ecol, s_prep, s_tabps, s_tab = sem("s_etr"), sem("s_ecol"), sem("s_prep"), sem("s_tabps"), sem("s_tab")
        s_ltr, s_iota = sem("s_ltr"), sem("s_iota")
        s_oh, s_used, s_self, s_cdone = sem("s_oh"), sem("s_used"), sem("s_self"), sem("s_cdone")
        s_cev, s_mk, s_mst, s_ctr, s_ctev = sem("s_cev"), sem("s_mk"), sem("s_mst"), sem("s_ctr"), sem("s_ctev")
        s_wst, s_att, s_whi, s_wlo, s_wcol, s_wcs = pair("s_wst"), sem("s_att"), sem("s_whi"), sem("s_wlo"), sem("s_wcol"), sem("s_wcs")
        s_nat, s_tr, s_thi, s_tlo, s_tuse = pair("s_nat"), sem("s_tr"), sem("s_thi"), sem("s_tlo"), sem("s_tuse")
        s_oev, s_hhi, s_ones = sem("s_oev"), sem("s_hhi"), sem("s_ones")
        s_a, s_aev = sem("s_a"), sem("s_aev")
        s_ml, s_mx, s_mcol = sem("s_ml"), sem("s_mx"), sem("s_mcol")
        s_diag, s_row, s_rev, s_sm = sem("s_diag"), sem("s_row"), sem("s_rev"), sem("s_sm")
        s_arg, s_exp, s_p, s_phi, s_plo, s_agg = sem("s_arg"), sem("s_exp"), sem("s_p"), sem("s_phi"), sem("s_plo"), sem("s_agg")
        s_b, s_den, s_rd, s_eexp, s_emin, s_y = sem("s_b"), sem("s_den"), sem("s_rd"), sem("s_eexp"), sem("s_emin"), sem("s_y")
        s_h2ev, s_hst, s_rl, s_split = sem("s_h2ev"), pair("s_hst"), pair("s_rl"), sem("s_split")
        s_sum, s_mean, s_sq, s_var, s_pow, s_fin, s_xst = (sem("s_sum"), sem("s_mean"), sem("s_sq"), sem("s_var"),
                                                           sem("s_pow"), sem("s_fin"), pair("s_xst"))

        FINAL = (1, LAST)
        def head(j): return j - 2 if 2 <= j < LAST else None
        def h_phase(j): return j not in FINAL
        def hw(j): return HID if head(j) is not None else D
        def ky(j): return KH if head(j) is not None else KD
        def tb(j): return 0 if j == 0 else 2 * NT + 2 * NT * head(j)
        def tg(j): return tb(j) + NT
        def ob(j): return {0: 0, 1: 2 * NT, LAST: 3 * NT + 2 * NT * HEADS}[j] if head(j) is None else 3 * NT + 2 * NT * head(j)
        def og(j): return ob(j) + (NT if h_phase(j) else 0)
        def ah(j): return {0: 0, 2: 2 * NT}[j]
        def ag(j): return NT if j == 0 else (3 + head(j)) * NT
        def hh(j): return j * NT
        def h2b(j): return 0 if j == 0 else (1 + head(j)) * NT
        AS = {j: acol[0:T, min(j, 1) if j < 2 else (1 if j < LAST else 2), :, :] for j in range(NATT)}
        AS[0], AS[1] = acol[0:T, 0, :, 0:2], acol[0:T, 0, :, 2:4]
        AS[LAST] = acol[0:T, 2, :, 0:2]
        def as_of(j): return AS[j][:, :, 0 if head(j) is None else 2 * head(j)]
        def ad_of(j): return AS[j][:, :, 1 if head(j) is None else 2 * head(j) + 1]

        WCOL = {"W1a": 0, "W2a": 2 * KD, "W1b": 4 * KD, "W2b": 4 * KD + 2 * HEADS * KD}
        def wc(t, name, k, n): return t[:, WCOL[name] + n * k:WCOL[name] + n * (k + 1)]
        events = []
        def event(key, w, k0, n, c0, width, hi, lo, att, cols):
            events.append(dict(key=key, w=w, k0=k0, n=n, c0=c0, width=width, hi=hi, lo=lo, att=att, cols=cols,
                               first=sum(e["n"] for e in events),
                               att_first=sum(1 for e in events if e["att"]),
                               col_first=sum(2 * e["n"] for e in events if e["att"])))
        event("W1a", W1a, 0, KD, 0, D, w0_hi, w0_lo, (s1a, d1a, 0), lambda k: WCOL["W1a"] + 2 * k)
        event("W2a", W2a, 0, KD, 0, D, w0_hi, w0_lo, (s2a, d2a, 0), lambda k: WCOL["W2a"] + 2 * k)
        for g in range(HEADS):
            event("W1b_att%d" % g, W1b, 0, KD, HID * g, HID, w1_hi if g == 0 else None, w1_lo if g == 0 else None,
                  (s1b, d1b, g), lambda k, g=g: WCOL["W1b"] + 2 * HEADS * k + 2 * g)
        for g in range(HEADS):
            event("W2b%d" % g, W2b, KH * g, KH, 0, D, w2_hi, w2_lo, (s2b, d2b, 0),
                  lambda k, g=g: WCOL["W2b"] + 2 * (KH * g + k))
            if g + 1 < HEADS:
                event("W1b%d" % (g + 1), W1b, 0, KD, HID * (g + 1), HID, w1_hi, w1_lo, None, None)
        EV = {e["key"]: e for e in events}
        def done(key): return EV[key]["first"] + EV[key]["n"]
        AT = {0: ["W2a"], 1: ["W1b_att%d" % g for g in range(HEADS)], LAST: []}
        for g in range(HEADS):
            AT[2 + g] = ["W2b%d" % g] + (["W1b%d" % (g + 1)] if g + 1 < HEADS else [])
        def w_free(key):
            if key == "W1a": return 0
            if key == "W2a": return NT
            if key.startswith("W1b_att"): return 2 * NT
            g = int(key[3:])
            return 2 * NT + 2 * NT * g if key.startswith("W2b") else 2 * NT + 2 * NT * (g - 1) + NT
        BIAS = [b1a, b2a] + [b1b] * HEADS + [b2b]
        ROUNDS = [(0, 4), (4, 4), (8, 2)]
        NROW = 3 * len(ROUNDS)
        def rl_split(j): return 0 if j == 1 else (2 + HEADS - 1) * PAIRS
        def rl_final(j): return rl_split(j) + PAIRS
        def rl_head(j): return (1 + head(j)) * PAIRS
        def hst(j): return 0 if j == 0 else (1 + head(j)) * PAIRS
        NSM = 6

        def pairs(eng, body, first=0, last=PAIRS):
            body(first)
            with eng.Fori(first + 1, last - 1, 1) as i:
                body(i)
            body(last - 1)

        def rows(i, u): return bass.ds(i * CP + u * T, T)
        def tile_of(i, u): return bass.ds(2 * i + u, 1)

        block = ctx.enter_context(nc.Block())

        @block.sync
        def _(sp):
            sp.dma_start(dst_i, dst.rearrange("(c e) -> c e", e=CP)).then_inc(s_edges, 16)
            sp.dma_start(src_i, src.rearrange("(c e) -> c e", e=CP)).then_inc(s_edges, 16)

            def weights(key):
                ev = EV[key]
                w = ev["width"]
                if ev["att"]:
                    va, vd, g = ev["att"]
                    a = ev["att_first"]
                    if key != "W1a":
                        sp.wait_ge(s_wcol, ev["col_first"])
                    if key in ("W2a", "W1b_att0", "W2b0", "W2b1", "W2b2", "W2b3"):
                        j = {"W2a": 0, "W1b_att0": 1}.get(key) if key[0:3] != "W2b" else 2 + int(key[3:])
                        sp.wait_ge(s_mx, NT * (j + 1))
                    for n, v in enumerate((va, vd)):
                        if key[0:2] == "W2" and key[2] == "b":
                            row = v[0:1, :]
                        elif key[0:3] == "W1b":
                            row = v[g:g + 1, :]
                        else:
                            row = v.rearrange("(a f) -> a f", a=1)
                        width = D if w == D else HID
                        sp.dma_start(arow[:, n * D:n * D + width], row.partition_broadcast(128)
                                     if False else row.broadcast_to([128, width])).then_inc(s_att, 16)
                for c in range(ev["n"]):
                    g = ev["first"] + c
                    if g >= 2:
                        sp.wait_ge(s_wlo, g - 1)
                    k = ev["k0"] + c
                    sp.dma_start(stage[:, g % 2, 0:w], ev["w"][128 * k:128 * (k + 1), ev["c0"]:ev["c0"] + w])\
                      .then_inc(s_wst[g % 2], 16)

            def bias(j):
                if j:
                    sp.wait_ge(s_oev, og(j - 1) + NT)
                w = hw(j)
                b = BIAS[j][w * head(j):w * (head(j) + 1)] if head(j) is not None else BIAS[j]
                sp.dma_start(brow[:, 0:w], b.rearrange("(a f) -> a f", a=1).broadcast_to([128, w])).then_inc(s_b, 16)

            def mask_load(j, i, u):
                if not (isinstance(i, int) and j == 0 and i == 0 and u == 0):
                    sp.wait_ge(s_mx, NT * j + 2 * i + u)
                sp.dma_start(mask[0:T, :], mask_dram[rows(i, u), :]).then_inc(s_ml, 16)

            weights("W1a")
            for t in range(NT):
                sp.wait_ge(s_mk, t + 1)
                sp.dma_start(mask_dram[T * t:T * (t + 1), :], mask[0:T, :]).then_inc(s_mst, 16)
            sp.wait_ge(s_mst, 16 * NT)
            for j in range(NATT):
                pairs(sp, lambda i: [mask_load(j, i, u) for u in range(2)])
                bias(j)
                for key in AT[j]:
                    weights(key)
            for u in range(2):
                sp.wait_ge(s_hst[u], 16 * (1 + HEADS) * PAIRS)
                sp.wait_ge(s_xst[u], 16 * 2 * PAIRS)

        @block.gpsimd
        def _(pool):
            g = nc.gpsimd
            g.memset(ident[:, :], 0.0).then_inc(s_iota, 1)
            g.memset(edge[0:NT, 20:30], 1.0).then_inc(s_iota, 1)
            g.memset(ones[:, :], 1.0)
            g.memset(expo[:, :], -0.5)
            g.memset(zeros[:, :], 0.0)
            g.iota(iota[:, :], pattern=[[1, N]], base=0, channel_multiplier=0, allow_small_or_imprecise_dtypes=True)
            g.iota(selfcol[:, :], pattern=[[T, NT]], base=0, channel_multiplier=1, allow_small_or_imprecise_dtypes=True)
            g.iota(edge[:, 0:NT], pattern=[[T, NT]], base=0, channel_multiplier=0, allow_small_or_imprecise_dtypes=True)
            g.iota(edge[:, 10:11], pattern=[[1, 1]], base=-NCP, channel_multiplier=1, allow_small_or_imprecise_dtypes=True)
            g.iota(edge[:, 11:12], pattern=[[1, 1]], base=1, channel_multiplier=1, allow_small_or_imprecise_dtypes=True)
            pool.wait_ge(s_iota, 2)
            g.affine_select(out=ident[:, :], in_=ident[:, :], compare_op=ALU.not_equal, fill=1.0, base=0,
                            pattern=[[-1, 128]], channel_multiplier=1)
            g.affine_select(out=edge[0:NT, 20:30], in_=edge[0:NT, 20:30], compare_op=ALU.is_gt, fill=0.0, base=0,
                            pattern=[[1, NT]], channel_multiplier=-1).then_inc(s_const, 1)

            def load_tile(srcd, j, i, u):
                t = tb(j) + 2 * i + u
                if not (j == 0 and isinstance(i, int) and i == 0):
                    pool.wait_ge(s_tr, 2 * (t - 1))
                pool.dma_start(nat[0:T, u, :], srcd[rows(i, u), :]).then_inc(s_nat[u], 16)

            def h2_load(j, i, u):
                pool.wait_ge(s_hst[u], 16 * (hst(j) + i))
                pool.dma_start(ring[0:T, u, :], h2_dram[rows(i, u), :]).then_inc(s_rl[u], 16)

            def h2_store(j, i, u):
                pool.wait_ge(s_h2ev, h2b(j) + 2 * i + u + 1)
                pool.dma_start(h2_dram[rows(i, u), :], ring[0:T, u, :]).then_inc(s_hst[u], 16)

            for j in range(NATT):
                f = NT * (j == LAST)
                if h_phase(j):
                    if j == 2:
                        for u in range(2):
                            pool.wait_ge(s_xst[u], 16 * PAIRS)
                    pairs(pool, lambda i: [load_tile(x if j == 0 else x1_dram, j, i, u) for u in range(2)])
                    more = head(j) is not None and head(j) > 0
                    if more:
                        for u in range(2):
                            h2_load(j, 0, u)

                    def step(i):
                        for u in range(2):
                            h2_store(j, i, u)
                            if more and not (isinstance(i, int) and i == PAIRS - 1):
                                h2_load(j, i + 1, u)
                    pairs(pool, step)
                else:
                    for u in range(2):
                        pool.wait_ge(s_hst[u], 16 * (PAIRS if j == 1 else (1 + HEADS) * PAIRS))

                    def split_load(i):
                        for u in range(2):
                            if not (isinstance(i, int) and i == 0):
                                pool.wait_ge(s_split, f + 2 * i + u - 1)
                            pool.dma_start(ring[0:T, u, :], h2_dram[rows(i, u), :]).then_inc(s_rl[u], 16)
                    pairs(pool, split_load)

                    def res_load(i, u):
                        if isinstance(i, int) and i == 0:
                            pool.wait_ge(s_split, f + NT)
                        pool.dma_start(ring[0:T, u, :], (x if j == 1 else x1_dram)[rows(i, u), :]).then_inc(s_rl[u], 16)

                    for u in range(2):
                        res_load(0, u)

                    def finish(i):
                        for u in range(2):
                            n = f + 2 * i + u
                            pool.wait_ge(s_var, n + 1)
                            g.tensor_tensor(rstd[0:T, u:u + 1], col[0:T, u, 5:6], expo[0:T, :], ALU.pow).then_inc(s_pow, 1)
                            if not (isinstance(i, int) and i == PAIRS - 1):
                                res_load(i + 1, u)
                            pool.wait_ge(s_fin, n + 1)
                            pool.dma_start((x1_dram if j == 1 else out)[rows(i, u), :], nat[0:T, u, :]).then_inc(s_xst[u], 16)
                    pairs(pool, finish)

        @block.scalar
        def _(act):
            a = nc.scalar.activation

            def weights(key):
                ev = EV[key]
                if ev["hi"] is None:
                    return
                if w_free(key):
                    act.wait_ge(s_tuse, w_free(key))
                if key == "W2b0":
                    act.wait_ge(s_agg, 2 * NT)
                for c in range(ev["n"]):
                    g = ev["first"] + c
                    act.wait_ge(s_wst[g % 2], 16 * (g // 2 + 1))
                    a(ev["hi"][:, c, :], stage[:, g % 2, 0:ev["width"]], ACT.Copy).then_inc(s_whi, 1)

            def transposed(t, u, K, func):
                n = K // 2
                for r in range(2):
                    act.wait_ge(s_tr, 2 * t + r + 1)
                    if r == 0 and not (isinstance(t, int) and t < 2):
                        act.wait_ge(s_tuse, t - 1)
                    a(tr_hi[:, u, n * r:n * (r + 1), :], ps_t[:, 0:n * T].rearrange("p (k n) -> p k n", n=T), func)\
                        .then_inc(s_thi, 1)

            def h_tile(j, i, u):
                t = tb(j) + 2 * i + u
                w = hw(j)
                h = h0_hi if w == D else h1_hi
                act.wait_ge(s_tuse, t + 1)
                if w == D:
                    o = h[0:T, tile_of(i, u), 0:D].rearrange("p a (b f) -> p (a b) f", b=2)
                    a(o, ps_o[0:T, 2 * u:2 * u + 2, 0:HALF], ACT.Copy).then_inc(s_hhi, 1)
                else:
                    a(h[0:T, tile_of(i, u), 0:w].rearrange("p a f -> p (a f)"), ps_o[0:T, 2 * u, 0:w], ACT.Copy)\
                        .then_inc(s_hhi, 1)

            def row(j, k):
                rr = NROW * j + k
                t0, n = ROUNDS[k % 3]
                to = (arow, r1, r2)[k // 3]
                act.wait_ge(s_row, rr + 1)
                a(to[0:T, T * t0:T * (t0 + n)], ps_h2[0:T, rr % 2, 0:T * n], ACT.Copy).then_inc(s_rev, 1)

            def exps(j, i, half):
                for s in range(PAIRS * half, PAIRS * (half + 1)):
                    act.wait_ge(s_arg, NT * (PAIRS * j + i) + s + 1)
                    a(P[0:T, s, :], P[0:T, s, :], ACT.Exp, bias=small[0:T, 5, s:s + 1]).then_inc(s_exp, 1)

            def p_high(j, i, u):
                p = NT * j + 2 * i + u
                act.wait_ge(s_p, NT * (PAIRS * j + i + 1))
                if not (isinstance(i, int) and i == 0 and j == 0):
                    act.wait_ge(s_agg, p - 1)
                a(p_hi[0:T, u, :, :], P[0:T, :, T * u:T * (u + 1)], ACT.Copy).then_inc(s_phi, 1)

            def evac(j, i, u):
                n = NT * j + 2 * i + u
                if j in FINAL:
                    f = NT * (j == LAST) + 2 * i + u
                    act.wait_ge(s_mean, f + 1)
                    a(junk[0:T, :], nat[0:T, u, :], ACT.Square, bias=col[0:T, u, 3:4], accum_out=col[0:T, u, 4:5])\
                        .then_inc(s_sq, 1)
                elif head(j) is not None:
                    act.wait_ge(s_oev, og(j) + 2 * i + u + 1)
                    a(junk[0:T, 0:HID], nat[0:T, u, 0:HID], ACT.Exp).then_inc(s_eexp, 1)

            def aggregate(j):
                exps(j, 0, 0)
                exps(j, 0, 1)
                p_high(j, 0, 0)
                p_high(j, 0, 1)
                for key in AT[j]:
                    weights(key)
                func = ACT.Relu if j == 0 else ACT.Copy

                def body(i):
                    peeled = isinstance(i, int)
                    more = not (peeled and i == PAIRS - 1)
                    for u, before in ((0, (i - 1, 1)), (1, (i, 0))):
                        if not (peeled and i == 0 and u == 0):
                            evac(j, *before)
                        if more:
                            exps(j, i + 1, u)
                        if j not in FINAL and not (peeled and i == 0 and u == 0):
                            transposed(tg(j) + 2 * before[0] + before[1], before[1], ky(j), func)
                    if more:
                        p_high(j, i + 1, 0)
                        p_high(j, i + 1, 1)
                pairs(act, body)
                evac(j, PAIRS - 1, 1)
                if j not in FINAL:
                    transposed(tg(j) + NT - 1, 1, ky(j), func)

            weights("W1a")
            for t in range(NT):
                act.wait_ge(s_cdone, t + 1)
                if t:
                    act.wait_ge(s_ctr, 3 * t)
                    act.wait_ge(s_mk, t)
                a(C[0:T, :], ps_c[0:T, 0:N], ACT.Copy).then_inc(s_cev, 1)
            for j in range(NATT):
                if h_phase(j):
                    ahead = j > 2
                    if ahead:
                        for k in range(3):
                            row(j, k)

                    transposed(tb(j), 0, KD, ACT.Copy)

                    def body(i):
                        for u in range(2):
                            if not (isinstance(i, int) and i == PAIRS - 1 and u == 1):
                                transposed(tb(j) + 2 * i + u + 1, 1 - u, KD, ACT.Copy)
                            h_tile(j, i, u)
                    pairs(act, body)
                    if not ahead:
                        for k in range(3):
                            row(j, k)
                else:
                    f = NT * (j == LAST)
                    for k in range(3):
                        row(j, k)
                    act.wait_ge(s_agg, NT * j)
                    if j == LAST:
                        act.wait_ge(s_tuse, 2 * NT + 2 * NT * HEADS)

                    def body(i):
                        for u in range(2):
                            act.wait_ge(s_rl[u], 16 * (rl_split(j) + i + 1))
                            a(h0_hi[0:T, tile_of(i, u), 0:D].rearrange("p a f -> p (a f)"), ring[0:T, u, :], ACT.Copy)\
                                .then_inc(s_hhi, 1)
                    pairs(act, body)
                for k in range(3, NROW):
                    row(j, k)
                aggregate(j)

        @block.vector
        def _(dve):
            v = nc.vector

            def weights(key):
                ev = EV[key]
                w = ev["width"]
                for c in range(ev["n"]):
                    g = ev["first"] + c
                    if ev["att"]:
                        if c == 0:
                            dve.wait_ge(s_att, 32 * (ev["att_first"] + 1))
                        dve.wait_ge(s_wst[g % 2], 16 * (g // 2 + 1))
                        to = ev["cols"](c)
                        for n in range(2):
                            m = ev["col_first"] + 2 * c + n
                            if m:
                                dve.wait_ge(s_wcol, m)
                            ins = v.tensor_tensor_reduce(out=junk[:, 0:w], in0=stage[:, g % 2, 0:w],
                                                         in1=arow[:, n * D:n * D + w], scale=1.0, scalar=0.0,
                                                         op0=ALU.mult, op1=ALU.add, accum_out=wc_raw[:, to + n:to + n + 1])
                            ins.then_inc(s_wcol, 1)
                    if ev["hi"] is not None:
                        dve.wait_ge(s_whi, whi[g] + 1)
                        v.tensor_tensor(ev["lo"][:, c, :], stage[:, g % 2, 0:w], ev["hi"][:, c, :].bitcast(f32),
                                        ALU.subtract).then_inc(s_wlo, 1)
                    else:
                        dve.wait_ge(s_wcol, ev["col_first"] + 2 * c + 2)
                        v.memset(started[:, :], 0.0).then_inc(s_wlo, 1)

            whi, n_hi = {}, 0
            for e in events:
                for c in range(e["n"]):
                    if e["hi"] is not None:
                        whi[e["first"] + c] = n_hi
                        n_hi += 1

            def split_cols(lo, hi, n):
                dve.wait_ge(s_wcol, cols_done[n])
                v.tensor_copy(wc_hi[:, lo:hi], wc_raw[:, lo:hi]).then_inc(s_wcs, 1)
                dve.wait_ge(s_wcs, 2 * n + 1)
                v.tensor_tensor(wc_lo[:, lo:hi], wc_raw[:, lo:hi], wc_hi[:, lo:hi].bitcast(f32), ALU.subtract)\
                    .then_inc(s_wcs, 1)

            cols_done = [EV["W1a"]["col_first"] + 2 * KD, EV["W2a"]["col_first"] + 2 * KD,
                         EV["W1b_att%d" % (HEADS - 1)]["col_first"] + 2 * KD] + \
                        [EV["W2b%d" % g]["col_first"] + 2 * KH for g in range(HEADS)]

            def cols_of(j):
                if j == 0: split_cols(WCOL["W2a"], WCOL["W1b"], 1)
                if j == 1: split_cols(WCOL["W1b"], WCOL["W2b"], 2)
                if head(j) is not None:
                    lo = WCOL["W2b"] + 2 * KH * head(j)
                    split_cols(lo, lo + 2 * KH, 3 + head(j))

            def low(t, u, K, relu):
                n = K // 2
                for r in range(2):
                    dve.wait_ge(s_thi, 2 * t + r + 1)
                    o = tr_lo[:, u, n * r:n * (r + 1), :]
                    p = ps_t[:, 0:n * T].rearrange("p (k n) -> p k n", n=T)
                    h = tr_hi[:, u, n * r:n * (r + 1), :].bitcast(f32)
                    if relu:
                        v.scalar_tensor_tensor(out=o, in0=p, scalar=0.0, in1=h, op0=ALU.max, op1=ALU.subtract)\
                            .then_inc(s_tlo, 1)
                    else:
                        v.tensor_tensor(o, p, h, ALU.subtract).then_inc(s_tlo, 1)

            def h_low(j, i, u):
                w = hw(j)
                dve.wait_ge(s_hhi, hh(j) + 2 * i + u + 1)
                if w == D:
                    def v3(t): return t[0:T, tile_of(i, u), 0:D].rearrange("p a (b f) -> p (a b) f", b=2)
                    v.tensor_tensor(v3(h0_lo), ps_o[0:T, 2 * u:2 * u + 2, 0:HALF], v3(h0_hi).bitcast(f32),
                                    ALU.subtract).then_inc(s_oev, 1)
                else:
                    def v2(t): return t[0:T, tile_of(i, u), 0:w].rearrange("p a f -> p (a f)")
                    v.tensor_tensor(v2(h1_lo), ps_o[0:T, 2 * u, 0:w], v2(h1_hi).bitcast(f32),
                                    ALU.subtract).then_inc(s_oev, 1)

            def a_cols(j, where, i, u):
                if where == "H":
                    n, to, c = ah(j), AS[j], (2 if j == 0 else 2 * HEADS)
                else:
                    n, to, c = ag(j), AS[1 if j == 0 else LAST], 2
                dve.wait_ge(s_a, n + 2 * i + u + 1)
                o = to[:, tile_of(i, u), 0:c].rearrange("p a c -> p (a c)")
                if where == "G" and head(j):
                    v.tensor_tensor(o, o, ps_a[0:T, 0:c], ALU.add).then_inc(s_aev, 1)
                else:
                    v.tensor_copy(o, ps_a[0:T, 0:c]).then_inc(s_aev, 1)

            def diag(j, k):
                rr = NROW * j + k
                t0, n = ROUNDS[k % 3]
                what = (as_of(j), small[0:T, 2, :], small[0:T, 3, :])[k // 3]
                if rr >= 5:
                    dve.wait_ge(s_row, rr - 4)
                o = flatP[0:T, 500 * (rr % 5):500 * (rr % 5) + n * T].rearrange("p (n c) -> p n c", c=T)
                v.tensor_tensor(o, ident[0:T, 0:T].unsqueeze(1).broadcast_to([T, n, T]),
                                what[:, t0:t0 + n].unsqueeze(2).broadcast_to([T, n, T]), ALU.mult).then_inc(s_diag, 1)

            def maxes(j, i, u):
                n = NT * j + 2 * i + u
                if isinstance(i, int) and i == 0 and u == 0:
                    dve.wait_ge(s_rev, NROW * j + 3)
                dve.wait_ge(s_ml, 16 * (n + 1))
                v.memset(started[0:T, :], 0.0)
                v.tensor_tensor_reduce(out=junk[0:T, 0:N // 2].bitcast(bf16), in0=arow[0:T, 0:N], in1=mask[0:T, :],
                                       scale=1.0, scalar=NEG, op0=ALU.add, op1=ALU.max,
                                       accum_out=mtile[0:T, u:u + 1]).then_inc(s_mx, 1)
                dve.wait_ge(s_mx, n + 1)
                v.tensor_copy(M[0:T, tile_of(i, u)], mtile[0:T, u:u + 1]).then_inc(s_mcol, 1)

            def columns(j):
                n = NSM * j
                sm = lambda q: small[0:T, q, :]
                dve.wait_ge(s_mcol, NT * (j + 1))
                v.tensor_tensor(sm(0), ad_of(j), M[0:T, :], ALU.add).then_inc(s_sm, 1)
                dve.wait_ge(s_sm, n + 1)
                v.scalar_tensor_tensor(out=sm(1), in0=sm(0), scalar=SLOPE, in1=sm(0), op0=ALU.mult, op1=ALU.max).then_inc(s_sm, 1)
                dve.wait_ge(s_sm, n + 2)
                v.tensor_tensor(sm(2), ad_of(j), sm(1), ALU.subtract).then_inc(s_sm, 1)
                v.scalar_tensor_tensor(out=sm(3), in0=ad_of(j), scalar=SLOPE, in1=sm(1), op0=ALU.mult, op1=ALU.subtract).then_inc(s_sm, 1)
                v.tensor_scalar(sm(4), as_of(j), 1.0 - SLOPE, None, ALU.mult).then_inc(s_sm, 1)
                v.tensor_scalar(sm(5), as_of(j), SLOPE, None, ALU.mult).then_inc(s_sm, 1)
                dve.wait_ge(s_sm, n + 6)

            def args(j, i, half):
                if half == 0 and not (isinstance(i, int) and i == 0):
                    dve.wait_ge(s_plo, NT * j + 2 * i)
                for s in range(PAIRS * half, PAIRS * (half + 1)):
                    v.scalar_tensor_tensor(out=P[0:T, s, :], in0=r1[0:T, bass.ds(i * CP, CP)], scalar=small[0:T, 4, s:s + 1],
                                           in1=r2[0:T, bass.ds(i * CP, CP)], op0=ALU.add, op1=ALU.max).then_inc(s_arg, 1)

            def counts(j, i, half):
                for s in range(PAIRS * half, PAIRS * (half + 1)):
                    dve.wait_ge(s_exp, NT * (PAIRS * j + i) + s + 1)
                    v.scalar_tensor_tensor(out=P[0:T, s, :], in0=P[0:T, s, :], scalar=1.0,
                                           in1=CT3[0:T, s, bass.ds(i * CP, CP)], op0=ALU.min, op1=ALU.mult).then_inc(s_p, 1)

            def p_low(j, i, u):
                p = NT * j + 2 * i + u
                dve.wait_ge(s_phi, p + 1)
                v.tensor_tensor(p_lo[0:T, u, :, :], P[0:T, :, T * u:T * (u + 1)], p_hi[0:T, u, :, :].bitcast(f32),
                                ALU.subtract).then_inc(s_plo, 1)

            def norm(j, i, u):
                n = NT * j + 2 * i + u
                w = hw(j) // 2
                dve.wait_ge(s_agg, n + 1)
                if j >= 2:
                    v.tensor_scalar(col[0:T, u, 0:1], ps_o[0:T, 2 * u + 1, w:w + 1], 1e-16, None, ALU.add).then_inc(s_den, 1)
                    dve.wait_ge(s_den, n - 2 * NT + 1)
                    v.reciprocal(col[0:T, u, 1:2], col[0:T, u, 0:1]).then_inc(s_rd, 1)
                else:
                    v.reciprocal(col[0:T, u, 1:2], ps_o[0:T, 2 * u + 1, w:w + 1]).then_inc(s_rd, 1)
                dve.wait_ge(s_rd, n + 1)
                if isinstance(i, int) and i == 0 and u == 0:
                    dve.wait_ge(s_b, 16 * (j + 1))
                if j in FINAL and not (isinstance(i, int) and i == 0 and j == 1):
                    if not (isinstance(i, int) and i == 0):
                        dve.wait_ge(s_xst[u], 16 * (PAIRS * (j == LAST) + i))
                v3 = lambda t: t.rearrange("p (b f) -> p b f", b=2)
                v.scalar_tensor_tensor(out=v3(nat[0:T, u, 0:2 * w]), in0=ps_o[0:T, 2 * u:2 * u + 2, 0:w], scalar=col[0:T, u, 1:2],
                                       in1=v3(brow[0:T, 0:2 * w]), op0=ALU.mult, op1=ALU.add).then_inc(s_oev, 1)

            def stage1(j, i, u):
                norm(j, i, u)
                if j in FINAL:
                    f = NT * (j == LAST) + 2 * i + u
                    dve.wait_ge(s_oev, og(j) + 2 * i + u + 1)
                    dve.wait_ge(s_rl[u], 16 * (rl_final(j) + i + 1))
                    v.scalar_tensor_tensor(out=nat[0:T, u, :], in0=nat[0:T, u, :], scalar=1.0, in1=ring[0:T, u, :],
                                           op0=ALU.mult, op1=ALU.add, accum_out=col[0:T, u, 2:3]).then_inc(s_sum, 1)
                    dve.wait_ge(s_sum, f + 1)
                    v.tensor_scalar(col[0:T, u, 3:4], col[0:T, u, 2:3], -1.0 / D, None, ALU.mult).then_inc(s_mean, 1)

            def stage2(j, i, u):
                if j in FINAL:
                    f = NT * (j == LAST) + 2 * i + u
                    dve.wait_ge(s_sq, f + 1)
                    v.tensor_scalar(col[0:T, u, 5:6], col[0:T, u, 4:5], 1.0 / D, EPS, ALU.mult, ALU.add).then_inc(s_var, 1)
                elif head(j) is not None:
                    e = NT * (j - 2) + 2 * i + u
                    dve.wait_ge(s_eexp, e + 1)
                    v.tensor_scalar(junk[0:T, 0:HID], junk[0:T, 0:HID], 1.0, -1.0, ALU.min, ALU.add).then_inc(s_emin, 1)
                    dve.wait_ge(s_emin, e + 1)
                    v.scalar_tensor_tensor(out=nat[0:T, u, 0:HID], in0=nat[0:T, u, 0:HID], scalar=0.0, in1=junk[0:T, 0:HID],
                                           op0=ALU.max, op1=ALU.add).then_inc(s_y, 1)

            def stage3(j, i, u):
                if j in FINAL:
                    return
                low(tg(j) + 2 * i + u, u, ky(j), j == 0)

            def stage4(j, i, u):
                if j in FINAL:
                    f = NT * (j == LAST) + 2 * i + u
                    dve.wait_ge(s_pow, f + 1)
                    v.tensor_scalar(nat[0:T, u, :], nat[0:T, u, :], col[0:T, u, 3:4], rstd[0:T, u:u + 1], ALU.add, ALU.mult)\
                        .then_inc(s_fin, 1)
                    return
                a_cols(j, "G", i, u)
                t = tg(j) + 2 * i + u
                dve.wait_ge(s_tuse, t + 1)
                if head(j):
                    dve.wait_ge(s_rl[u], 16 * (rl_head(j) + i + 1))
                    r3 = ring[0:T, u, :].rearrange("p (b f) -> p b f", b=2)
                    v.tensor_tensor(r3, r3, ps_h2[0:T, :, 0:HALF], ALU.add).then_inc(s_h2ev, 1)
                else:
                    if not (isinstance(i, int) and i == 0 and j == 0):
                        dve.wait_ge(s_hst[u], 16 * (hst(j) + i))
                    v.tensor_copy(ring[0:T, u, :].rearrange("p (b f) -> p b f", b=2), ps_h2[0:T, :, 0:HALF])\
                        .then_inc(s_h2ev, 1)

            def aggregate(j):
                for half in range(2):
                    args(j, 0, half)
                    counts(j, 0, half)
                p_low(j, 0, 0)
                p_low(j, 0, 1)
                for key in AT[j]:
                    weights(key)
                cols_of(j)

                def body(i):
                    peeled = isinstance(i, int)
                    more = not (peeled and i == PAIRS - 1)
                    for u, before, before2 in ((0, (i - 1, 1), (i - 1, 0)), (1, (i, 0), (i - 1, 1))):
                        has = not (peeled and i == 0 and u == 0)
                        has2 = not (peeled and i == 0)
                        if has:
                            stage1(j, *before)
                        if has2:
                            stage4(j, *before2)
                        if more:
                            args(j, i + 1, u)
                        if has:
                            stage2(j, *before)
                        if more:
                            counts(j, i + 1, u)
                        if has:
                            stage3(j, *before)
                    if more:
                        p_low(j, i + 1, 0)
                        p_low(j, i + 1, 1)
                pairs(dve, body)
                stage1(j, PAIRS - 1, 1)
                stage4(j, PAIRS - 1, 0)
                stage2(j, PAIRS - 1, 1)
                stage3(j, PAIRS - 1, 1)
                stage4(j, PAIRS - 1, 1)

            dve.sem_inc(s_oh, 2 * NCP)
            dve.wait_ge(s_edges, 32)
            v.tensor_copy(dst_f, dst_i)
            v.tensor_copy(src_f, src_i).then_inc(s_conv, 1)
            dve.wait_ge(s_conv, 1)
            v.tensor_reduce(out=edge[0:NCP, 12:13], in_=dst_f, axis=AX.X, op=ALU.min)
            v.tensor_reduce(out=edge[0:NCP, 13:14], in_=dst_f, axis=AX.X, op=ALU.max).then_inc(s_prep, 1)
            dve.wait_ge(s_prep, 1)
            dve.wait_ge(s_const, 1)
            ed = lambda a, b, p=NCP: edge[0:p, a:b]
            v.tensor_scalar(ed(30, 40), ed(0, NT), ed(13, 14), None, ALU.is_le)
            v.tensor_scalar(ed(40, 50), ed(0, NT), float(T - 1), ed(12, 13), ALU.add, ALU.is_ge).then_inc(s_prep, 1)
            dve.wait_ge(s_prep, 2)
            v.tensor_tensor(ed(30, 40), ed(30, 40), ed(40, 50), ALU.mult).then_inc(s_prep, 1)
            dve.wait_ge(s_prep, 3)
            v.tensor_scalar(ed(40, 50), ed(30, 40), ed(10, 11), None, ALU.mult)
            v.tensor_scalar(ed(50, 60), ed(30, 40), ed(11, 12), None, ALU.mult).then_inc(s_prep, 1)
            dve.wait_ge(s_etr, 1)
            v.tensor_copy(ecol[0:T], ps_t[0:T, 0:4 * NCP].rearrange("p (q c) -> p q c", q=4)).then_inc(s_ecol, 1)
            dve.wait_ge(s_ltr, 1)
            ps_lim = ps_a
            v.tensor_reduce(out=ed(14, 15, NT), in_=ps_lim[0:NT, 0:NCP], axis=AX.X, op=ALU.min)
            v.tensor_reduce(out=ed(15, 16, NT), in_=ps_lim[0:NT, NCP:2 * NCP], axis=AX.X, op=ALU.max).then_inc(s_prep, 1)
            dve.wait_ge(s_prep, 5)
            v.tensor_scalar(ed(14, 15, NT), ed(14, 15, NT), float(NCP), float(NCP - 1), ALU.add, ALU.min).then_inc(s_prep, 1)
            dve.wait_ge(s_prep, 6)
            v.scalar_tensor_tensor(out=ed(15, 16, NT), in0=ed(14, 15, NT), scalar=1.0, in1=ed(15, 16, NT), op0=ALU.add, op1=ALU.max)\
                .then_inc(s_prep, 1)
            dve.wait_ge(s_prep, 7)
            v.tensor_tensor(ed(16, 17, NT), ed(15, 16, NT), ed(14, 15, NT), ALU.subtract).then_inc(s_prep, 1)
            dve.wait_ge(s_tabps, 1)
            v.tensor_copy(edge[0:1, 20:30], ps_a[0:1, 192:192 + NT])
            v.tensor_copy(edge[0:1, 30:50], ps_a[0:1, 160:180]).then_inc(s_prep, 1)
            dve.wait_ge(s_prep, 9)
            v.tensor_copy(tab[0:1, 0:2 * NT], edge[0:1, 30:50])
            v.scalar_tensor_tensor(out=tab[0:1, 2 * NT:3 * NT], in0=edge[0:1, 20:30], scalar=float(NCP), in1=edge[0:1, 30:40],
                                   op0=ALU.add, op1=ALU.subtract).then_inc(s_tab, 1)
            weights("W1a")
            split_cols(0, WCOL["W2a"], 0)
            v.memset(h0_hi[0:T, :, D:D + 2].bitcast(f32), 1.0)
            v.memset(h0_lo[0:T, :, D:D + 2].bitcast(f32), 0.0).then_inc(s_ones, 1)
            dve.wait_ge(s_tab, 1)

            def from_counts(t):
                dve.wait_ge(s_cev, t + 1)
                if t:
                    dve.wait_ge(s_mst, 16 * t)
                v.tensor_scalar(mask[0:T, :], C[0:T, :], 0.5, NEG, ALU.is_lt, ALU.mult).then_inc(s_mk, 1)
                for r, (t0, n) in enumerate(ROUNDS):
                    rr = 3 * t + r
                    dve.wait_ge(s_ctr, rr + 1)
                    v.tensor_copy(CT3[0:T, t0:t0 + n, T * t:T * (t + 1)],
                                  ps_h2[0:T, rr % 2, 0:n * T].rearrange("p (n c) -> p n c", c=T)).then_inc(s_ctev, 1)

            dve.wait_ge(s_ecol, 1)
            for t in range(NT):
                lo = dve.value_load(tab[0:1, t:t + 1], min_val=0, max_val=NCP - 1)
                hi = dve.value_load(tab[0:1, NT + t:NT + t + 1], min_val=1, max_val=NCP)
                sh = dve.value_load(tab[0:1, 2 * NT + t:2 * NT + t + 1], min_val=1, max_val=NCP * NT)
                with dve.Fori(lo, hi, 1) as c:
                    for q in range(2):
                        dve.wait_ge(s_used, 2 * (c + sh) + q + 1)
                        v.tensor_scalar(oh_dst[q][0:T, 0:T], iota[0:T, T * t:T * (t + 1)], ecol[0:T, q, bass.ds(c, 1)], None, ALU.is_equal)
                        v.tensor_scalar(oh_src[q][0:T, :], iota[0:T, :], ecol[0:T, 2 + q, bass.ds(c, 1)], None, ALU.is_equal)\
                            .then_inc(s_oh, 1)
                if t:
                    dve.wait_ge(s_cdone, t)
                v.tensor_scalar(oh_dst[2][0:T, 0:T], iota[0:T, T * t:T * (t + 1)], selfcol[0:T, t:t + 1], None, ALU.is_equal)
                v.tensor_scalar(oh_src[2][0:T, :], iota[0:T, :], selfcol[0:T, t:t + 1], None, ALU.is_equal).then_inc(s_self, 1)
                if t:
                    from_counts(t - 1)
            from_counts(NT - 1)

            for j in range(NATT):
                if h_phase(j):
                    ahead = j > 2
                    if ahead:
                        for k in range(3):
                            diag(j, k)
                    if j == 2:
                        dve.wait_ge(s_agg, 2 * NT)
                        v.memset(h1_hi[0:T, :, HID:HID + 2].bitcast(f32), 1.0)
                        v.memset(h1_lo[0:T, :, HID:HID + 2].bitcast(f32), 0.0).then_inc(s_ones, 1)

                    low(tb(j), 0, KD, False)

                    def body(i):
                        for u in range(2):
                            if not (isinstance(i, int) and i == PAIRS - 1 and u == 1):
                                low(tb(j) + 2 * i + u + 1, 1 - u, KD, False)
                            if not ahead:
                                a_cols(j, "H", i, u)
                            h_low(j, i, u)
                            if ahead:
                                maxes(j, i, u)
                    pairs(dve, body)
                    if not ahead:
                        dve.wait_ge(s_aev, ah(j) + NT)
                        for k in range(3):
                            diag(j, k)
                        pairs(dve, lambda i: [maxes(j, i, u) for u in range(2)])
                else:
                    f = NT * (j == LAST)
                    dve.wait_ge(s_aev, ag(j - 1) + NT)
                    for k in range(3):
                        diag(j, k)
                    if j == LAST:
                        dve.wait_ge(s_tuse, 2 * NT + 2 * NT * HEADS)
                        v.memset(h0_hi[0:T, :, D:D + 2].bitcast(f32), 1.0)
                        v.memset(h0_lo[0:T, :, D:D + 2].bitcast(f32), 0.0).then_inc(s_ones, 1)

                    def body(i):
                        for u in range(2):
                            dve.wait_ge(s_hhi, hh(j) + 2 * i + u + 1)
                            h = lambda t: t[0:T, tile_of(i, u), 0:D].rearrange("p a f -> p (a f)")
                            v.tensor_tensor(h(h0_lo), ring[0:T, u, :], h(h0_hi).bitcast(f32), ALU.subtract).then_inc(s_split, 1)
                            maxes(j, i, u)
                    pairs(dve, body)
                columns(j)
                for k in range(3, NROW):
                    diag(j, k)
                dve.wait_ge(s_rev, NROW * (j + 1))
                aggregate(j)

        @block.tensor
        def _(pe):
            mm = nc.tensor.matmul

            def three(o, ah_, al_, bh_, bl_, first, last):
                mm(o, ah_, bh_, start=first, stop=False)
                mm(o, ah_, bl_, start=False, stop=False)
                return mm(o, al_, bh_, start=False, stop=last)

            def transposes(t, u, K, ready):
                n = K // 2
                for r in range(2):
                    if r == 0:
                        ready()
                    pe.wait_ge(s_tlo, 2 * t + r) if not (isinstance(t, int) and t == 0 and r == 0) else None
                    for k in range(n):
                        kk = n * r + k
                        ins = nc.tensor.transpose(ps_t[:, T * k:T * (k + 1)], nat[0:T, u, 128 * kk:128 * (kk + 1)], ident[0:T, 0:T])
                    ins.then_inc(s_tr, 1)

            def cols(name, k0, K, n, u, nth):
                if nth is not None:
                    pe.wait_ge(s_aev, nth)
                for k in range(K):
                    ins = three(ps_a[0:T, 0:n], tr_hi[:, u, k, :], tr_lo[:, u, k, :], wc(wc_hi, name, k0 + k, n),
                                wc(wc_lo, name, k0 + k, n), k == 0, k == K - 1)
                ins.then_inc(s_a, 1)

            def product(o, K, u, w_hi, w_lo, parts):
                for k in range(K):
                    for a_, b_, st, sp_ in ((tr_hi, w_hi, k == 0, False), (tr_hi, w_lo, False, False), (tr_lo, w_hi, False, k == K - 1)):
                        for b, (c0, c1) in enumerate(parts):
                            ins = mm(o[:, b, 0:c1 - c0], a_[:, u, k, :], b_[:, k, c0:c1], start=st, stop=sp_)
                ins.then_inc(s_tuse, 1)

            def sum_tile(j, i, u, middle):
                p, o = NT * j + 2 * i + u, og(j) + 2 * i + u
                w = hw(j) // 2
                h_hi, h_lo = (h0_hi, h0_lo) if hw(j) == D else (h1_hi, h1_lo)
                pe.wait_ge(s_plo, p + 1)
                pe.wait_ge(s_oev, o - 1)
                for s in range(NT):
                    for a_, b_, st, sp_ in ((p_hi, h_hi, s == 0, False), (p_hi, h_lo, False, False), (p_lo, h_hi, False, s == NT - 1)):
                        for b, (c0, c1) in enumerate(((0, w), (w, 2 * w + 2))):
                            ins = mm(ps_o[0:T, 2 * u + b, 0:c1 - c0], a_[0:T, u, s, :], b_[0:T, s, c0:c1], start=st, stop=sp_)
                    if s == NT - 1:
                        ins.then_inc(s_agg, 1)
                    if s == NT // 2 - 1 and middle:
                        middle()

            def row(j, k):
                rr = NROW * j + k
                t0, n = ROUNDS[k % 3]
                pe.wait_ge(s_diag, rr + 1)
                if rr >= 2:
                    pe.wait_ge(s_rev, rr - 1)
                if k == 0:
                    if j == 0:
                        pe.wait_ge(s_ctev, 3 * NT)
                    else:
                        pe.wait_ge(s_h2ev, h2b(j - 1) + NT if j != 2 else NT)
                mm(ps_h2[0:T, rr % 2, 0:n * T], ones_sq[0:T, :], flatP[0:T, 500 * (rr % 5):500 * (rr % 5) + n * T],
                   start=True, stop=True).then_inc(s_row, 1)

            ones_sq = ones

            def y_ready(j, i, u):
                def f():
                    if head(j) is None:
                        pe.wait_ge(s_oev, og(j) + 2 * i + u + 1)
                    else:
                        pe.wait_ge(s_y, NT * head(j) + 2 * i + u + 1)
                return f

            def next_h(j, i, u):
                t = tg(j) + 2 * i + u
                pe.wait_ge(s_tlo, 2 * t + 2)
                key, name = ("W2a", "W2a") if j == 0 else ("W2b%d" % head(j), "W2b")
                if isinstance(i, int) and i == 0 and u == 0:
                    pe.wait_ge(s_wlo, done(key))
                    pe.wait_ge(s_wcs, 2 * (2 if j == 0 else 4 + head(j)))
                    pe.wait_ge(s_rev, NROW * (j + 1))
                cols(name, 0 if j == 0 else KH * head(j), ky(j), 2, u, ag(j) + 2 * i + u)
                n = h2b(j) + 2 * i + u
                if not (isinstance(i, int) and i == 0 and u == 0 and j == 0):
                    pe.wait_ge(s_h2ev, n)
                hi, lo = (w0_hi, w0_lo) if j == 0 else (w2_hi, w2_lo)
                product(ps_h2[0:T], ky(j), u, hi, lo, ((0, HALF), (HALF, D)))

            pe.sem_inc(s_used, 2 * NCP + 2)
            pe.wait_ge(s_const, 1)
            pe.wait_ge(s_conv, 1)
            for q, t in enumerate((dst_f, dst_f, src_f, src_f)):
                ins = nc.tensor.transpose(ps_t[0:T, NCP * q:NCP * (q + 1)], t[:, T * (q % 2):T * (q % 2 + 1)], ident[0:NCP, 0:NCP])
            ins.then_inc(s_etr, 1)
            pe.wait_ge(s_prep, 4)
            nc.tensor.transpose(ps_a[0:NT, 0:NCP], edge[0:NCP, 40:50], ident[0:NCP, 0:NCP])
            nc.tensor.transpose(ps_a[0:NT, NCP:2 * NCP], edge[0:NCP, 50:60], ident[0:NCP, 0:NCP]).then_inc(s_ltr, 1)
            pe.wait_ge(s_prep, 8)
            mm(ps_a[0:1, 160:170], edge[0:NT, 14:15], ident[0:NT, 0:NT], start=True, stop=True)
            mm(ps_a[0:1, 170:180], edge[0:NT, 15:16], ident[0:NT, 0:NT], start=True, stop=True)
            mm(ps_a[0:1, 192:202], edge[0:NT, 16:17], edge[0:NT, 20:30], start=True, stop=True).then_inc(s_tabps, 1)
            pe.wait_ge(s_tab, 1)

            BANKS = ((0, 512), (512, 1024), (1024, N))

            def transpose_counts(t):
                pe.wait_ge(s_cev, t + 1)
                for r, (t0, n) in enumerate(ROUNDS):
                    rr = 3 * t + r
                    if rr >= 2:
                        pe.wait_ge(s_ctev, rr - 1)
                    for q in range(n):
                        ins = nc.tensor.transpose(ps_h2[0:T, rr % 2, T * q:T * (q + 1)], C[0:T, T * (t0 + q):T * (t0 + q + 1)],
                                                  ident[0:T, 0:T])
                    ins.then_inc(s_ctr, 1)

            for t in range(NT):
                lo = pe.value_load(tab[0:1, t:t + 1], min_val=0, max_val=NCP - 1)
                hi = pe.value_load(tab[0:1, NT + t:NT + t + 1], min_val=1, max_val=NCP)
                sh = pe.value_load(tab[0:1, 2 * NT + t:2 * NT + t + 1], min_val=1, max_val=NCP * NT)
                if t:
                    pe.wait_ge(s_cev, t)
                for b, (c0, c1) in enumerate(BANKS):
                    mm(ps_o[0:T, b, 0:c1 - c0], zeros[0:T, 0:T], iota[0:T, c0:c1], start=True, stop=False)
                with pe.Fori(lo, hi, 1) as c:
                    for q in range(2):
                        pe.wait_ge(s_oh, 2 * (c + sh) + q + 1)
                        for b, (c0, c1) in enumerate(BANKS):
                            ins = mm(ps_o[0:T, b, 0:c1 - c0], oh_dst[q][0:T, 0:T], oh_src[q][0:T, c0:c1], start=False, stop=False)
                        ins.then_inc(s_used, 1)
                pe.wait_ge(s_self, t + 1)
                for b, (c0, c1) in enumerate(BANKS):
                    ins = mm(ps_o[0:T, b, 0:c1 - c0], oh_dst[2][0:T, 0:T], oh_src[2][0:T, c0:c1], start=False, stop=True)
                ins.then_inc(s_cdone, 1)
                if t:
                    transpose_counts(t - 1)
            transpose_counts(NT - 1)
            pe.wait_ge(s_ecol, 1)

            for j in range(NATT):
                if h_phase(j):
                    ahead = j > 2
                    if ahead:
                        for k in range(3):
                            row(j, k)
                    w = hw(j)
                    hi, lo = (w0_hi, w0_lo) if j == 0 else (w1_hi, w1_lo)
                    parts = ((0, HALF), (HALF, D)) if j == 0 else ((0, HID),)
                    n_nat = 0 if j == 0 else PAIRS * (1 + head(j))

                    def nat_ready(i, u):
                        return lambda: pe.wait_ge(s_nat[u], 16 * (n_nat + i + 1))

                    def h_tile(i, u):
                        t, o = tb(j) + 2 * i + u, ob(j) + 2 * i + u
                        first = isinstance(i, int) and i == 0
                        pe.wait_ge(s_tlo, 2 * t + 2)
                        if first and u == 0:
                            pe.wait_ge(s_wlo, done({0: "W1a", 2: "W1b_att%d" % (HEADS - 1)}.get(j, "W1b%d" % head(j) if j > 2 else "")))
                            if j == 0:
                                pe.wait_ge(s_cev, NT)
                            pe.wait_ge(s_wcs, 2 if j == 0 else 6)
                        if not ahead:
                            cols("W1a" if j == 0 else "W1b", 0, KD, 2 if j == 0 else 2 * HEADS, u,
                                 None if j == 0 and first and u == 0 else ah(j) + 2 * i + u)
                        if not (j == 0 and first):
                            pe.wait_ge(s_oev, o - 1)
                        product(ps_o[0:T, 2 * u:2 * u + 2], KD, u, hi, lo, parts)

                    transposes(tb(j), 0, KD, nat_ready(0, 0))

                    def body(i):
                        transposes(tb(j) + 2 * i + 1, 1, KD, nat_ready(i, 1))
                        h_tile(i, 0)
                        if not (isinstance(i, int) and i == PAIRS - 1):
                            transposes(tb(j) + 2 * i + 2, 0, KD, nat_ready(i + 1, 0))
                        h_tile(i, 1)
                    pairs(pe, body)
                    if not ahead:
                        for k in range(3):
                            row(j, k)
                    pe.wait_ge(s_oev, ob(j) + NT)
                else:
                    for k in range(3):
                        row(j, k)
                    pe.wait_ge(s_split, NT * (1 if j == 1 else 2))
                pe.wait_ge(s_ones, {0: 1, 1: 1, LAST: 3}.get(j, 2))
                for k in range(3, NROW):
                    row(j, k)

                def body(i):
                    peeled = isinstance(i, int)
                    for u, b in ((0, (i - 1, 1)), (1, (i, 0))):
                        has = j not in FINAL and not (peeled and i == 0 and u == 0)
                        tt = tg(j) + 2 * b[0] + b[1] if has else None
                        sum_tile(j, i, u, (lambda: transposes(tt, b[1], ky(j), y_ready(j, *b))) if has else None)
                        if has:
                            next_h(j, *b)
                pairs(pe, body)
                if j not in FINAL:
                    transposes(tg(j) + NT - 1, 1, ky(j), y_ready(j, PAIRS - 1, 1))
                    next_h(j, PAIRS - 1, 1)


_INS = ["x", "src", "dst",
        "L0_gnn_W1", "L0_gnn_att_src1", "L0_gnn_att_dst1", "L0_gnn_b1", "L0_gnn_W2", "L0_gnn_att_src2", "L0_gnn_att_dst2", "L0_gnn_b2",
        "L1_gnn_W1", "L1_gnn_a1_src", "L1_gnn_a1_dst", "L1_gnn_b1", "L1_gnn_W2", "L1_gnn_a2_src", "L1_gnn_a2_dst", "L1_gnn_b2"]


def kernel(**inputs):
    import numpy as np
    import concourse.bacc as bacc
    from concourse import mybir as mb
    from concourse.bass_utils import run_bass_kernel_spmd as run

    nc = bacc.Bacc("TRN2", target_bir_lowering=False, num_devices=1)
    arrays, args = {}, []
    for name in _INS:
        a = np.ascontiguousarray(inputs[name])
        arrays["in_" + name] = a
        args.append(nc.dram_tensor("in_" + name, a.shape, mb.dt.from_np(a.dtype), kind="ExternalInput").ap())
    args.append(nc.dram_tensor("out_0", (N, D), mb.dt.float32, kind="ExternalOutput").ap())
    gnn(nc, *args)
    r = run(nc, [arrays], core_ids=[0])
    return r.results[0]["out_0"]
```

```python
import concourse.bass as bass
from concourse import mybir
from contextlib import ExitStack

N, E, D, HEADS, HID = 1250, 20000, 768, 4, 512
T = 125
NT = N // T
PAIRS = NT // 2
KD = D // 128
KH = HID // 128
HALF = D // 2
CP = 2 * T
NCP = E // CP
NEG = -3.0e38
SLOPE = 0.2
EPS = 1e-5
AC = 2 * HEADS
HW0, HW1 = D + 2, HID + 2
NATT = 3 + HEADS
LAST = NATT - 1


def gnn(nc, x, src, dst, W1a, s1a, d1a, b1a, W2a, s2a, d2a, b2a, W1b, s1b, d1b, b1b, W2b, s2b, d2b, b2b, out):
    f32, f32r, bf16, f16 = mybir.dt.float32, mybir.dt.float32r, mybir.dt.bfloat16, mybir.dt.float16
    i32, u16 = mybir.dt.int32, mybir.dt.uint16
    ALU, ACT, AX = mybir.AluOpType, mybir.ActivationFunctionType, mybir.AxisListType
    ctx = ExitStack()
    with ctx:
        def sb(name, shape, dt):
            return ctx.enter_context(nc.sbuf_tensor(name, shape, dt))

        def sem(name):
            return ctx.enter_context(nc.semaphore(name))

        def pair(name):
            return [sem(name + "0"), sem(name + "1")]

        mask_dram = nc.dram_tensor("mask_dram", (N, N), bf16).ap()
        h2_dram = nc.dram_tensor("h2_dram", (N, D), f32).ap()
        x1_dram = nc.dram_tensor("x1_dram", (N, D), f32).ap()

        CT = sb("CT", [128, NT * N], u16)
        mask = sb("mask", [128, 2, N], bf16)
        tr_hi = sb("tr_hi", [128, 2, KD, T], f32r)
        tr_lo = sb("tr_lo", [128, 2, KD, T], f32r)
        nat = sb("nat", [128, 2, D], f32)
        hb = sb("hb", [128, 2 * NT * HW0], f32r)
        ring = sb("ring", [128, 2, D], f32)
        P = sb("P", [128, NT, CP], f32)
        p_hi = sb("p_hi", [128, 2, NT, T], f32r)
        p_lo = sb("p_lo", [128, 2, NT, T], f32r)
        prow = sb("prow", [128, 2, CP], f32)
        arow = sb("arow", [128, N], f32)
        attv = sb("attv", [128, 2, D], f32)
        wb = sb("wb", [128, 2 * KD * (HID + AC) + KH * (D + 2)], f32r)
        stage = sb("stage", [128, 2, D], f32)
        junk = sb("junk", [128, D], f32)
        brow = sb("brow", [128, D], f32)
        ident = sb("ident", [128, 128], f32)
        ones = sb("ones", [128, T], f32)
        wc_raw = sb("wc_raw", [128, 52 + 52], f32)
        acol = sb("acol", [128, 3, NT, 2 * HEADS], f32)
        mtile = sb("mtile", [128, 2], f32)
        started = sb("started", [128, 3], f32)
        M = sb("M", [128, NT], f32)
        asc = sb("asc", [128, 2, NT], f32)
        pc = sb("pc", [128, 4, 2], f32)
        col = sb("col", [128, 2, 6], f32)
        rstd = sb("rstd", [128, 2], f32)
        expo = sb("expo", [128, 1], f32)
        tab = sb("tab", [1, 3 * NT], i32)

        h0_hi = hb[:, 0:NT * HW0].rearrange("p (s f) -> p s f", f=HW0)
        h0_lo = hb[:, NT * HW0:2 * NT * HW0].rearrange("p (s f) -> p s f", f=HW0)
        h1_hi = hb[:, 0:NT * HW1].rearrange("p (s f) -> p s f", f=HW1)
        h1_lo = hb[:, NT * HW1:2 * NT * HW1].rearrange("p (s f) -> p s f", f=HW1)
        TAIL = 2 * NT * HW1
        WA, WB, WC = KD * (D + 2), KD * (HID + AC), KH * (D + 2)
        w0_hi = wb[:, 0:WA].rearrange("p (k f) -> p k f", f=D + 2)
        w0_lo = wb[:, WA:2 * WA].rearrange("p (k f) -> p k f", f=D + 2)
        w1_hi = wb[:, 0:WB].rearrange("p (k f) -> p k f", f=HID + AC)
        w1_lo = wb[:, WB:2 * WB].rearrange("p (k f) -> p k f", f=HID + AC)
        w2_hi = wb[:, 2 * WB:2 * WB + WC].rearrange("p (k f) -> p k f", f=D + 2)
        w2_lo = hb[:, TAIL:TAIL + WC].rearrange("p (k f) -> p k f", f=D + 2)
        CT3 = CT[:, :].rearrange("p (s d) -> p s d", d=N)
        flatP = P[:, :, :].rearrange("p s d -> p (s d)")
        iota = flatP[:, 0:625].bitcast(f16)
        oh_src = [flatP[:, 625:1250].bitcast(f16), flatP[:, 1250:1875].bitcast(f16), brow[:, 0:625].bitcast(f16)]
        oh_dst = [flatP[:, 1875:1938].bitcast(f16), flatP[:, 1938:2001].bitcast(f16), brow[:, 625:688].bitcast(f16)]
        zeros = flatP[:, 2001:2064].bitcast(f16)
        ecol = ring[:, 0, 0:4 * NCP].rearrange("p (q c) -> p q c", q=4)
        edge = ring[:, 1, 0:64]
        selfcol = ring[:, 1, 64:64 + NT]
        C = arow[:, :]
        CTw = CT[:, :].bitcast(i32)
        CTf = CT[:, :].bitcast(f32)
        dst_i, src_i = CTw[0:NCP, 0:CP], CTw[0:NCP, CP:2 * CP]
        dst_f, src_f = CTf[0:NCP, 2 * CP:3 * CP], CTf[0:NCP, 3 * CP:4 * CP]

        ps_o = ctx.enter_context(nc.psum_tensor("ps_o", [128, 4, 512], f32))
        ps_h2 = ctx.enter_context(nc.psum_tensor("ps_h2", [128, 2, 512], f32))
        ps_t = ctx.enter_context(nc.psum_tensor("ps_t", [128, 512], f32))
        ps_a = ctx.enter_context(nc.psum_tensor("ps_a", [128, 512], f32))
        ps_c = ps_o[:, 0:3, :].rearrange("p b f -> p (b f)")

        s_edges, s_x_const, s_conv, s_const = sem("s_edges"), sem("s_x_const"), sem("s_conv"), sem("s_const")
        s_etr, s_ecol, s_prep, s_tabps, s_tab = sem("s_etr"), sem("s_ecol"), sem("s_prep"), sem("s_tabps"), sem("s_tab")
        s_ltr, s_iota = sem("s_ltr"), sem("s_iota")
        s_oh, s_used, s_self, s_cdone = sem("s_oh"), sem("s_used"), sem("s_self"), sem("s_cdone")
        s_cev, s_mk, s_mst, s_ctr, s_ctev = sem("s_cev"), sem("s_mk"), pair("s_mst"), sem("s_ctr"), sem("s_ctev")
        s_wst, s_att, s_whi, s_wlo, s_wcol, s_wcs, s_hcol = (pair("s_wst"), sem("s_att"), sem("s_whi"), sem("s_wlo"), sem("s_wcol"),
                                                                 sem("s_wcs"), sem("s_hcol"))
        s_nat, s_tr, s_thi, s_tlo, s_tuse = pair("s_nat"), sem("s_tr"), sem("s_thi"), sem("s_tlo"), sem("s_tuse")
        s_oev, s_hhi, s_ones = sem("s_oev"), sem("s_hhi"), sem("s_ones")
        s_ml, s_mx, s_mcol = pair("s_ml"), sem("s_mx"), sem("s_mcol")
        s_diag, s_row, s_rev, s_as = sem("s_diag"), sem("s_row"), sem("s_rev"), sem("s_as")
        s_pc, s_pdiag, s_prow, s_prev = sem("s_pc"), sem("s_pdiag"), sem("s_prow"), sem("s_prev")
        s_arg, s_exp, s_p, s_phi, s_plo, s_agg = sem("s_arg"), sem("s_exp"), sem("s_p"), sem("s_phi"), sem("s_plo"), sem("s_agg")
        s_b, s_den, s_rd, s_eexp, s_emin, s_y = sem("s_b"), sem("s_den"), sem("s_rd"), sem("s_eexp"), sem("s_emin"), sem("s_y")
        s_h2ev, s_hst, s_rl, s_split = sem("s_h2ev"), pair("s_hst"), pair("s_rl"), sem("s_split")
        s_sum, s_mean, s_sq, s_var, s_pow, s_fin, s_xst = (sem("s_sum"), sem("s_mean"), sem("s_sq"), sem("s_var"),
                                                           sem("s_pow"), sem("s_fin"), pair("s_xst"))

        FINAL = (1, LAST)
        def head(j): return j - 2 if 2 <= j < LAST else None
        def h_phase(j): return j not in FINAL
        def hw(j): return HID if head(j) is not None else D
        def ky(j): return KH if head(j) is not None else KD
        def tb(j): return 0 if j == 0 else 2 * NT + 2 * NT * head(j)
        def tg(j): return tb(j) + NT
        def ob(j): return {0: 0, 1: 2 * NT, LAST: 3 * NT + 2 * NT * HEADS}[j] if head(j) is None else 3 * NT + 2 * NT * head(j)
        def og(j): return ob(j) + (NT if h_phase(j) else 0)
        def ahead(j): return j > 2 and j != LAST
        def hh(j): return j * NT
        def h2b(j): return 0 if j == 0 else (1 + head(j)) * NT
        AS = {j: acol[0:T, min(j, 1) if j < 2 else (1 if j < LAST else 2), :, :] for j in range(NATT)}
        AS[0], AS[1] = acol[0:T, 0, :, 0:2], acol[0:T, 0, :, 2:4]
        AS[LAST] = acol[0:T, 2, :, 0:2]
        def as_of(j): return AS[j][:, :, 0 if head(j) is None else 2 * head(j)]
        def ad_of(j): return AS[j][:, :, 1 if head(j) is None else 2 * head(j) + 1]

        WCOL = {"W1a": 0, "W2a": 2 * KD, "W1b": 4 * KD, "W2b": 4 * KD + 2 * HEADS * KD}
        events = []
        def event(key, w, k0, n, c0, width, hi, lo, att, cols):
            events.append(dict(key=key, w=w, k0=k0, n=n, c0=c0, width=width, hi=hi, lo=lo, att=att, cols=cols,
                               first=sum(e["n"] for e in events),
                               att_first=sum(1 for e in events if e["att"]),
                               col_first=sum(2 * e["n"] for e in events if e["att"])))
        event("W1a", W1a, 0, KD, 0, D, w0_hi, w0_lo, (s1a, d1a, 0), lambda k: WCOL["W1a"] + 2 * k)
        event("W2a", W2a, 0, KD, 0, D, w0_hi, w0_lo, (s2a, d2a, 0), lambda k: WCOL["W2a"] + 2 * k)
        for g in list(range(1, HEADS)) + [0]:
            event("W1b0" if g == 0 else "W1b_att%d" % g, W1b, 0, KD, HID * g, HID, w1_hi if g == 0 else None,
                  w1_lo if g == 0 else None, (s1b, d1b, g), lambda k, g=g: WCOL["W1b"] + AC * k + 2 * g)
        for g in range(HEADS):
            event("W2b%d" % g, W2b, KH * g, KH, 0, D, w2_hi, w2_lo, (s2b, d2b, 0),
                  lambda k, g=g: WCOL["W2b"] + 2 * (KH * g + k))
            if g + 1 < HEADS:
                event("W1b%d" % (g + 1), W1b, 0, KD, HID * (g + 1), HID, w1_hi, w1_lo, None, None)
        EV = {e["key"]: e for e in events}
        def done(key): return EV[key]["first"] + EV[key]["n"]
        AT = {0: (["W2a"], ["W1b_att1"], ["W1b_att2"]), 1: (["W1b_att3"], ["W1b0"], []), LAST: ([], [], [])}
        for g in range(HEADS):
            AT[2 + g] = (["W2b%d" % g], ["W1b%d" % (g + 1)] if g + 1 < HEADS else [], [])
        def w_free(key):
            if key == "W1a": return 0
            if key == "W2a": return NT
            if key == "W1b0": return 2 * NT
            g = int(key[3:])
            return 2 * NT + 2 * NT * g if key.startswith("W2b") else 2 * NT + 2 * NT * (g - 1) + NT
        BIAS = [b1a, b2a] + [b1b] * HEADS + [b2b]
        ROUNDS = [(0, 4), (4, 4), (8, 2)]
        NROW = len(ROUNDS)
        def rl_split(j): return 0 if j == 1 else (2 + HEADS - 1) * PAIRS
        def rl_final(j): return rl_split(j) + PAIRS
        def rl_head(j): return (1 + head(j)) * PAIRS
        def hst(j): return 0 if j == 0 else (1 + head(j)) * PAIRS

        def pairs(eng, body, after_first=None, before_last=None):
            body(0)
            if after_first:
                after_first()
            with eng.Fori(1, PAIRS - 1, 1) as i:
                body(i)
            if before_last:
                before_last()
            body(PAIRS - 1)

        def rows(i, u): return bass.ds(i * CP + u * T, T)
        def tile_of(i, u): return bass.ds(2 * i + u, 1)

        block = ctx.enter_context(nc.Block())

        @block.sync
        def _(sp):
            sp.dma_start(dst_i, dst.rearrange("(c e) -> c e", e=CP)).then_inc(s_edges, 16)
            sp.dma_start(src_i, src.rearrange("(c e) -> c e", e=CP)).then_inc(s_edges, 16)

            def weights(key):
                ev = EV[key]
                w = ev["width"]
                if ev["att"]:
                    va, vd, g = ev["att"]
                    a = ev["att_first"]
                    if key != "W1a":
                        sp.wait_ge(s_wcol, ev["col_first"])
                    for n, v in enumerate((va, vd)):
                        if key[0:2] == "W2" and key[2] == "b":
                            row = v[0:1, :]
                        elif key[0:3] == "W1b":
                            row = v[g:g + 1, :]
                        else:
                            row = v.rearrange("(a f) -> a f", a=1)
                        width = D if w == D else HID
                        sp.dma_start(attv[:, n, 0:width], row.broadcast_to([128, width])).then_inc(s_att, 16)
                for c in range(ev["n"]):
                    g = ev["first"] + c
                    if g >= 2:
                        sp.wait_ge(s_wlo, g - 1)
                    k = ev["k0"] + c
                    sp.dma_start(stage[:, g % 2, 0:w], ev["w"][128 * k:128 * (k + 1), ev["c0"]:ev["c0"] + w])\
                      .then_inc(s_wst[g % 2], 16)

            def bias(j):
                if j:
                    sp.wait_ge(s_oev, og(j - 1) + NT)
                else:
                    sp.wait_ge(s_cdone, NT)
                w = hw(j)
                b = BIAS[j][w * head(j):w * (head(j) + 1)] if head(j) is not None else BIAS[j]
                sp.dma_start(brow[:, 0:w], b.rearrange("(a f) -> a f", a=1).broadcast_to([128, w])).then_inc(s_b, 16)

            def mask_load(j, i, u):
                if not (isinstance(i, int) and j == 0 and i == 0):
                    sp.wait_ge(s_mx, NT * j + 2 * i + u - 1)
                sp.dma_start(mask[0:T, u, :], mask_dram[rows(i, u), :]).then_inc(s_ml[u], 16)

            weights("W1a")
            for t in range(NT):
                sp.wait_ge(s_mk, t + 1)
                sp.dma_start(mask_dram[T * t:T * (t + 1), :], mask[0:T, t % 2, :]).then_inc(s_mst[t % 2], 16)
            for u in range(2):
                sp.wait_ge(s_mst[u], 16 * PAIRS)
            for j in range(NATT):
                def masks(i):
                    for u in range(2):
                        mask_load(j, i, u)
                if ahead(j):
                    pairs(sp, masks)
                else:
                    masks(0)
                bias(j)
                for key in AT[j][0]:
                    weights(key)
                if not ahead(j):
                    masks(1)
                for key in AT[j][1]:
                    weights(key)
                if not ahead(j):
                    with sp.Fori(2, PAIRS, 1) as i:
                        masks(i)
                for key in AT[j][2]:
                    weights(key)
            for u in range(2):
                sp.wait_ge(s_hst[u], 16 * (1 + HEADS) * PAIRS)
                sp.wait_ge(s_xst[u], 16 * 2 * PAIRS)

        @block.gpsimd
        def _(pool):
            g = nc.gpsimd
            g.memset(ident[:, :], 0.0).then_inc(s_iota, 1)
            g.memset(edge[0:NT, 20:30], 1.0).then_inc(s_iota, 1)
            g.memset(ones[:, :], 1.0)
            g.memset(expo[:, :], -0.5)
            g.memset(zeros[:, :], 0.0)
            g.iota(iota[:, :], pattern=[[1, N]], base=0, channel_multiplier=0, allow_small_or_imprecise_dtypes=True)
            g.iota(selfcol[:, :], pattern=[[T, NT]], base=0, channel_multiplier=1, allow_small_or_imprecise_dtypes=True)
            g.iota(edge[:, 0:NT], pattern=[[T, NT]], base=0, channel_multiplier=0, allow_small_or_imprecise_dtypes=True)
            g.iota(edge[:, 10:11], pattern=[[1, 1]], base=-NCP, channel_multiplier=1, allow_small_or_imprecise_dtypes=True)
            g.iota(edge[:, 11:12], pattern=[[1, 1]], base=1, channel_multiplier=1, allow_small_or_imprecise_dtypes=True)
            pool.wait_ge(s_iota, 2)
            g.affine_select(out=ident[:, :], in_=ident[:, :], compare_op=ALU.not_equal, fill=1.0, base=0,
                            pattern=[[-1, 128]], channel_multiplier=1)
            g.affine_select(out=edge[0:NT, 20:30], in_=edge[0:NT, 20:30], compare_op=ALU.is_gt, fill=0.0, base=0,
                            pattern=[[1, NT]], channel_multiplier=-1).then_inc(s_const, 1)

            def load_tile(srcd, j, i, u):
                t = tb(j) + 2 * i + u
                if not (j == 0 and isinstance(i, int) and i == 0):
                    pool.wait_ge(s_tr, 2 * (t - 1))
                pool.dma_start(nat[0:T, u, :], srcd[rows(i, u), :]).then_inc(s_nat[u], 16)

            def h2_load(j, i, u):
                pool.wait_ge(s_hst[u], 16 * (hst(j) + i))
                pool.dma_start(ring[0:T, u, :], h2_dram[rows(i, u), :]).then_inc(s_rl[u], 16)

            def h2_store(j, i, u):
                pool.wait_ge(s_h2ev, h2b(j) + 2 * i + u + 1)
                pool.dma_start(h2_dram[rows(i, u), :], ring[0:T, u, :]).then_inc(s_hst[u], 16)

            for j in range(NATT):
                f = NT * (j == LAST)
                if h_phase(j):
                    if j == 2:
                        for u in range(2):
                            pool.wait_ge(s_xst[u], 16 * PAIRS)
                    pairs(pool, lambda i: [load_tile(x if j == 0 else x1_dram, j, i, u) for u in range(2)])
                    more = head(j) is not None and head(j) > 0
                    if more:
                        for u in range(2):
                            h2_load(j, 0, u)

                    def step(i):
                        for u in range(2):
                            h2_store(j, i, u)
                            if more and not (isinstance(i, int) and i == PAIRS - 1):
                                h2_load(j, i + 1, u)
                    pairs(pool, step)
                else:
                    for u in range(2):
                        pool.wait_ge(s_hst[u], 16 * (PAIRS if j == 1 else (1 + HEADS) * PAIRS))

                    def split_load(i):
                        for u in range(2):
                            if not (isinstance(i, int) and i == 0):
                                pool.wait_ge(s_split, f + 2 * i + u - 1)
                            pool.dma_start(ring[0:T, u, :], h2_dram[rows(i, u), :]).then_inc(s_rl[u], 16)
                    pairs(pool, split_load)

                    def res_load(i, u):
                        if isinstance(i, int) and i == 0:
                            pool.wait_ge(s_split, f + NT)
                        pool.dma_start(ring[0:T, u, :], (x if j == 1 else x1_dram)[rows(i, u), :]).then_inc(s_rl[u], 16)

                    for u in range(2):
                        res_load(0, u)

                    def finish(i):
                        for u in range(2):
                            n = f + 2 * i + u
                            pool.wait_ge(s_var, n + 1)
                            g.tensor_tensor(rstd[0:T, u:u + 1], col[0:T, u, 5:6], expo[0:T, :], ALU.pow).then_inc(s_pow, 1)
                            if not (isinstance(i, int) and i == PAIRS - 1):
                                res_load(i + 1, u)
                            pool.wait_ge(s_fin, n + 1)
                            pool.dma_start((x1_dram if j == 1 else out)[rows(i, u), :], nat[0:T, u, :]).then_inc(s_xst[u], 16)
                    pairs(pool, finish)

        @block.scalar
        def _(act):
            a = nc.scalar.activation

            def weights(key):
                ev = EV[key]
                if ev["hi"] is None:
                    return
                if w_free(key):
                    act.wait_ge(s_tuse, w_free(key))
                if key == "W2b0":
                    act.wait_ge(s_agg, 2 * NT)
                for c in range(ev["n"]):
                    g = ev["first"] + c
                    act.wait_ge(s_wst[g % 2], 16 * (g // 2 + 1))
                    a(ev["hi"][:, c, 0:ev["width"]], stage[:, g % 2, 0:ev["width"]], ACT.Copy).then_inc(s_whi, 1)

            def transposed(t, u, K, func, rounds=(0, 1)):
                n = K // 2
                for r in rounds:
                    act.wait_ge(s_tr, 2 * t + r + 1)
                    if r == 0 and not (isinstance(t, int) and t < 2):
                        act.wait_ge(s_tuse, t - 1)
                    a(tr_hi[:, u, n * r:n * (r + 1), :], ps_t[:, 0:n * T].rearrange("p (k n) -> p k n", n=T), func)\
                        .then_inc(s_thi, 1)

            def h_tile(j, i, u):
                t = tb(j) + 2 * i + u
                w = hw(j)
                h = h0_hi if w == D else h1_hi
                act.wait_ge(s_tuse, t + 1)
                if w == D:
                    o = h[0:T, tile_of(i, u), 0:D].rearrange("p a (b f) -> p (a b) f", b=2)
                    a(o, ps_o[0:T, 2 * u:2 * u + 2, 0:HALF], ACT.Copy).then_inc(s_hhi, 1)
                else:
                    o = h[0:T, tile_of(i, u), 0:w].rearrange("p a (b f) -> p (a b) f", b=2)
                    a(o, ps_o[0:T, 2 * u:2 * u + 2, 0:w // 2], ACT.Copy).then_inc(s_hhi, 1)

            def row(j, k):
                rr = NROW * j + k
                t0, n = ROUNDS[k]
                act.wait_ge(s_row, rr + 1)
                a(arow[0:T, T * t0:T * (t0 + n)], ps_h2[0:T, rr % 2, 0:T * n], ACT.Copy).then_inc(s_rev, 1)

            def pair_row(j, i):
                act.wait_ge(s_prow, PAIRS * j + i + 1)
                if not (isinstance(i, int) and i == 0 and j == 0):
                    act.wait_ge(s_arg, NT * (PAIRS * j + i))
                a(prow[0:T, :, :], ps_a[0:T, 0:2 * CP].rearrange("p (a c) -> p a c", a=2), ACT.Copy).then_inc(s_prev, 1)

            def exps(j, i, half):
                for s in range(PAIRS * half, PAIRS * (half + 1)):
                    act.wait_ge(s_arg, NT * (PAIRS * j + i) + s + 1)
                    a(P[0:T, s, :], P[0:T, s, :], ACT.Exp, bias=asc[0:T, 1, s:s + 1]).then_inc(s_exp, 1)

            def p_high(j, i, u):
                p = NT * j + 2 * i + u
                act.wait_ge(s_p, NT * (PAIRS * j + i + 1))
                if not (isinstance(i, int) and i == 0 and j == 0):
                    act.wait_ge(s_agg, p - 1)
                a(p_hi[0:T, u, :, :], P[0:T, :, T * u:T * (u + 1)], ACT.Copy).then_inc(s_phi, 1)

            def evac(j, i, u):
                n = NT * j + 2 * i + u
                if j in FINAL:
                    f = NT * (j == LAST) + 2 * i + u
                    act.wait_ge(s_mean, f + 1)
                    a(junk[0:T, :], nat[0:T, u, :], ACT.Square, bias=col[0:T, u, 3:4], accum_out=col[0:T, u, 4:5])\
                        .then_inc(s_sq, 1)
                elif head(j) is not None:
                    act.wait_ge(s_oev, og(j) + 2 * i + u + 1)
                    a(junk[0:T, 0:HID], nat[0:T, u, 0:HID], ACT.Exp).then_inc(s_eexp, 1)

            def aggregate(j):
                if not ahead(j):
                    pair_row(j, 0)
                    exps(j, 0, 0)
                exps(j, 0, 1)
                p_high(j, 0, 0)
                p_high(j, 0, 1)
                for key in AT[j][0]:
                    weights(key)
                func = ACT.Relu if j == 0 else ACT.Copy

                def body(i):
                    peeled = isinstance(i, int)
                    more = not (peeled and i == PAIRS - 1)
                    for u, before in ((0, (i - 1, 1)), (1, (i, 0))):
                        has = not (peeled and i == 0 and u == 0)
                        tt = tg(j) + 2 * before[0] + before[1] if j not in FINAL and has else None
                        if has:
                            evac(j, *before)
                        if u == 1 and more:
                            exps(j, i + 1, 1)
                        if tt is not None:
                            transposed(tt, before[1], ky(j), func, (0,))
                        if u == 0 and more:
                            pair_row(j, i + 1)
                        if tt is not None:
                            transposed(tt, before[1], ky(j), func, (1,))
                        if u == 0 and more:
                            exps(j, i + 1, 0)
                    if more:
                        p_high(j, i + 1, 0)
                        p_high(j, i + 1, 1)
                pairs(act, body, lambda: [weights(key) for key in AT[j][1]], lambda: [weights(key) for key in AT[j][2]])
                evac(j, PAIRS - 1, 1)
                if j not in FINAL:
                    transposed(tg(j) + NT - 1, 1, ky(j), func)

            def counts_out(t):
                for r, (t0, n) in enumerate(ROUNDS):
                    rr = 3 * t + r
                    act.wait_ge(s_ctr, rr + 1)
                    a(CT3[0:T, t0:t0 + n, T * t:T * (t + 1)],
                      ps_h2[0:T, rr % 2, 0:n * T].rearrange("p (n c) -> p n c", c=T), ACT.Copy).then_inc(s_ctev, 1)

            weights("W1a")
            for t in range(NT):
                if t:
                    counts_out(t - 1)
                    act.wait_ge(s_mk, t)
                act.wait_ge(s_cdone, t + 1)
                a(C[0:T, :], ps_c[0:T, 0:N], ACT.Copy).then_inc(s_cev, 1)
            counts_out(NT - 1)
            for j in range(NATT):
                if h_phase(j):
                    if ahead(j):
                        for k in range(3):
                            row(j, k)

                    transposed(tb(j), 0, KD, ACT.Copy)

                    def body(i):
                        for u in range(2):
                            if not (isinstance(i, int) and i == PAIRS - 1 and u == 1):
                                transposed(tb(j) + 2 * i + u + 1, 1 - u, KD, ACT.Copy)
                            h_tile(j, i, u)
                    if ahead(j):
                        pairs(act, body, lambda: pair_row(j, 0), lambda: exps(j, 0, 0))
                    else:
                        pairs(act, body)
                        for k in range(3):
                            row(j, k)
                else:
                    f = NT * (j == LAST)
                    for k in range(3):
                        row(j, k)
                    act.wait_ge(s_agg, NT * j)
                    if j == LAST:
                        act.wait_ge(s_tuse, 2 * NT + 2 * NT * HEADS)

                    def body(i):
                        for u in range(2):
                            act.wait_ge(s_rl[u], 16 * (rl_split(j) + i + 1))
                            a(h0_hi[0:T, tile_of(i, u), 0:D].rearrange("p a f -> p (a f)"), ring[0:T, u, :], ACT.Copy)\
                                .then_inc(s_hhi, 1)
                    pairs(act, body)
                aggregate(j)

        @block.vector
        def _(dve):
            v = nc.vector

            def weights(key):
                ev = EV[key]
                w = ev["width"]
                for c in range(ev["n"]):
                    g = ev["first"] + c
                    if ev["att"]:
                        if c == 0:
                            dve.wait_ge(s_att, 32 * (ev["att_first"] + 1))
                        dve.wait_ge(s_wst[g % 2], 16 * (g // 2 + 1))
                        to = ev["cols"](c)
                        for n in range(2):
                            m = ev["col_first"] + 2 * c + n
                            if m:
                                dve.wait_ge(s_wcol, m)
                            ins = v.tensor_tensor_reduce(out=junk[:, 0:w], in0=stage[:, g % 2, 0:w],
                                                         in1=attv[:, n, 0:w], scale=1.0, scalar=0.0,
                                                         op0=ALU.mult, op1=ALU.add, accum_out=wc_raw[:, to + n:to + n + 1])
                            ins.then_inc(s_wcol, 1)
                    if ev["hi"] is not None:
                        dve.wait_ge(s_whi, whi[g] + 1)
                        own = ev["att"] and key != "W1b0"
                        ins = v.tensor_tensor(ev["lo"][:, c, 0:w], stage[:, g % 2, 0:w], ev["hi"][:, c, 0:w].bitcast(f32),
                                              ALU.subtract)
                        if own:
                            dve.wait_ge(s_wcol, ev["col_first"] + 2 * c + 2)
                            v.tensor_copy(ev["hi"][:, c, w:w + 2], wc_raw[:, to:to + 2]).then_inc(s_wcs, 1)
                            wcs[0] += 1
                            dve.wait_ge(s_wcs, wcs[0])
                            ins = v.tensor_tensor(ev["lo"][:, c, w:w + 2], wc_raw[:, to:to + 2],
                                                  ev["hi"][:, c, w:w + 2].bitcast(f32), ALU.subtract)
                        ins.then_inc(s_wlo, 1)
                    else:
                        dve.wait_ge(s_wcol, ev["col_first"] + 2 * c + 2)
                        v.memset(started[:, 2:3], 0.0).then_inc(s_wlo, 1)

            whi, n_hi = {}, 0
            for e in events:
                for c in range(e["n"]):
                    if e["hi"] is not None:
                        whi[e["first"] + c] = n_hi
                        n_hi += 1

            def head_cols():
                raw = wc_raw[:, WCOL["W1b"]:WCOL["W2b"]].rearrange("p (k c) -> p k c", c=AC)
                dve.wait_ge(s_wcol, EV["W1b0"]["col_first"] + 2 * KD)
                v.tensor_copy(w1_hi[:, :, HID:HID + AC], raw).then_inc(s_wcs, 1)
                wcs[0] += 1
                dve.wait_ge(s_wcs, wcs[0])
                v.tensor_tensor(w1_lo[:, :, HID:HID + AC], raw, w1_hi[:, :, HID:HID + AC].bitcast(f32), ALU.subtract)\
                    .then_inc(s_hcol, 1)

            wcs = [0]

            def low(t, u, K, relu):
                n = K // 2
                for r in range(2):
                    dve.wait_ge(s_thi, 2 * t + r + 1)
                    o = tr_lo[:, u, n * r:n * (r + 1), :]
                    p = ps_t[:, 0:n * T].rearrange("p (k n) -> p k n", n=T)
                    h = tr_hi[:, u, n * r:n * (r + 1), :].bitcast(f32)
                    if relu:
                        v.scalar_tensor_tensor(out=o, in0=p, scalar=0.0, in1=h, op0=ALU.max, op1=ALU.subtract)\
                            .then_inc(s_tlo, 1)
                    else:
                        v.tensor_tensor(o, p, h, ALU.subtract).then_inc(s_tlo, 1)

            def h_low(j, i, u):
                w = hw(j)
                dve.wait_ge(s_hhi, hh(j) + 2 * i + u + 1)
                if w == D:
                    def v3(t): return t[0:T, tile_of(i, u), 0:D].rearrange("p a (b f) -> p (a b) f", b=2)
                    v.tensor_tensor(v3(h0_lo), ps_o[0:T, 2 * u:2 * u + 2, 0:HALF], v3(h0_hi).bitcast(f32),
                                    ALU.subtract).then_inc(s_oev, 1)
                else:
                    def v2(t): return t[0:T, tile_of(i, u), 0:w].rearrange("p a (b f) -> p (a b) f", b=2)
                    v.tensor_tensor(v2(h1_lo), ps_o[0:T, 2 * u:2 * u + 2, 0:w // 2], v2(h1_hi).bitcast(f32),
                                    ALU.subtract).then_inc(s_oev, 1)

            def a_cols(j, where, i, u):
                if where == "H":
                    to, c, p = AS[j], (2 if j == 0 else AC), ps_o[0:T, 2 * u + 1, hw(j) // 2:hw(j) // 2 + (2 if j == 0 else AC)]
                else:
                    to, c, p = AS[1 if j == 0 else LAST], 2, ps_h2[0:T, 1, HALF:HALF + 2]
                o = to[:, tile_of(i, u), 0:c].rearrange("p a c -> p (a c)")
                if where == "G" and head(j):
                    v.tensor_tensor(o, o, p, ALU.add)
                else:
                    v.tensor_copy(o, p)

            def diag(j, k):
                rr = NROW * j + k
                t0, n = ROUNDS[k]
                o = flatP[0:T, 500 * k:500 * k + n * T].rearrange("p (n c) -> p n c", c=T)
                if j and k == 0:
                    dve.wait_ge(s_plo, NT * j)
                v.tensor_tensor(o, ident[0:T, 0:T].unsqueeze(1).broadcast_to([T, n, T]),
                                as_of(j)[:, t0:t0 + n].unsqueeze(2).broadcast_to([T, n, T]), ALU.mult).then_inc(s_diag, 1)

            def scaled(j):
                if j:
                    dve.wait_ge(s_arg, NT * PAIRS * j)
                    dve.wait_ge(s_exp, NT * PAIRS * j)
                v.tensor_scalar(asc[0:T, 0, :], as_of(j), 1.0 - SLOPE, None, ALU.mult)
                v.tensor_scalar(asc[0:T, 1, :], as_of(j), SLOPE, None, ALU.mult).then_inc(s_as, 1)

            def maxes(j, i, u):
                n = NT * j + 2 * i + u
                if isinstance(i, int) and i == 0 and u == 0:
                    dve.wait_ge(s_rev, NROW * (j + 1))
                dve.wait_ge(s_ml[u], 16 * (PAIRS * j + i + 1))
                v.memset(started[0:T, u:u + 1], 0.0)
                v.tensor_tensor_reduce(out=mask[0:T, u, :], in0=arow[0:T, :], in1=mask[0:T, u, :],
                                       scale=1.0, scalar=NEG, op0=ALU.add, op1=ALU.max,
                                       accum_out=mtile[0:T, u:u + 1]).then_inc(s_mx, 1)
                if ahead(j):
                    dve.wait_ge(s_mx, n + 1)
                    v.tensor_copy(M[0:T, tile_of(i, u)], mtile[0:T, u:u + 1]).then_inc(s_mcol, 1)

            def pair_cols(j, i):
                n = 4 * (PAIRS * j + i)
                two = bass.ds(2 * i, 2)
                if ahead(j):
                    dve.wait_ge(s_mcol, NT * (j - 3) + 2 * i + 2)
                    mx = M[0:T, two]
                else:
                    dve.wait_ge(s_mx, NT * j + 2 * i + 2)
                    mx = mtile[0:T, :]
                ad = ad_of(j)[:, two]
                v.tensor_tensor(pc[0:T, 0, :], ad, mx, ALU.add).then_inc(s_pc, 1)
                dve.wait_ge(s_pc, n + 1)
                v.scalar_tensor_tensor(out=pc[0:T, 1, :], in0=pc[0:T, 0, :], scalar=SLOPE, in1=pc[0:T, 0, :], op0=ALU.mult, op1=ALU.max)\
                    .then_inc(s_pc, 1)
                dve.wait_ge(s_pc, n + 2)
                v.tensor_tensor(pc[0:T, 2, :], ad, pc[0:T, 1, :], ALU.subtract).then_inc(s_pc, 1)
                v.scalar_tensor_tensor(out=pc[0:T, 3, :], in0=ad, scalar=SLOPE, in1=pc[0:T, 1, :], op0=ALU.mult, op1=ALU.subtract)\
                    .then_inc(s_pc, 1)

            def pair_diag(j, i):
                n = PAIRS * j + i
                dve.wait_ge(s_pc, 4 * n + 4)
                if isinstance(i, int) and i == 0:
                    dve.wait_ge(s_row, NROW * (j + 1))
                else:
                    dve.wait_ge(s_plo, NT * j + 2 * i)
                v.tensor_tensor(flatP[0:T, 0:2 * CP].rearrange("p (n c) -> p n c", c=T),
                                ident[0:T, 0:T].unsqueeze(1).broadcast_to([T, 4, T]),
                                pc[0:T, 2:4, :].rearrange("p a c -> p (a c)").unsqueeze(2).broadcast_to([T, 4, T]), ALU.mult)\
                    .then_inc(s_pdiag, 1)

            def args(j, i, half):
                if half == 0:
                    if isinstance(i, int) and i == 0:
                        dve.wait_ge(s_as, j + 1)
                    dve.wait_ge(s_prev, PAIRS * j + i + 1)
                for s in range(PAIRS * half, PAIRS * (half + 1)):
                    v.scalar_tensor_tensor(out=P[0:T, s, :], in0=prow[0:T, 0, :], scalar=asc[0:T, 0, s:s + 1],
                                           in1=prow[0:T, 1, :], op0=ALU.add, op1=ALU.max).then_inc(s_arg, 1)

            def counts(j, i, half):
                for s in range(PAIRS * half, PAIRS * (half + 1)):
                    dve.wait_ge(s_exp, NT * (PAIRS * j + i) + s + 1)
                    v.scalar_tensor_tensor(out=P[0:T, s, :], in0=P[0:T, s, :], scalar=1.0,
                                           in1=CT3[0:T, s, bass.ds(i * CP, CP)], op0=ALU.min, op1=ALU.mult).then_inc(s_p, 1)

            def p_low(j, i, u):
                p = NT * j + 2 * i + u
                dve.wait_ge(s_phi, p + 1)
                v.tensor_tensor(p_lo[0:T, u, :, :], P[0:T, :, T * u:T * (u + 1)], p_hi[0:T, u, :, :].bitcast(f32),
                                ALU.subtract).then_inc(s_plo, 1)

            def norm(j, i, u):
                n = NT * j + 2 * i + u
                w = hw(j) // 2
                dve.wait_ge(s_agg, n + 1)
                if j >= 2:
                    v.tensor_scalar(col[0:T, u, 0:1], ps_o[0:T, 2 * u + 1, w:w + 1], 1e-16, None, ALU.add).then_inc(s_den, 1)
                    dve.wait_ge(s_den, n - 2 * NT + 1)
                    v.reciprocal(col[0:T, u, 1:2], col[0:T, u, 0:1]).then_inc(s_rd, 1)
                else:
                    v.reciprocal(col[0:T, u, 1:2], ps_o[0:T, 2 * u + 1, w:w + 1]).then_inc(s_rd, 1)
                dve.wait_ge(s_rd, n + 1)
                if isinstance(i, int) and i == 0 and u == 0:
                    dve.wait_ge(s_b, 16 * (j + 1))
                if j in FINAL and not (isinstance(i, int) and i == 0 and j == 1):
                    if not (isinstance(i, int) and i == 0):
                        dve.wait_ge(s_xst[u], 16 * (PAIRS * (j == LAST) + i))
                v3 = lambda t: t.rearrange("p (b f) -> p b f", b=2)
                v.scalar_tensor_tensor(out=v3(nat[0:T, u, 0:2 * w]), in0=ps_o[0:T, 2 * u:2 * u + 2, 0:w], scalar=col[0:T, u, 1:2],
                                       in1=v3(brow[0:T, 0:2 * w]), op0=ALU.mult, op1=ALU.add).then_inc(s_oev, 1)

            def stage1(j, i, u):
                norm(j, i, u)
                if j in FINAL:
                    f = NT * (j == LAST) + 2 * i + u
                    dve.wait_ge(s_oev, og(j) + 2 * i + u + 1)
                    dve.wait_ge(s_rl[u], 16 * (rl_final(j) + i + 1))
                    v.scalar_tensor_tensor(out=nat[0:T, u, :], in0=nat[0:T, u, :], scalar=1.0, in1=ring[0:T, u, :],
                                           op0=ALU.mult, op1=ALU.add, accum_out=col[0:T, u, 2:3]).then_inc(s_sum, 1)
                    dve.wait_ge(s_sum, f + 1)
                    v.tensor_scalar(col[0:T, u, 3:4], col[0:T, u, 2:3], -1.0 / D, None, ALU.mult).then_inc(s_mean, 1)

            def stage2(j, i, u):
                if j in FINAL:
                    f = NT * (j == LAST) + 2 * i + u
                    dve.wait_ge(s_sq, f + 1)
                    v.tensor_scalar(col[0:T, u, 5:6], col[0:T, u, 4:5], 1.0 / D, EPS, ALU.mult, ALU.add).then_inc(s_var, 1)
                elif head(j) is not None:
                    e = NT * (j - 2) + 2 * i + u
                    dve.wait_ge(s_eexp, e + 1)
                    v.tensor_scalar(junk[0:T, 0:HID], junk[0:T, 0:HID], 1.0, -1.0, ALU.min, ALU.add).then_inc(s_emin, 1)
                    dve.wait_ge(s_emin, e + 1)
                    v.scalar_tensor_tensor(out=nat[0:T, u, 0:HID], in0=nat[0:T, u, 0:HID], scalar=0.0, in1=junk[0:T, 0:HID],
                                           op0=ALU.max, op1=ALU.add).then_inc(s_y, 1)

            def stage3(j, i, u):
                if j in FINAL:
                    return
                low(tg(j) + 2 * i + u, u, ky(j), j == 0)

            def stage4(j, i, u):
                if j in FINAL:
                    f = NT * (j == LAST) + 2 * i + u
                    dve.wait_ge(s_pow, f + 1)
                    v.tensor_scalar(nat[0:T, u, :], nat[0:T, u, :], col[0:T, u, 3:4], rstd[0:T, u:u + 1], ALU.add, ALU.mult)\
                        .then_inc(s_fin, 1)
                    return
                t = tg(j) + 2 * i + u
                dve.wait_ge(s_tuse, t + 1)
                a_cols(j, "G", i, u)
                if head(j):
                    dve.wait_ge(s_rl[u], 16 * (rl_head(j) + i + 1))
                    r3 = ring[0:T, u, :].rearrange("p (b f) -> p b f", b=2)
                    v.tensor_tensor(r3, r3, ps_h2[0:T, :, 0:HALF], ALU.add).then_inc(s_h2ev, 1)
                else:
                    if not (isinstance(i, int) and i == 0 and j == 0):
                        dve.wait_ge(s_hst[u], 16 * (hst(j) + i))
                    v.tensor_copy(ring[0:T, u, :].rearrange("p (b f) -> p b f", b=2), ps_h2[0:T, :, 0:HALF])\
                        .then_inc(s_h2ev, 1)

            def aggregate(j):
                if not ahead(j):
                    scaled(j)
                    maxes(j, 0, 0)
                    maxes(j, 0, 1)
                    pair_cols(j, 0)
                    pair_diag(j, 0)
                    args(j, 0, 0)
                    args(j, 0, 1)
                counts(j, 0, 0)
                counts(j, 0, 1)
                p_low(j, 0, 0)
                p_low(j, 0, 1)
                for key in AT[j][0]:
                    weights(key)

                def body(i):
                    peeled = isinstance(i, int)
                    more = not (peeled and i == PAIRS - 1)
                    for u, before, before2 in ((0, (i - 1, 1), (i - 1, 0)), (1, (i, 0), (i - 1, 1))):
                        has = not (peeled and i == 0 and u == 0)
                        if has:
                            stage1(j, *before)
                        if not (peeled and i == 0):
                            stage4(j, *before2)
                        if u == 0 and more and not ahead(j):
                            maxes(j, i + 1, 0)
                        if u == 1 and more:
                            args(j, i + 1, 1)
                        if has:
                            stage2(j, *before)
                        if u == 0 and more:
                            if not ahead(j):
                                maxes(j, i + 1, 1)
                            pair_cols(j, i + 1)
                            pair_diag(j, i + 1)
                        if has:
                            stage3(j, *before)
                        if u == 0 and more:
                            args(j, i + 1, 0)
                        if more:
                            counts(j, i + 1, u)
                    if more:
                        p_low(j, i + 1, 0)
                        p_low(j, i + 1, 1)

                def first_done():
                    for key in AT[j][1]:
                        weights(key)
                    if j == 1:
                        head_cols()
                pairs(dve, body, first_done, lambda: [weights(key) for key in AT[j][2]])
                stage1(j, PAIRS - 1, 1)
                stage4(j, PAIRS - 1, 0)
                stage2(j, PAIRS - 1, 1)
                stage3(j, PAIRS - 1, 1)
                stage4(j, PAIRS - 1, 1)

            dve.sem_inc(s_oh, 2 * NCP)
            dve.wait_ge(s_edges, 32)
            v.tensor_copy(dst_f, dst_i)
            v.tensor_copy(src_f, src_i).then_inc(s_conv, 1)
            dve.wait_ge(s_conv, 1)
            v.tensor_reduce(out=edge[0:NCP, 12:13], in_=dst_f, axis=AX.X, op=ALU.min)
            v.tensor_reduce(out=edge[0:NCP, 13:14], in_=dst_f, axis=AX.X, op=ALU.max).then_inc(s_prep, 1)
            dve.wait_ge(s_prep, 1)
            dve.wait_ge(s_const, 1)
            ed = lambda a, b, p=NCP: edge[0:p, a:b]
            v.tensor_scalar(ed(30, 40), ed(0, NT), ed(13, 14), None, ALU.is_le)
            v.tensor_scalar(ed(40, 50), ed(0, NT), float(T - 1), ed(12, 13), ALU.add, ALU.is_ge).then_inc(s_prep, 1)
            dve.wait_ge(s_prep, 2)
            v.tensor_tensor(ed(30, 40), ed(30, 40), ed(40, 50), ALU.mult).then_inc(s_prep, 1)
            dve.wait_ge(s_prep, 3)
            v.tensor_scalar(ed(40, 50), ed(30, 40), ed(10, 11), None, ALU.mult)
            v.tensor_scalar(ed(50, 60), ed(30, 40), ed(11, 12), None, ALU.mult).then_inc(s_prep, 1)
            dve.wait_ge(s_etr, 1)
            v.tensor_copy(ecol[0:T], ps_t[0:T, 0:4 * NCP].rearrange("p (q c) -> p q c", q=4)).then_inc(s_ecol, 1)
            dve.wait_ge(s_ltr, 1)
            ps_lim = ps_a
            v.tensor_reduce(out=ed(14, 15, NT), in_=ps_lim[0:NT, 0:NCP], axis=AX.X, op=ALU.min)
            v.tensor_reduce(out=ed(15, 16, NT), in_=ps_lim[0:NT, NCP:2 * NCP], axis=AX.X, op=ALU.max).then_inc(s_prep, 1)
            dve.wait_ge(s_prep, 5)
            v.tensor_scalar(ed(14, 15, NT), ed(14, 15, NT), float(NCP), float(NCP - 1), ALU.add, ALU.min).then_inc(s_prep, 1)
            dve.wait_ge(s_prep, 6)
            v.scalar_tensor_tensor(out=ed(15, 16, NT), in0=ed(14, 15, NT), scalar=1.0, in1=ed(15, 16, NT), op0=ALU.add, op1=ALU.max)\
                .then_inc(s_prep, 1)
            dve.wait_ge(s_prep, 7)
            v.tensor_tensor(ed(16, 17, NT), ed(15, 16, NT), ed(14, 15, NT), ALU.subtract).then_inc(s_prep, 1)
            dve.wait_ge(s_tabps, 1)
            v.tensor_copy(edge[0:1, 20:30], ps_a[0:1, 192:192 + NT])
            v.tensor_copy(edge[0:1, 30:50], ps_a[0:1, 160:180]).then_inc(s_prep, 1)
            dve.wait_ge(s_prep, 9)
            v.tensor_copy(tab[0:1, 0:2 * NT], edge[0:1, 30:50])
            v.scalar_tensor_tensor(out=tab[0:1, 2 * NT:3 * NT], in0=edge[0:1, 20:30], scalar=float(NCP), in1=edge[0:1, 30:40],
                                   op0=ALU.add, op1=ALU.subtract).then_inc(s_tab, 1)
            weights("W1a")
            v.memset(h0_hi[0:T, :, D:D + 2].bitcast(f32), 1.0)
            v.memset(h0_lo[0:T, :, D:D + 2].bitcast(f32), 0.0).then_inc(s_ones, 1)
            dve.wait_ge(s_tab, 1)

            def from_counts(t):
                dve.wait_ge(s_cev, t + 1)
                if t >= 2:
                    dve.wait_ge(s_mst[t % 2], 16 * (t // 2))
                v.tensor_scalar(mask[0:T, t % 2, :], C[0:T, :], 0.5, NEG, ALU.is_lt, ALU.mult).then_inc(s_mk, 1)

            dve.wait_ge(s_ecol, 1)
            for t in range(NT):
                lo = dve.value_load(tab[0:1, t:t + 1], min_val=0, max_val=NCP - 1)
                hi = dve.value_load(tab[0:1, NT + t:NT + t + 1], min_val=1, max_val=NCP)
                sh = dve.value_load(tab[0:1, 2 * NT + t:2 * NT + t + 1], min_val=1, max_val=NCP * NT)
                with dve.Fori(lo, hi, 1) as c:
                    for q in range(2):
                        dve.wait_ge(s_used, 2 * (c + sh) + q + 1)
                        v.tensor_scalar(oh_dst[q][0:T, 0:T], iota[0:T, T * t:T * (t + 1)], ecol[0:T, q, bass.ds(c, 1)], None, ALU.is_equal)
                        v.tensor_scalar(oh_src[q][0:T, :], iota[0:T, :], ecol[0:T, 2 + q, bass.ds(c, 1)], None, ALU.is_equal)\
                            .then_inc(s_oh, 1)
                if t:
                    dve.wait_ge(s_cdone, t)
                v.tensor_scalar(oh_dst[2][0:T, 0:T], iota[0:T, T * t:T * (t + 1)], selfcol[0:T, t:t + 1], None, ALU.is_equal)
                v.tensor_scalar(oh_src[2][0:T, :], iota[0:T, :], selfcol[0:T, t:t + 1], None, ALU.is_equal).then_inc(s_self, 1)
                if t:
                    from_counts(t - 1)
            from_counts(NT - 1)

            for j in range(NATT):
                if h_phase(j):
                    if ahead(j):
                        for k in range(3):
                            diag(j, k)
                        scaled(j)
                    if j == 2:
                        dve.wait_ge(s_agg, 2 * NT)
                        v.memset(h1_hi[0:T, :, HID:HID + 2].bitcast(f32), 1.0)
                        v.memset(h1_lo[0:T, :, HID:HID + 2].bitcast(f32), 0.0).then_inc(s_ones, 1)

                    low(tb(j), 0, KD, False)

                    def body(i):
                        for u in range(2):
                            if not (isinstance(i, int) and i == PAIRS - 1 and u == 1):
                                low(tb(j) + 2 * i + u + 1, 1 - u, KD, False)
                            if ahead(j):
                                h_low(j, i, u)
                                maxes(j, i, u)
                            else:
                                dve.wait_ge(s_hhi, hh(j) + 2 * i + u + 1)
                                a_cols(j, "H", i, u)
                                h_low(j, i, u)

                    def first_row():
                        pair_cols(j, 0)
                        pair_diag(j, 0)

                    def first_args():
                        args(j, 0, 0)
                        args(j, 0, 1)

                    if ahead(j):
                        pairs(dve, body, first_row, first_args)
                    else:
                        pairs(dve, body)
                        dve.wait_ge(s_oev, ob(j) + NT)
                        for k in range(3):
                            diag(j, k)
                else:
                    dve.wait_ge(s_h2ev, h2b(j - 1) + NT)
                    for k in range(3):
                        diag(j, k)
                    if j == LAST:
                        dve.wait_ge(s_tuse, 2 * NT + 2 * NT * HEADS)
                        v.memset(h0_hi[0:T, :, D:D + 2].bitcast(f32), 1.0)
                        v.memset(h0_lo[0:T, :, D:D + 2].bitcast(f32), 0.0).then_inc(s_ones, 1)

                    def body(i):
                        for u in range(2):
                            dve.wait_ge(s_hhi, hh(j) + 2 * i + u + 1)
                            h = lambda t: t[0:T, tile_of(i, u), 0:D].rearrange("p a f -> p (a f)")
                            v.tensor_tensor(h(h0_lo), ring[0:T, u, :], h(h0_hi).bitcast(f32), ALU.subtract).then_inc(s_split, 1)
                    pairs(dve, body)
                aggregate(j)

        @block.tensor
        def _(pe):
            mm = nc.tensor.matmul

            def transposes(t, u, K, ready, r):
                n = K // 2
                if r == 0:
                    ready()
                if not (isinstance(t, int) and t == 0 and r == 0):
                    pe.wait_ge(s_tlo, 2 * t + r)
                for k in range(n):
                    kk = n * r + k
                    ins = nc.tensor.transpose(ps_t[:, T * k:T * (k + 1)], nat[0:T, u, 128 * kk:128 * (kk + 1)], ident[0:T, 0:T])
                ins.then_inc(s_tr, 1)

            def product(o, K, u, w_hi, w_lo, parts, between={}):
                for k in range(K):
                    for a_, b_, st, sp_ in ((tr_hi, w_hi, k == 0, False), (tr_hi, w_lo, False, False), (tr_lo, w_hi, False, k == K - 1)):
                        for b, (c0, c1) in enumerate(parts):
                            ins = mm(o[:, b, 0:c1 - c0], a_[:, u, k, :], b_[:, k, c0:c1], start=st, stop=sp_)
                    if k in between:
                        between[k]()
                    if k == K - 1:
                        ins.then_inc(s_tuse, 1)

            def sum_tile(j, i, u, between):
                p, o = NT * j + 2 * i + u, og(j) + 2 * i + u
                w = hw(j) // 2
                h_hi, h_lo = (h0_hi, h0_lo) if hw(j) == D else (h1_hi, h1_lo)
                pe.wait_ge(s_plo, p + 1)
                pe.wait_ge(s_oev, o - 1)
                for s in range(NT):
                    for a_, b_, st, sp_ in ((p_hi, h_hi, s == 0, False), (p_hi, h_lo, False, False), (p_lo, h_hi, False, s == NT - 1)):
                        for b, (c0, c1) in enumerate(((0, w), (w, 2 * w + 2))):
                            ins = mm(ps_o[0:T, 2 * u + b, 0:c1 - c0], a_[0:T, u, s, :], b_[0:T, s, c0:c1], start=st, stop=sp_)
                    if s == NT - 1:
                        ins.then_inc(s_agg, 1)
                    if s in between:
                        between[s]()

            def row(j, k):
                rr = NROW * j + k
                n = ROUNDS[k][1]
                pe.wait_ge(s_diag, rr + 1)
                if rr >= 2:
                    pe.wait_ge(s_rev, rr - 1)
                if k == 0:
                    if j == 0:
                        pe.wait_ge(s_ctev, 3 * NT)
                    else:
                        pe.wait_ge(s_h2ev, h2b(j - 1) + NT if j != 2 else NT)
                mm(ps_h2[0:T, rr % 2, 0:n * T], ones[0:T, :], flatP[0:T, 500 * k:500 * k + n * T],
                   start=True, stop=True).then_inc(s_row, 1)

            def pair_row(j, i):
                n = PAIRS * j + i
                pe.wait_ge(s_pdiag, n + 1)
                if not (isinstance(i, int) and i == 0 and j == 0):
                    pe.wait_ge(s_prev, n)
                mm(ps_a[0:T, 0:2 * CP], ones[0:T, :], flatP[0:T, 0:2 * CP], start=True, stop=True).then_inc(s_prow, 1)

            def y_ready(j, i, u):
                def f():
                    if head(j) is None:
                        pe.wait_ge(s_oev, og(j) + 2 * i + u + 1)
                    else:
                        pe.wait_ge(s_y, NT * head(j) + 2 * i + u + 1)
                return f

            def next_h(j, i, u):
                t = tg(j) + 2 * i + u
                pe.wait_ge(s_tlo, 2 * t + 2)
                if isinstance(i, int) and i == 0 and u == 0:
                    pe.wait_ge(s_wlo, done("W2a" if j == 0 else "W2b%d" % head(j)))
                    pe.wait_ge(s_rev, NROW * (j + 1))
                n = h2b(j) + 2 * i + u
                if not (isinstance(i, int) and i == 0 and u == 0 and j == 0):
                    pe.wait_ge(s_h2ev, n)
                hi, lo = (w0_hi, w0_lo) if j == 0 else (w2_hi, w2_lo)
                product(ps_h2[0:T], ky(j), u, hi, lo, ((0, HALF), (HALF, D + 2)))

            pe.sem_inc(s_used, 2 * NCP + 2)
            pe.wait_ge(s_const, 1)
            pe.wait_ge(s_conv, 1)
            for q, t in enumerate((dst_f, dst_f, src_f, src_f)):
                ins = nc.tensor.transpose(ps_t[0:T, NCP * q:NCP * (q + 1)], t[:, T * (q % 2):T * (q % 2 + 1)], ident[0:NCP, 0:NCP])
            ins.then_inc(s_etr, 1)
            pe.wait_ge(s_prep, 4)
            nc.tensor.transpose(ps_a[0:NT, 0:NCP], edge[0:NCP, 40:50], ident[0:NCP, 0:NCP])
            nc.tensor.transpose(ps_a[0:NT, NCP:2 * NCP], edge[0:NCP, 50:60], ident[0:NCP, 0:NCP]).then_inc(s_ltr, 1)
            pe.wait_ge(s_prep, 8)
            mm(ps_a[0:1, 160:170], edge[0:NT, 14:15], ident[0:NT, 0:NT], start=True, stop=True)
            mm(ps_a[0:1, 170:180], edge[0:NT, 15:16], ident[0:NT, 0:NT], start=True, stop=True)
            mm(ps_a[0:1, 192:202], edge[0:NT, 16:17], edge[0:NT, 20:30], start=True, stop=True).then_inc(s_tabps, 1)
            pe.wait_ge(s_tab, 1)

            BANKS = ((0, 512), (512, 1024), (1024, N))

            def transpose_counts(t):
                pe.wait_ge(s_cev, t + 1)
                for r, (t0, n) in enumerate(ROUNDS):
                    rr = 3 * t + r
                    if rr >= 2:
                        pe.wait_ge(s_ctev, rr - 1)
                    for q in range(n):
                        ins = nc.tensor.transpose(ps_h2[0:T, rr % 2, T * q:T * (q + 1)], C[0:T, T * (t0 + q):T * (t0 + q + 1)],
                                                  ident[0:T, 0:T])
                    ins.then_inc(s_ctr, 1)

            for t in range(NT):
                lo = pe.value_load(tab[0:1, t:t + 1], min_val=0, max_val=NCP - 1)
                hi = pe.value_load(tab[0:1, NT + t:NT + t + 1], min_val=1, max_val=NCP)
                sh = pe.value_load(tab[0:1, 2 * NT + t:2 * NT + t + 1], min_val=1, max_val=NCP * NT)
                if t:
                    pe.wait_ge(s_cev, t)
                for b, (c0, c1) in enumerate(BANKS):
                    mm(ps_o[0:T, b, 0:c1 - c0], zeros[0:T, 0:T], iota[0:T, c0:c1], start=True, stop=False)
                with pe.Fori(lo, hi, 1) as c:
                    for q in range(2):
                        pe.wait_ge(s_oh, 2 * (c + sh) + q + 1)
                        for b, (c0, c1) in enumerate(BANKS):
                            ins = mm(ps_o[0:T, b, 0:c1 - c0], oh_dst[q][0:T, 0:T], oh_src[q][0:T, c0:c1], start=False, stop=False)
                        ins.then_inc(s_used, 1)
                pe.wait_ge(s_self, t + 1)
                for b, (c0, c1) in enumerate(BANKS):
                    ins = mm(ps_o[0:T, b, 0:c1 - c0], oh_dst[2][0:T, 0:T], oh_src[2][0:T, c0:c1], start=False, stop=True)
                ins.then_inc(s_cdone, 1)
                if t:
                    transpose_counts(t - 1)
            transpose_counts(NT - 1)
            pe.wait_ge(s_ecol, 1)

            for j in range(NATT):
                if h_phase(j):
                    if ahead(j):
                        for k in range(3):
                            row(j, k)
                    hi, lo = (w0_hi, w0_lo) if j == 0 else (w1_hi, w1_lo)
                    w = hw(j) // 2
                    parts = ((0, w), (w, 2 * w + {0: 2, 2: AC}.get(j, 0)))
                    n_nat = 0 if j == 0 else PAIRS * (1 + head(j))

                    def nat_ready(i, u):
                        return lambda: pe.wait_ge(s_nat[u], 16 * (n_nat + i + 1))

                    def h_tile(i, u):
                        t, o = tb(j) + 2 * i + u, ob(j) + 2 * i + u
                        first = isinstance(i, int) and i == 0
                        pe.wait_ge(s_tlo, 2 * t + 2)
                        if first and u == 0:
                            pe.wait_ge(s_wlo, done({0: "W1a"}.get(j, "W1b%d" % (head(j) or 0))))
                            if j == 0:
                                pe.wait_ge(s_cev, NT)
                            else:
                                pe.wait_ge(s_hcol, 1)
                        if not (j == 0 and first):
                            pe.wait_ge(s_oev, o - 1)
                        between = {}
                        if not (isinstance(i, int) and i == PAIRS - 1 and u == 1):
                            nxt = (i, 1) if u == 0 else (i + 1, 0)
                            between = {1: lambda: transposes(t + 1, 1 - u, KD, nat_ready(*nxt), 0),
                                       3: lambda: transposes(t + 1, 1 - u, KD, None, 1)}
                        product(ps_o[0:T, 2 * u:2 * u + 2], KD, u, hi, lo, parts, between)

                    for r in range(2):
                        transposes(tb(j), 0, KD, nat_ready(0, 0), r)

                    def body(i):
                        h_tile(i, 0)
                        h_tile(i, 1)
                    if ahead(j):
                        pairs(pe, body, lambda: pair_row(j, 0))
                    else:
                        pairs(pe, body)
                        for k in range(3):
                            row(j, k)
                        pair_row(j, 0)
                    pe.wait_ge(s_oev, ob(j) + NT)
                else:
                    for k in range(3):
                        row(j, k)
                    pair_row(j, 0)
                    pe.wait_ge(s_split, NT * (1 if j == 1 else 2))
                pe.wait_ge(s_ones, {0: 1, 1: 1, LAST: 3}.get(j, 2))

                def body(i):
                    peeled = isinstance(i, int)
                    more = not (peeled and i == PAIRS - 1)
                    for u, b in ((0, (i - 1, 1)), (1, (i, 0))):
                        has = j not in FINAL and not (peeled and i == 0 and u == 0)
                        between = {}
                        if has:
                            tt = tg(j) + 2 * b[0] + b[1]
                            between[4] = lambda: transposes(tt, b[1], ky(j), y_ready(j, *b), 0)
                            between[8] = lambda: transposes(tt, b[1], ky(j), None, 1)
                        if u == 0 and more:
                            between[6] = lambda: pair_row(j, i + 1)
                        sum_tile(j, i, u, between)
                        if has:
                            next_h(j, *b)
                pairs(pe, body)
                if j not in FINAL:
                    for r in range(2):
                        transposes(tg(j) + NT - 1, 1, ky(j), y_ready(j, PAIRS - 1, 1), r)
                    next_h(j, PAIRS - 1, 1)


_INS = ["x", "src", "dst",
        "L0_gnn_W1", "L0_gnn_att_src1", "L0_gnn_att_dst1", "L0_gnn_b1", "L0_gnn_W2", "L0_gnn_att_src2", "L0_gnn_att_dst2", "L0_gnn_b2",
        "L1_gnn_W1", "L1_gnn_a1_src", "L1_gnn_a1_dst", "L1_gnn_b1", "L1_gnn_W2", "L1_gnn_a2_src", "L1_gnn_a2_dst", "L1_gnn_b2"]


def kernel(**inputs):
    import numpy as np
    import concourse.bacc as bacc
    from concourse import mybir as mb
    from concourse.bass_utils import run_bass_kernel_spmd as run

    nc = bacc.Bacc("TRN2", target_bir_lowering=False, num_devices=1)
    arrays, args = {}, []
    for name in _INS:
        a = np.ascontiguousarray(inputs[name])
        arrays["in_" + name] = a
        args.append(nc.dram_tensor("in_" + name, a.shape, mb.dt.from_np(a.dtype), kind="ExternalInput").ap())
    args.append(nc.dram_tensor("out_0", (N, D), mb.dt.float32, kind="ExternalOutput").ap())
    gnn(nc, *args)
    r = run(nc, [arrays], core_ids=[0])
    return r.results[0]["out_0"]
```

```python
import concourse.bass as bass
from concourse import mybir
from contextlib import ExitStack

N, E, D, HEADS, HID = 1250, 20000, 768, 4, 512
T = 125
NT = N // T
PAIRS = NT // 2
KD = D // 128
KH = HID // 128
HALF = D // 2
CP = 2 * T
CH = 4
EC = CH * T
NS = E // EC
NEG = -3.0e38
SLOPE = 0.2
EPS = 1e-5
AC = 2 * HEADS
HW0, HW1 = D + 2, HID + 2
NATT = 3 + HEADS
LAST = NATT - 1


def gnn(nc, x, src, dst, W1a, s1a, d1a, b1a, W2a, s2a, d2a, b2a, W1b, s1b, d1b, b1b, W2b, s2b, d2b, b2b, out):
    f32, f32r, bf16, f16 = mybir.dt.float32, mybir.dt.float32r, mybir.dt.bfloat16, mybir.dt.float16
    i32, u16 = mybir.dt.int32, mybir.dt.uint16
    ALU, ACT, AX = mybir.AluOpType, mybir.ActivationFunctionType, mybir.AxisListType
    ctx = ExitStack()
    with ctx:
        def sb(name, shape, dt):
            return ctx.enter_context(nc.sbuf_tensor(name, shape, dt))

        def sem(name):
            return ctx.enter_context(nc.semaphore(name))

        def pair(name):
            return [sem(name + "0"), sem(name + "1")]

        mask_dram = nc.dram_tensor("mask_dram", (N, N), bf16).ap()
        h2_dram = nc.dram_tensor("h2_dram", (N, D), f32).ap()
        x1_dram = nc.dram_tensor("x1_dram", (N, D), f32).ap()

        CT = sb("CT", [128, NT * N], u16)
        mask = sb("mask", [128, 2, N], bf16)
        tr_hi = sb("tr_hi", [128, 2, KD, T], f32r)
        tr_lo = sb("tr_lo", [128, 2, KD, T], f32r)
        nat = sb("nat", [128, 2, D], f32)
        hb = sb("hb", [128, 2 * NT * HW0], f32r)
        ring = sb("ring", [128, 2, D], f32)
        P = sb("P", [128, NT, CP], f32)
        p_hi = sb("p_hi", [128, 2, NT, T], f32r)
        p_lo = sb("p_lo", [128, 2, NT, T], f32r)
        prow = sb("prow", [128, 2, CP], f32)
        arow = sb("arow", [128, N], f32)
        attv = sb("attv", [128, 2, D], f32)
        wb = sb("wb", [128, 2 * KD * (HID + AC) + KH * (D + 2)], f32r)
        stage = sb("stage", [128, 2, D], f32)
        junk = sb("junk", [128, D], f32)
        brow = sb("brow", [128, D], f32)
        ident = sb("ident", [128, 128], f32)
        ones = sb("ones", [128, T], f32)
        wc_raw = sb("wc_raw", [128, KD * (2 + AC)], f32)
        acol = sb("acol", [128, 3, NT, 2 * HEADS], f32)
        mtile = sb("mtile", [128, 2], f32)
        started = sb("started", [128, 4], f32)
        wct = sb("wct", [128, 2], f32)
        M = sb("M", [128, NT], f32)
        asc = sb("asc", [128, 2, NT], f32)
        pc = sb("pc", [128, 4, 2], f32)
        col = sb("col", [128, 2, 6], f32)
        rstd = sb("rstd", [128, 2, 2], f32)
        expo = sb("expo", [128, 1], f32)
        tab = sb("tab", [1, 3 * NT], i32)

        h0_hi = hb[:, 0:NT * HW0].rearrange("p (s f) -> p s f", f=HW0)
        h0_lo = hb[:, NT * HW0:2 * NT * HW0].rearrange("p (s f) -> p s f", f=HW0)
        h1_hi = hb[:, 0:NT * HW1].rearrange("p (s f) -> p s f", f=HW1)
        h1_lo = hb[:, NT * HW1:2 * NT * HW1].rearrange("p (s f) -> p s f", f=HW1)
        TAIL = 2 * NT * HW1
        WA, WB, WC = KD * (D + 2), KD * (HID + AC), KH * (D + 2)
        w0_hi = wb[:, 0:WA].rearrange("p (k f) -> p k f", f=D + 2)
        w0_lo = wb[:, WA:2 * WA].rearrange("p (k f) -> p k f", f=D + 2)
        w1_hi = wb[:, 0:WB].rearrange("p (k f) -> p k f", f=HID + AC)
        w1_lo = wb[:, WB:2 * WB].rearrange("p (k f) -> p k f", f=HID + AC)
        w2_hi = wb[:, 2 * WB:2 * WB + WC].rearrange("p (k f) -> p k f", f=D + 2)
        w2_lo = hb[:, TAIL:TAIL + WC].rearrange("p (k f) -> p k f", f=D + 2)
        CT3 = CT[:, :].rearrange("p (s d) -> p s d", d=N)
        flatP = P[:, :, :].rearrange("p s d -> p (s d)")
        iota = flatP[:, 0:625].bitcast(f16)
        flat_stage = stage[:, :, :].rearrange("p u f -> p (u f)")
        oh_src = [t.bitcast(f16) for t in (flatP[:, 625:1250], flatP[:, 1250:1875], flat_stage[:, 0:625], flat_stage[:, 625:1250],
                                           brow[:, 0:625])]
        oh_dst = [flat_stage[:, 1250 + 63 * q:1250 + 63 * (q + 1)].bitcast(f16) for q in range(CH)] + [brow[:, 625:688].bitcast(f16)]
        zeros = flatP[:, 2001:2064].bitcast(f16)
        ecol = ring[:, 0, 0:2 * CH * NS].rearrange("p (q c) -> p q c", q=2 * CH)
        edge = ring[:, 1, 0:64]
        selfcol = ring[:, 1, 64:64 + NT]
        C = [arow[:, :], attv[:, :, :].rearrange("p n f -> p (n f)")[:, 0:N]]
        CTw = CT[:, :].bitcast(i32)
        CTf = CT[:, :].bitcast(f32)
        dst_i, src_i = CTw[0:NS, 0:EC], CTw[0:NS, EC:2 * EC]
        dst_f, src_f = CTf[0:NS, 2 * EC:3 * EC], CTf[0:NS, 3 * EC:4 * EC]

        ps_o = ctx.enter_context(nc.psum_tensor("ps_o", [128, 4, 512], f32))
        ps_h2 = ctx.enter_context(nc.psum_tensor("ps_h2", [128, 2, 512], f32))
        ps_t = ctx.enter_context(nc.psum_tensor("ps_t", [128, 512], f32))
        ps_a = ctx.enter_context(nc.psum_tensor("ps_a", [128, 512], f32))
        ps_c = ps_o[:, 0:3, :].rearrange("p b f -> p (b f)")
        ps_ct = [ps_h2[:, 0, :], ps_h2[:, 1, :], ps_t[:, :]]

        s_edges, s_conv, s_const = sem("s_edges"), sem("s_conv"), sem("s_const")
        s_etr, s_ecol, s_prep, s_tabps, s_tab = sem("s_etr"), sem("s_ecol"), sem("s_prep"), sem("s_tabps"), sem("s_tab")
        s_ltr, s_iota = sem("s_ltr"), sem("s_iota")
        s_oh, s_used, s_self, s_cdone = sem("s_oh"), sem("s_used"), sem("s_self"), sem("s_cdone")
        s_cev, s_mk, s_mst, s_ctr, s_ctev = sem("s_cev"), sem("s_mk"), pair("s_mst"), sem("s_ctr"), sem("s_ctev")
        s_wst, s_att, s_whi, s_wlo, s_wcol, s_wcs, s_hcol, s_w1lo = (pair("s_wst"), sem("s_att"), sem("s_whi"), sem("s_wlo"), sem("s_wcol"),
                                                                 sem("s_wcs"), sem("s_hcol"), sem("s_w1lo"))
        s_nat, s_tr, s_thi, s_tlo, s_tuse = pair("s_nat"), sem("s_tr"), sem("s_thi"), sem("s_tlo"), sem("s_tuse")
        s_oev, s_hhi, s_ones = sem("s_oev"), sem("s_hhi"), sem("s_ones")
        s_ml, s_mx, s_mcol = pair("s_ml"), sem("s_mx"), sem("s_mcol")
        s_diag, s_row, s_rev, s_as = sem("s_diag"), sem("s_row"), sem("s_rev"), sem("s_as")
        s_pc, s_pdiag, s_prow, s_prev = sem("s_pc"), sem("s_pdiag"), sem("s_prow"), sem("s_prev")
        s_arg, s_exp, s_p, s_phi, s_plo, s_agg = sem("s_arg"), sem("s_exp"), sem("s_p"), sem("s_phi"), pair("s_plo"), sem("s_agg")
        s_phalf, s_split2 = sem("s_phalf"), sem("s_split2")
        s_b, s_den, s_rd, s_eexp, s_emin, s_y = sem("s_b"), sem("s_den"), sem("s_rd"), sem("s_eexp"), sem("s_emin"), sem("s_y")
        s_h2ev, s_hst, s_rl, s_split = sem("s_h2ev"), pair("s_hst"), pair("s_rl"), sem("s_split")
        s_back = [sem("s_back%d" % q) for q in range(6)]
        s_sum, s_mean, s_sq, s_var, s_pow, s_fin, s_xst = (sem("s_sum"), sem("s_mean"), sem("s_sq"), sem("s_var"),
                                                           sem("s_pow"), sem("s_fin"), pair("s_xst"))

        FINAL = (1, LAST)
        def head(j): return j - 2 if 2 <= j < LAST else None
        def h_phase(j): return j not in FINAL
        def hw(j): return HID if head(j) is not None else D
        def ky(j): return KH if head(j) is not None else KD
        def tb(j): return 0 if j == 0 else 2 * NT + 2 * NT * head(j)
        def tg(j): return tb(j) + NT
        def ob(j): return {0: 0, 1: 2 * NT, LAST: 3 * NT + 2 * NT * HEADS}[j] if head(j) is None else 3 * NT + 2 * NT * head(j)
        def og(j): return ob(j) + (NT if h_phase(j) else 0)
        def ahead(j): return j > 2 and j != LAST
        def hh(j): return j * NT
        def h2b(j): return 0 if j == 0 else (1 + head(j)) * NT
        AS = {j: acol[0:T, min(j, 1) if j < 2 else (1 if j < LAST else 2), :, :] for j in range(NATT)}
        AS[0], AS[1] = acol[0:T, 0, :, 0:2], acol[0:T, 0, :, 2:4]
        AS[LAST] = acol[0:T, 2, :, 0:2]
        def as_of(j): return AS[j][:, :, 0 if head(j) is None else 2 * head(j)]
        def ad_of(j): return AS[j][:, :, 1 if head(j) is None else 2 * head(j) + 1]

        events = []
        def event(key, w, n, k0, c0, width, hi=None, lo=None, att=None, raw=None, ring=True):
            prev = events[-1] if events else None
            e = dict(key=key, w=w, n=n, k0=k0, c0=c0, width=width, hi=hi, lo=lo, att=att, raw=raw, ring=ring, prev=prev,
                     first=sum(e["n"] for e in events),
                     att_first=sum(1 for e in events if e["att"]),
                     col_first=sum(2 * e["n"] for e in events if e["att"]),
                     hi_first=sum(e["n"] for e in events if e["hi"] is not None),
                     own_first=sum(e["n"] for e in events if e["att"] and e["hi"] is not None),
                     slot_first=[sum(e["n"] // 2 if e["ring"] else e["n"] * (1 - q) for e in events) for q in range(2)])
            events.append(e)
        RAW1 = 2 * KD
        def att1(g):
            event("W1b_att%d" % g, W1b, KD, 0, HID * g, HID, att=(s1b, d1b, g), raw=lambda c: RAW1 + AC * c + 2 * g)
        event("W1a", W1a, KD, 0, 0, D, w0_hi, w0_lo, (s1a, d1a, None))
        att1(1)
        event("W2a_att", W2a, KD, 0, 0, D, att=(s2a, d2a, None), raw=lambda c: 2 * c)
        att1(2)
        event("W2a", W2a, KD, 0, 0, D, w0_hi, w0_lo)
        att1(3)
        att1(0)
        for g in range(HEADS):
            event("W1b%d" % g, W1b, KD, 0, HID * g, HID, w1_hi, w1_lo)
            event("W2b%d" % g, W2b, KH, KH * g, 0, D, w2_hi, w2_lo, (s2b, d2b, 0), ring=False)
        EV = {e["key"]: e for e in events}
        def done(key): return EV[key]["first"] + EV[key]["n"]
        AT = {("H", 0): ("W1b_att1", "W2a_att", "W1b_att2"), ("G", 0): ("W2a", "W1b_att3", "W1b_att0"), ("G", 1): (None, "W1b0", None)}
        for g in range(HEADS):
            AT["H", 2 + g] = "W2b%d" % g
            if g + 1 < HEADS:
                AT["G", 2 + g] = (None, "W1b%d" % (g + 1), None)

        def weights_at(chunk, phase, j, i, u, points=(0, 1, 2), halves=False):
            at = AT.get((phase, j))
            if isinstance(at, str):
                if 1 in points and (u == 1 or halves) and not (isinstance(i, int) and i == PAIRS - 1):
                    chunk(at, i, None, *((u,) if halves else ()))
            elif at:
                if not isinstance(i, int):
                    if 1 in points:
                        chunk(at[1], i - 1, u)
                elif at[0 if i == 0 else 2]:
                    spread = (((0, 1), (2,), (3,)), ((4,), (5,), ()))
                    for c in [c for point in points for c in spread[u][point]]:
                        chunk(at[0 if i == 0 else 2], c // 2, c % 2)

        def number(ev, h, q):
            return 2 * h + q if ev["ring"] else h
        def w_free(key):
            if key == "W1a": return 0
            if key == "W2a": return NT
            if key == "W1b0": return 2 * NT
            g = int(key[3:])
            return 2 * NT + 2 * NT * g if key.startswith("W2b") else 2 * NT + 2 * NT * (g - 1) + NT
        BIAS = [b1a, b2a] + [b1b] * HEADS + [b2b]
        ROUNDS = [(0, 4), (4, 4), (8, 2)]
        NROW = len(ROUNDS)
        def rl_final(j): return 0 if j == 1 else HEADS * PAIRS
        def rl_head(j): return head(j) * PAIRS
        BACK = [stage[0:T, 0, :], stage[0:T, 1, :], attv[0:T, 0, :], attv[0:T, 1, :], nat[0:T, 0, :], nat[0:T, 1, :]]
        def back(t): return ring[0:T, t % 2, :] if t >= NT - 2 else BACK[t % len(BACK)]
        def back_loads(j, t): return (0 if j == 1 else 1 + (t % len(BACK) < NT - 2 - len(BACK))) + t // len(BACK) + 1
        EARLY = 3
        def hst(j): return 0 if j == 0 else (1 + head(j)) * PAIRS

        def pairs(eng, body, after_first=None, before_last=None):
            body(0)
            if after_first:
                after_first()
            with eng.Fori(1, PAIRS - 1, 1) as i:
                body(i)
            if before_last:
                before_last()
            body(PAIRS - 1)

        def rows(i, u): return bass.ds(i * CP + u * T, T)
        def tile_of(i, u): return bass.ds(2 * i + u, 1)

        block = ctx.enter_context(nc.Block())

        @block.sync
        def _(sp):
            sp.dma_start(dst_i, dst.rearrange("(c e) -> c e", e=EC)).then_inc(s_edges, 16)
            sp.dma_start(src_i, src.rearrange("(c e) -> c e", e=EC)).then_inc(s_edges, 16)

            def chunk(key, h, q):
                ev = EV[key]
                w, c = ev["width"], number(ev, h, q)
                if ev["att"] and isinstance(h, int) and c == 0:
                    vectors(ev)
                g = ev["first"] + c
                if not isinstance(h, int) or not ev["ring"] or (ev["prev"] and not ev["prev"]["ring"]):
                    sp.wait_ge(s_wlo, g)
                elif g >= 2:
                    sp.wait_ge(s_wlo, g - 1)
                rows_ = bass.ds(128 * (ev["k0"] + c), 128)
                sp.dma_start(stage[:, q or 0, 0:w], ev["w"][rows_, ev["c0"]:ev["c0"] + w]).then_inc(s_wst[q or 0], 16)

            def vectors(ev):
                va, vd, g = ev["att"]
                if ev["col_first"]:
                    sp.wait_ge(s_wcol, ev["col_first"])
                for n, v in enumerate((va, vd)):
                    row = v.rearrange("(a f) -> a f", a=1) if g is None else v[g:g + 1, :]
                    w = ev["width"]
                    sp.dma_start(attv[:, n, 0:w], row.broadcast_to([128, w])).then_inc(s_att, 16)

            def bias(j):
                if j:
                    sp.wait_ge(s_oev, og(j - 1) + NT)
                else:
                    sp.wait_ge(s_cdone, NT)
                w = hw(j)
                b = BIAS[j][w * head(j):w * (head(j) + 1)] if head(j) is not None else BIAS[j]
                sp.dma_start(brow[:, 0:w], b.rearrange("(a f) -> a f", a=1).broadcast_to([128, w])).then_inc(s_b, 16)

            def mask_load(j, i, u):
                if not (isinstance(i, int) and j == 0 and i == 0):
                    sp.wait_ge(s_mx, NT * j + 2 * i + u - 1)
                sp.dma_start(mask[0:T, u, :], mask_dram[rows(i, u), :]).then_inc(s_ml[u], 16)

            for c in range(KD):
                chunk("W1a", c // 2, c % 2)
            for t in range(NT):
                sp.wait_ge(s_mk, t + 1)
                sp.dma_start(mask_dram[T * t:T * (t + 1), :], mask[0:T, t % 2, :]).then_inc(s_mst[t % 2], 16)
            for u in range(2):
                sp.wait_ge(s_mst[u], 16 * PAIRS)
            sp.wait_ge(s_ctev, 3 * NT)

            def load_back(j, t):
                sp.wait_ge(s_hst[t % 2], 16 * (hst(j - 1) + t // 2 + 1))
                if t == 0:
                    sp.wait_ge(s_wlo, done("W1b_att0" if j == 1 else "W2b%d" % (HEADS - 1)))
                if t == 4:
                    sp.wait_ge(s_tr, 2 * (tg(j - 1) + NT))
                if t >= len(BACK):
                    sp.wait_ge(s_split, PAIRS * (j == LAST) + t - len(BACK) + 1)
                sp.dma_start(back(t), h2_dram[T * t:T * (t + 1), :]).then_inc(s_back[t % len(BACK)], 16)

            def vectors_before_loop(phase, j):
                at = AT.get((phase, j))
                if at and not isinstance(at, str) and at[1] and EV[at[1]]["att"]:
                    vectors(EV[at[1]])

            for j in range(NATT):
                def in_h(i):
                    for u in range(2):
                        if ahead(j):
                            mask_load(j, i, u)
                    for u in range(2):
                        weights_at(chunk, "H", j, i, u)

                def in_g(i):
                    for u in range(2):
                        if not ahead(j) and not (isinstance(i, int) and i == PAIRS - 1):
                            mask_load(j, i + 1, u)
                    for u in range(2):
                        weights_at(chunk, "G", j, i, u)

                if h_phase(j):
                    pairs(sp, in_h, lambda: vectors_before_loop("H", j))
                for u in range(2):
                    if not ahead(j):
                        mask_load(j, 0, u)
                if j in FINAL:
                    for t in range(4):
                        load_back(j, t)
                bias(j)
                if j in FINAL:
                    for t in range(4, NT - 2):
                        load_back(j, t)
                if j in FINAL:
                    sp.wait_ge(s_split2, PAIRS * (1 + (j == LAST)))
                pairs(sp, in_g, lambda: vectors_before_loop("G", j))
            for u in range(2):
                sp.wait_ge(s_hst[u], 16 * (1 + HEADS) * PAIRS)
                sp.wait_ge(s_xst[u], 16 * 2 * PAIRS)

        @block.gpsimd
        def _(pool):
            g = nc.gpsimd
            g.memset(ident[:, :], 0.0).then_inc(s_iota, 1)
            g.memset(edge[0:NT, 20:30], 1.0).then_inc(s_iota, 1)
            g.memset(ones[:, :], 1.0)
            g.memset(expo[:, :], -0.5)
            g.memset(zeros[:, :], 0.0)
            g.iota(iota[:, :], pattern=[[1, N]], base=0, channel_multiplier=0, allow_small_or_imprecise_dtypes=True)
            g.iota(selfcol[:, :], pattern=[[T, NT]], base=0, channel_multiplier=1, allow_small_or_imprecise_dtypes=True)
            g.iota(edge[:, 0:NT], pattern=[[T, NT]], base=0, channel_multiplier=0, allow_small_or_imprecise_dtypes=True)
            g.iota(edge[:, 10:11], pattern=[[1, 1]], base=-NS, channel_multiplier=1, allow_small_or_imprecise_dtypes=True)
            g.iota(edge[:, 11:12], pattern=[[1, 1]], base=1, channel_multiplier=1, allow_small_or_imprecise_dtypes=True)
            pool.wait_ge(s_iota, 2)
            g.affine_select(out=ident[:, :], in_=ident[:, :], compare_op=ALU.not_equal, fill=1.0, base=0,
                            pattern=[[-1, 128]], channel_multiplier=1)
            g.affine_select(out=edge[0:NT, 20:30], in_=edge[0:NT, 20:30], compare_op=ALU.is_gt, fill=0.0, base=0,
                            pattern=[[1, NT]], channel_multiplier=-1).then_inc(s_const, 1)

            def load_tile(srcd, j, i, u):
                t = tb(j) + 2 * i + u
                if not (j == 0 and isinstance(i, int) and i == 0):
                    if not (j == 2 and isinstance(i, int) and i == 0):
                        pool.wait_ge(s_tr, 2 * (t - 1))
                pool.dma_start(nat[0:T, u, :], srcd[rows(i, u), :]).then_inc(s_nat[u], 16)

            def p_low(j, i):
                pool.wait_ge(s_phi, NT * j + 2 * i + 2)
                g.tensor_tensor(p_lo[0:T, 1, :, :], P[0:T, :, T:CP], p_hi[0:T, 1, :, :].bitcast(f32), ALU.subtract)\
                    .then_inc(s_plo[1], 1)

            def h2_load(j, i, u):
                pool.wait_ge(s_hst[u], 16 * (hst(j) + i))
                pool.dma_start(ring[0:T, u, :], h2_dram[rows(i, u), :]).then_inc(s_rl[u], 16)

            def h2_store(j, i, u):
                pool.wait_ge(s_h2ev, h2b(j) + 2 * i + u + 1)
                pool.dma_start(h2_dram[rows(i, u), :], ring[0:T, u, :]).then_inc(s_hst[u], 16)

            for u in range(2):
                load_tile(x, 0, 0, u)
            for c in range(KD):
                pool.wait_ge(s_whi, c + 1)
                g.tensor_tensor(w0_lo[:, c, 0:D], stage[:, c % 2, 0:D], w0_hi[:, c, 0:D].bitcast(f32), ALU.subtract).then_inc(s_w1lo, 1)

            for j in range(NATT):
                f = NT * (j == LAST)
                if h_phase(j):
                    pairs(pool, lambda i: [load_tile(x if j == 0 else x1_dram, j, i, u) for u in range(2)
                                           if not (isinstance(i, int) and i == 0)])
                    more = head(j) is not None and head(j) > 0
                    if more:
                        for u in range(2):
                            h2_load(j, 0, u)

                    p_low(j, 0)

                    def step(i):
                        if not (isinstance(i, int) and i == PAIRS - 1):
                            p_low(j, i + 1)
                        for u in range(2):
                            if isinstance(i, int) and i == PAIRS - 1 and ahead(j + 1):
                                load_tile(x1_dram, j + 1, 0, u)
                            h2_store(j, i, u)
                            if more and not (isinstance(i, int) and i == PAIRS - 1):
                                h2_load(j, i + 1, u)
                    pairs(pool, step)
                else:
                    for t in range(PAIRS, NT):
                        pool.wait_ge(s_hhi, hh(j) + t + 1)
                        g.tensor_tensor(h0_lo[0:T, t, 0:D], back(t), h0_hi[0:T, t, 0:D].bitcast(f32), ALU.subtract)\
                            .then_inc(s_split2, 1)

                    def res_load(i, u):
                        if isinstance(i, int) and i == 0:
                            pool.wait_ge(s_split2, f // 2 + PAIRS)
                            pool.wait_ge(s_hst[u], 16 * (hst(j - 1) + PAIRS))
                        pool.dma_start(ring[0:T, u, :], (x if j == 1 else x1_dram)[rows(i, u), :]).then_inc(s_rl[u], 16)

                    for u in range(2):
                        res_load(0, u)
                    p_low(j, 0)

                    def finish(i):
                        for u in range(2):
                            n = f + 2 * i + u
                            pool.wait_ge(s_var, n + 1)
                            g.tensor_tensor(rstd[0:T, u, 0:1], col[0:T, u, 5:6], expo[0:T, :], ALU.pow).then_inc(s_pow, 1)
                            pool.wait_ge(s_pow, 2 * n + 1)
                            g.tensor_tensor(rstd[0:T, u, 1:2], col[0:T, u, 3:4], rstd[0:T, u, 0:1], ALU.mult).then_inc(s_pow, 1)
                            last = isinstance(i, int) and i == PAIRS - 1
                            if not last:
                                res_load(i + 1, u)
                            elif j == 1 and u == 1:
                                next_block(0)
                            if u == 0 and not last:
                                p_low(j, i + 1)
                            pool.wait_ge(s_fin, n + 1)
                            pool.dma_start((x1_dram if j == 1 else out)[rows(i, u), :], nat[0:T, u, :]).then_inc(s_xst[u], 16)

                    def next_block(u):
                        pool.wait_ge(s_xst[u], 16 * PAIRS)
                        load_tile(x1_dram, 2, 0, u)
                    pairs(pool, finish)
                    if j == 1:
                        next_block(1)

        @block.scalar
        def _(act):
            a = nc.scalar.activation

            def chunk(key, h, q):
                ev = EV[key]
                c = number(ev, h, q)
                if ev["hi"] is None:
                    return
                if isinstance(h, int) and c == 0:
                    free(key)
                act.wait_ge(s_wst[q or 0], 16 * (ev["slot_first"][q or 0] + h + 1))
                o = ev["hi"][:, c, 0:ev["width"]] if isinstance(h, int) else \
                    ev["hi"][:, bass.ds(c, 1), 0:ev["width"]].rearrange("p a f -> p (a f)")
                a(o, stage[:, q or 0, 0:ev["width"]], ACT.Copy).then_inc(s_whi, 1)

            def free(key):
                if w_free(key):
                    act.wait_ge(s_tuse, w_free(key))
                if key == "W2b0":
                    act.wait_ge(s_agg, 2 * NT)

            def free_before_loop(phase, j):
                at = AT.get((phase, j))
                if at and not isinstance(at, str) and at[1] and EV[at[1]]["hi"] is not None:
                    free(at[1])

            def transposed(t, u, K, func, rounds=(0, 1)):
                n = K // 2
                for r in rounds:
                    act.wait_ge(s_tr, 2 * t + r + 1)
                    if r == 0 and not (isinstance(t, int) and t < 2):
                        act.wait_ge(s_tuse, t - 1)
                    a(tr_hi[:, u, n * r:n * (r + 1), :], ps_t[:, 0:n * T].rearrange("p (k n) -> p k n", n=T), func)\
                        .then_inc(s_thi, 1)

            def h_tile(j, i, u):
                t = tb(j) + 2 * i + u
                w = hw(j)
                h = h0_hi if w == D else h1_hi
                act.wait_ge(s_tuse, t + 1)
                if w == D:
                    o = h[0:T, tile_of(i, u), 0:D].rearrange("p a (b f) -> p (a b) f", b=2)
                    a(o, ps_o[0:T, 2 * u:2 * u + 2, 0:HALF], ACT.Copy).then_inc(s_hhi, 1)
                else:
                    o = h[0:T, tile_of(i, u), 0:w].rearrange("p a (b f) -> p (a b) f", b=2)
                    a(o, ps_o[0:T, 2 * u:2 * u + 2, 0:w // 2], ACT.Copy).then_inc(s_hhi, 1)

            def row(j, k):
                rr = NROW * j + k
                t0, n = ROUNDS[k]
                act.wait_ge(s_row, rr + 1)
                a(arow[0:T, T * t0:T * (t0 + n)], ps_h2[0:T, rr % 2, 0:T * n], ACT.Copy).then_inc(s_rev, 1)

            def pair_row(j, i):
                act.wait_ge(s_prow, PAIRS * j + i + 1)
                if not (isinstance(i, int) and i == 0 and j == 0):
                    act.wait_ge(s_arg, NT * (PAIRS * j + i))
                a(prow[0:T, :, :], ps_a[0:T, 0:2 * CP].rearrange("p (a c) -> p a c", a=2), ACT.Copy).then_inc(s_prev, 1)

            def exps(j, i, half):
                for s in range(PAIRS * half, PAIRS * (half + 1)):
                    act.wait_ge(s_arg, NT * (PAIRS * j + i) + s + 1)
                    a(P[0:T, s, :], P[0:T, s, :], ACT.Exp, bias=asc[0:T, 1, s:s + 1]).then_inc(s_exp, 1)

            def p_high(j, i, u):
                p = NT * j + 2 * i + u
                first = isinstance(i, int) and i == 0
                if u == 0 and first:
                    act.wait_ge(s_p, NT * PAIRS * j + PAIRS)
                    if j:
                        act.wait_ge(s_agg, p - 1)
                    a(p_hi[0:T, u, 0:PAIRS, :], P[0:T, 0:PAIRS, 0:T], ACT.Copy).then_inc(s_phalf, 1)
                s0 = PAIRS if u == 0 and first else 0
                act.wait_ge(s_p, NT * (PAIRS * j + i + 1))
                if not (first and j == 0):
                    act.wait_ge(s_agg, p - 1)
                a(p_hi[0:T, u, s0:NT, :], P[0:T, s0:NT, T * u:T * (u + 1)], ACT.Copy).then_inc(s_phi, 1)

            def split_high(j, tiles):
                for t in tiles:
                    if t == 0:
                        act.wait_ge(s_agg, NT * j)
                    if t < NT - 2:
                        act.wait_ge(s_back[t % len(BACK)], 16 * back_loads(j, t))
                    else:
                        act.wait_ge(s_h2ev, h2b(j - 1) + t + 1)
                    a(h0_hi[0:T, t, 0:D], back(t), ACT.Copy).then_inc(s_hhi, 1)

            def normalised(j, i, u):
                f = NT * (j == LAST) + 2 * i + u
                act.wait_ge(s_pow, 2 * f + 2)
                a(nat[0:T, u, :], nat[0:T, u, :], ACT.Identity, scale=rstd[0:T, u, 0:1], bias=rstd[0:T, u, 1:2]).then_inc(s_fin, 1)

            def evac(j, i, u):
                n = NT * j + 2 * i + u
                if j in FINAL:
                    f = NT * (j == LAST) + 2 * i + u
                    act.wait_ge(s_mean, f + 1)
                    a(junk[0:T, :], nat[0:T, u, :], ACT.Square, bias=col[0:T, u, 3:4], accum_out=col[0:T, u, 4:5])\
                        .then_inc(s_sq, 1)
                elif head(j) is not None:
                    act.wait_ge(s_oev, og(j) + 2 * i + u + 1)
                    a(junk[0:T, 0:HID], nat[0:T, u, 0:HID], ACT.Exp).then_inc(s_eexp, 1)

            def aggregate(j):
                if not ahead(j):
                    pair_row(j, 0)
                    exps(j, 0, 0)
                    exps(j, 0, 1)
                p_high(j, 0, 0)
                p_high(j, 0, 1)
                func = ACT.Relu if j == 0 else ACT.Copy

                def body(i):
                    peeled = isinstance(i, int)
                    more = not (peeled and i == PAIRS - 1)
                    for u, before in ((0, (i - 1, 1)), (1, (i, 0))):
                        has = not (peeled and i == 0 and u == 0)
                        tt = tg(j) + 2 * before[0] + before[1] if j not in FINAL and has else None
                        if j in FINAL:
                            if not (peeled and i == 0):
                                normalised(j, i - 1, u)
                            if u == 0 and more:
                                pair_row(j, i + 1)
                            if has:
                                evac(j, *before)
                            if more:
                                exps(j, i + 1, u)
                            if u == 1 and more:
                                p_high(j, i + 1, 0)
                                p_high(j, i + 1, 1)
                            weights_at(chunk, "G", j, i, u)
                            continue
                        if has:
                            evac(j, *before)
                        if j == 0 and peeled and i == 0:
                            weights_at(chunk, "G", j, i, u)
                        if tt is not None:
                            transposed(tt, before[1], ky(j), func, (0,))
                        if u == 1 and more:
                            exps(j, i + 1, 1)
                        if u == 0 and more:
                            pair_row(j, i + 1)
                        if tt is not None:
                            transposed(tt, before[1], ky(j), func, (1,))
                        if not (j == 0 and peeled and i == 0):
                            weights_at(chunk, "G", j, i, u)
                        if u == 0 and more:
                            exps(j, i + 1, 0)
                        if u == 1 and more:
                            p_high(j, i + 1, 0)
                            p_high(j, i + 1, 1)
                pairs(act, body, lambda: free_before_loop("G", j))
                if j in FINAL:
                    normalised(j, PAIRS - 1, 0)
                evac(j, PAIRS - 1, 1)
                if j in FINAL:
                    normalised(j, PAIRS - 1, 1)
                if j not in FINAL:
                    transposed(tg(j) + NT - 1, 1, ky(j), func)

            def counts_out(t):
                for r, (t0, n) in enumerate(ROUNDS):
                    rr = 3 * t + r
                    act.wait_ge(s_ctr, rr + 1)
                    a(CT3[0:T, t0:t0 + n, T * t:T * (t + 1)],
                      ps_ct[r][0:T, 0:n * T].rearrange("p (n c) -> p n c", c=T), ACT.Copy).then_inc(s_ctev, 1)

            for c in range(KD):
                chunk("W1a", c // 2, c % 2)
            for t in range(NT):
                if t >= 2:
                    act.wait_ge(s_mk, t - 1)
                act.wait_ge(s_cdone, t + 1)
                a(C[t % 2][0:T, :], ps_c[0:T, 0:N], ACT.Copy).then_inc(s_cev, 1)
                if t:
                    counts_out(t - 1)
            counts_out(NT - 1)
            for j in range(NATT):
                if h_phase(j):
                    for r in range(2):
                        transposed(tb(j), 0, KD, ACT.Copy, (r,))
                        if ahead(j):
                            row(j, r)
                    if ahead(j):
                        row(j, 2)

                    def body(i):
                        for u in range(2):
                            if not (isinstance(i, int) and i == PAIRS - 1 and u == 1):
                                transposed(tb(j) + 2 * i + u + 1, 1 - u, KD, ACT.Copy, (0,))
                                if ahead(j) and isinstance(i, int) and i == PAIRS - 1:
                                    pair_row(j, 0)
                                transposed(tb(j) + 2 * i + u + 1, 1 - u, KD, ACT.Copy, (1,))
                            weights_at(chunk, "H", j, i, u)
                            if ahead(j) and isinstance(i, int) and i == PAIRS - 1:
                                if u == 0:
                                    h_tile(j, i, u)
                                    exps(j, 0, 0)
                                else:
                                    exps(j, 0, 1)
                                    h_tile(j, i, u)
                            else:
                                h_tile(j, i, u)
                                if not ahead(j) and isinstance(i, int) and i == PAIRS - 1 and u == 1:
                                    row(j, 0)
                    pairs(act, body)
                    if not ahead(j):
                        row(j, 1)
                        row(j, 2)
                else:
                    split_high(j, range(EARLY))
                    for k in range(3):
                        row(j, k)
                    split_high(j, range(EARLY, NT))
                aggregate(j)

        @block.vector
        def _(dve):
            v = nc.vector

            def chunk(key, h, q, half=None):
                ev = EV[key]
                w, c, u = ev["width"], number(ev, h, q), q or 0
                g = ev["first"] + c
                at = (lambda t, a, b: t[:, c, a:b]) if isinstance(h, int) else \
                     (lambda t, a, b: t[:, bass.ds(c, 1), a:b].rearrange("p a f -> p (a f)"))
                if ev["att"] and half != 1:
                    dve.wait_ge(s_att, 32 * (ev["att_first"] + 1))
                    for n in range(2):
                        m = ev["col_first"] + 2 * c + n
                        if n == 0:
                            dve.wait_ge(s_wst[u], 16 * (ev["slot_first"][u] + h + 1))
                            if not (isinstance(g, int) and g == 0):
                                dve.wait_ge(s_wlo, g)
                        if not (isinstance(m, int) and m == 0):
                            dve.wait_ge(s_wcol, m)
                        v.memset(started[:, 2 + n:3 + n], 0.0)
                        v.tensor_tensor_reduce(out=junk[:, 0:w], in0=stage[:, u, 0:w], in1=attv[:, n, 0:w], scale=1.0, scalar=0.0,
                                               op0=ALU.mult, op1=ALU.add, accum_out=wct[:, n:n + 1]).then_inc(s_wcol, 1)
                if half == 0:
                    return
                if ev["hi"] is not None and key != "W1a":
                    dve.wait_ge(s_whi, ev["hi_first"] + c + 1)
                    ins = v.tensor_tensor(at(ev["lo"], 0, w), stage[:, u, 0:w], at(ev["hi"], 0, w).bitcast(f32), ALU.subtract)
                if ev["att"]:
                    dve.wait_ge(s_wcol, ev["col_first"] + 2 * c + 2)
                    if ev["hi"] is None:
                        to = ev["raw"](c)
                        ins = v.tensor_copy(wc_raw[:, bass.ds(to, 2)], wct[:, :])
                    else:
                        if key == "W1a":
                            dve.wait_ge(s_w1lo, c + 1)
                        v.tensor_copy(at(ev["hi"], w, w + 2), wct[:, :]).then_inc(s_wcs, 1)
                        dve.wait_ge(s_wcs, ev["own_first"] + c + 1)
                        ins = v.tensor_tensor(at(ev["lo"], w, w + 2), wct[:, :], at(ev["hi"], w, w + 2).bitcast(f32), ALU.subtract)
                ins.then_inc(s_wlo, 1)

            def columns(hi, lo, w, raw, n, last, count):
                dve.wait_ge(s_wlo, done(last))
                r = wc_raw[:, raw:raw + KD * n].rearrange("p (k c) -> p k c", c=n)
                v.tensor_copy(hi[:, :, w:w + n], r).then_inc(s_hcol, 1)
                dve.wait_ge(s_hcol, count + 1)
                v.tensor_tensor(lo[:, :, w:w + n], r, hi[:, :, w:w + n].bitcast(f32), ALU.subtract).then_inc(s_hcol, 1)

            def low(t, u, K, relu, rounds=(0, 1)):
                n = K // 2
                for r in rounds:
                    dve.wait_ge(s_thi, 2 * t + r + 1)
                    o = tr_lo[:, u, n * r:n * (r + 1), :]
                    p = ps_t[:, 0:n * T].rearrange("p (k n) -> p k n", n=T)
                    h = tr_hi[:, u, n * r:n * (r + 1), :].bitcast(f32)
                    if relu:
                        v.scalar_tensor_tensor(out=o, in0=p, scalar=0.0, in1=h, op0=ALU.max, op1=ALU.subtract)\
                            .then_inc(s_tlo, 1)
                    else:
                        v.tensor_tensor(o, p, h, ALU.subtract).then_inc(s_tlo, 1)

            def h_low(j, i, u):
                w = hw(j)
                dve.wait_ge(s_hhi, hh(j) + 2 * i + u + 1)
                if w == D:
                    def v3(t): return t[0:T, tile_of(i, u), 0:D].rearrange("p a (b f) -> p (a b) f", b=2)
                    v.tensor_tensor(v3(h0_lo), ps_o[0:T, 2 * u:2 * u + 2, 0:HALF], v3(h0_hi).bitcast(f32),
                                    ALU.subtract).then_inc(s_oev, 1)
                else:
                    def v2(t): return t[0:T, tile_of(i, u), 0:w].rearrange("p a (b f) -> p (a b) f", b=2)
                    v.tensor_tensor(v2(h1_lo), ps_o[0:T, 2 * u:2 * u + 2, 0:w // 2], v2(h1_hi).bitcast(f32),
                                    ALU.subtract).then_inc(s_oev, 1)

            def a_cols(j, where, i, u):
                if where == "H":
                    to, c, p = AS[j], (2 if j == 0 else AC), ps_o[0:T, 2 * u + 1, hw(j) // 2:hw(j) // 2 + (2 if j == 0 else AC)]
                else:
                    to, c, p = AS[1 if j == 0 else LAST], 2, ps_h2[0:T, 1, HALF:HALF + 2]
                o = to[:, tile_of(i, u), 0:c].rearrange("p a c -> p (a c)")
                if where == "G" and head(j):
                    v.tensor_tensor(o, o, p, ALU.add)
                else:
                    v.tensor_copy(o, p)

            def diag(j, k):
                rr = NROW * j + k
                t0, n = ROUNDS[k]
                o = flatP[0:T, 500 * k:500 * k + n * T].rearrange("p (n c) -> p n c", c=T)
                if j and k == 0:
                    for u in range(2):
                        dve.wait_ge(s_plo[u], PAIRS * j)
                v.tensor_tensor(o, ident[0:T, 0:T].unsqueeze(1).broadcast_to([T, n, T]),
                                as_of(j)[:, t0:t0 + n].unsqueeze(2).broadcast_to([T, n, T]), ALU.mult).then_inc(s_diag, 1)

            def scaled(j):
                if j:
                    dve.wait_ge(s_arg, NT * PAIRS * j)
                    dve.wait_ge(s_exp, NT * PAIRS * j)
                v.tensor_scalar(asc[0:T, 0, :], as_of(j), 1.0 - SLOPE, None, ALU.mult)
                v.tensor_scalar(asc[0:T, 1, :], as_of(j), SLOPE, None, ALU.mult).then_inc(s_as, 1)

            def maxes(j, i, u):
                n = NT * j + 2 * i + u
                if isinstance(i, int) and i == 0 and u == 0:
                    dve.wait_ge(s_rev, NROW * (j + 1))
                dve.wait_ge(s_ml[u], 16 * (PAIRS * j + i + 1))
                v.memset(started[0:T, u:u + 1], 0.0)
                v.tensor_tensor_reduce(out=mask[0:T, u, :], in0=arow[0:T, :], in1=mask[0:T, u, :],
                                       scale=1.0, scalar=NEG, op0=ALU.add, op1=ALU.max,
                                       accum_out=mtile[0:T, u:u + 1]).then_inc(s_mx, 1)
                if ahead(j):
                    dve.wait_ge(s_mx, n + 1)
                    v.tensor_copy(M[0:T, tile_of(i, u)], mtile[0:T, u:u + 1]).then_inc(s_mcol, 1)

            def pair_cols(j, i):
                n = 4 * (PAIRS * j + i)
                two = bass.ds(2 * i, 2)
                if ahead(j):
                    dve.wait_ge(s_mcol, NT * (j - 3) + 2 * i + 2)
                    mx = M[0:T, two]
                else:
                    dve.wait_ge(s_mx, NT * j + 2 * i + 2)
                    mx = mtile[0:T, :]
                ad = ad_of(j)[:, two]
                v.tensor_tensor(pc[0:T, 0, :], ad, mx, ALU.add).then_inc(s_pc, 1)
                dve.wait_ge(s_pc, n + 1)
                v.scalar_tensor_tensor(out=pc[0:T, 1, :], in0=pc[0:T, 0, :], scalar=SLOPE, in1=pc[0:T, 0, :], op0=ALU.mult, op1=ALU.max)\
                    .then_inc(s_pc, 1)
                dve.wait_ge(s_pc, n + 2)
                v.tensor_tensor(pc[0:T, 2, :], ad, pc[0:T, 1, :], ALU.subtract).then_inc(s_pc, 1)
                v.scalar_tensor_tensor(out=pc[0:T, 3, :], in0=ad, scalar=SLOPE, in1=pc[0:T, 1, :], op0=ALU.mult, op1=ALU.subtract)\
                    .then_inc(s_pc, 1)

            def pair_diag(j, i):
                n = PAIRS * j + i
                dve.wait_ge(s_pc, 4 * n + 4)
                if isinstance(i, int) and i == 0:
                    dve.wait_ge(s_row, NROW * (j + 1))
                else:
                    for u in range(2):
                        dve.wait_ge(s_plo[u], PAIRS * j + i)
                v.tensor_tensor(flatP[0:T, 0:2 * CP].rearrange("p (n c) -> p n c", c=T),
                                ident[0:T, 0:T].unsqueeze(1).broadcast_to([T, 4, T]),
                                pc[0:T, 2:4, :].rearrange("p a c -> p (a c)").unsqueeze(2).broadcast_to([T, 4, T]), ALU.mult)\
                    .then_inc(s_pdiag, 1)

            def args(j, i, half):
                if half == 0:
                    if isinstance(i, int) and i == 0:
                        dve.wait_ge(s_as, j + 1)
                    dve.wait_ge(s_prev, PAIRS * j + i + 1)
                for s in range(PAIRS * half, PAIRS * (half + 1)):
                    v.scalar_tensor_tensor(out=P[0:T, s, :], in0=prow[0:T, 0, :], scalar=asc[0:T, 0, s:s + 1],
                                           in1=prow[0:T, 1, :], op0=ALU.add, op1=ALU.max).then_inc(s_arg, 1)

            def counts(j, i, half):
                for s in range(PAIRS * half, PAIRS * (half + 1)):
                    dve.wait_ge(s_exp, NT * (PAIRS * j + i) + s + 1)
                    v.scalar_tensor_tensor(out=P[0:T, s, :], in0=P[0:T, s, :], scalar=1.0,
                                           in1=CT3[0:T, s, bass.ds(i * CP, CP)], op0=ALU.min, op1=ALU.mult).then_inc(s_p, 1)

            def p_low(j, i):
                s0 = 0
                if isinstance(i, int) and i == 0:
                    s0 = PAIRS
                    dve.wait_ge(s_phalf, j + 1)
                    v.tensor_tensor(p_lo[0:T, 0, 0:s0, :], P[0:T, 0:s0, 0:T], p_hi[0:T, 0, 0:s0, :].bitcast(f32), ALU.subtract)
                dve.wait_ge(s_phi, NT * j + 2 * i + 1)
                v.tensor_tensor(p_lo[0:T, 0, s0:NT, :], P[0:T, s0:NT, 0:T], p_hi[0:T, 0, s0:NT, :].bitcast(f32), ALU.subtract)\
                    .then_inc(s_plo[0], 1)

            def norm(j, i, u):
                n = NT * j + 2 * i + u
                w = hw(j) // 2
                dve.wait_ge(s_agg, n + 1)
                if j >= 2:
                    v.tensor_scalar(col[0:T, u, 0:1], ps_o[0:T, 2 * u + 1, w:w + 1], 1e-16, None, ALU.add).then_inc(s_den, 1)
                    dve.wait_ge(s_den, n - 2 * NT + 1)
                    v.reciprocal(col[0:T, u, 1:2], col[0:T, u, 0:1]).then_inc(s_rd, 1)
                else:
                    v.reciprocal(col[0:T, u, 1:2], ps_o[0:T, 2 * u + 1, w:w + 1]).then_inc(s_rd, 1)
                dve.wait_ge(s_rd, n + 1)
                if isinstance(i, int) and i == 0 and u == 0:
                    dve.wait_ge(s_b, 16 * (j + 1))
                if j in FINAL and not (isinstance(i, int) and i == 0 and j == 1):
                    if not (isinstance(i, int) and i == 0):
                        dve.wait_ge(s_xst[u], 16 * (PAIRS * (j == LAST) + i))
                v3 = lambda t: t.rearrange("p (b f) -> p b f", b=2)
                v.scalar_tensor_tensor(out=v3(nat[0:T, u, 0:2 * w]), in0=ps_o[0:T, 2 * u:2 * u + 2, 0:w], scalar=col[0:T, u, 1:2],
                                       in1=v3(brow[0:T, 0:2 * w]), op0=ALU.mult, op1=ALU.add).then_inc(s_oev, 1)

            def split_low(j, tiles):
                if j in FINAL:
                    for t in tiles:
                        dve.wait_ge(s_hhi, hh(j) + t + 1)
                        v.tensor_tensor(h0_lo[0:T, t, 0:D], back(t), h0_hi[0:T, t, 0:D].bitcast(f32), ALU.subtract).then_inc(s_split, 1)

            def stage1(j, i, u):
                norm(j, i, u)
                if j in FINAL:
                    f = NT * (j == LAST) + 2 * i + u
                    dve.wait_ge(s_oev, og(j) + 2 * i + u + 1)
                    dve.wait_ge(s_rl[u], 16 * (rl_final(j) + i + 1))
                    v.scalar_tensor_tensor(out=nat[0:T, u, :], in0=nat[0:T, u, :], scalar=1.0, in1=ring[0:T, u, :],
                                           op0=ALU.mult, op1=ALU.add, accum_out=col[0:T, u, 2:3]).then_inc(s_sum, 1)
                    dve.wait_ge(s_sum, f + 1)
                    v.tensor_scalar(col[0:T, u, 3:4], col[0:T, u, 2:3], -1.0 / D, None, ALU.mult).then_inc(s_mean, 1)

            def stage2(j, i, u):
                if j in FINAL:
                    f = NT * (j == LAST) + 2 * i + u
                    dve.wait_ge(s_sq, f + 1)
                    v.tensor_scalar(col[0:T, u, 5:6], col[0:T, u, 4:5], 1.0 / D, EPS, ALU.mult, ALU.add).then_inc(s_var, 1)
                elif head(j) is not None:
                    e = NT * (j - 2) + 2 * i + u
                    dve.wait_ge(s_eexp, e + 1)
                    v.tensor_scalar(junk[0:T, 0:HID], junk[0:T, 0:HID], 1.0, -1.0, ALU.min, ALU.add).then_inc(s_emin, 1)
                    dve.wait_ge(s_emin, e + 1)
                    v.scalar_tensor_tensor(out=nat[0:T, u, 0:HID], in0=nat[0:T, u, 0:HID], scalar=0.0, in1=junk[0:T, 0:HID],
                                           op0=ALU.max, op1=ALU.add).then_inc(s_y, 1)

            def stage3(j, i, u, rounds=(0, 1)):
                if j not in FINAL:
                    low(tg(j) + 2 * i + u, u, ky(j), j == 0, rounds)

            def stage4(j, i, u):
                t = tg(j) + 2 * i + u
                dve.wait_ge(s_tuse, t + 1)
                a_cols(j, "G", i, u)
                if head(j):
                    dve.wait_ge(s_rl[u], 16 * (rl_head(j) + i + 1))
                    r3 = ring[0:T, u, :].rearrange("p (b f) -> p b f", b=2)
                    v.tensor_tensor(r3, r3, ps_h2[0:T, :, 0:HALF], ALU.add).then_inc(s_h2ev, 1)
                else:
                    if not (isinstance(i, int) and i == 0 and j == 0):
                        dve.wait_ge(s_hst[u], 16 * (hst(j) + i))
                    v.tensor_copy(ring[0:T, u, :].rearrange("p (b f) -> p b f", b=2), ps_h2[0:T, :, 0:HALF])\
                        .then_inc(s_h2ev, 1)

            def aggregate(j):
                if not ahead(j):
                    scaled(j)
                    maxes(j, 0, 0)
                    maxes(j, 0, 1)
                    pair_cols(j, 0)
                    pair_diag(j, 0)
                    split_low(j, range(EARLY, PAIRS))
                    args(j, 0, 0)
                    args(j, 0, 1)
                    counts(j, 0, 0)
                    counts(j, 0, 1)
                p_low(j, 0)

                def body(i):
                    peeled = isinstance(i, int)
                    more = not (peeled and i == PAIRS - 1)
                    for u, before, before2 in ((0, (i - 1, 1), (i - 1, 0)), (1, (i, 0), (i - 1, 1))):
                        has = not (peeled and i == 0 and u == 0)
                        if j in FINAL:
                            if u == 0 and more:
                                maxes(j, i + 1, 0)
                                maxes(j, i + 1, 1)
                                pair_cols(j, i + 1)
                                pair_diag(j, i + 1)
                            if has:
                                stage1(j, *before)
                            if more:
                                args(j, i + 1, u)
                            if has:
                                stage2(j, *before)
                            if more:
                                counts(j, i + 1, u)
                            if u == 1 and more:
                                p_low(j, i + 1)
                            weights_at(chunk, "G", j, i, u)
                            continue
                        if has:
                            stage1(j, *before)
                        if not (peeled and i == 0):
                            stage4(j, *before2)
                        if u == 0 and more and not ahead(j):
                            maxes(j, i + 1, 0)
                        if has:
                            stage2(j, *before)
                        if u == 1 and more:
                            args(j, i + 1, 1)
                        if u == 0 and more:
                            if not ahead(j):
                                maxes(j, i + 1, 1)
                            pair_cols(j, i + 1)
                            pair_diag(j, i + 1)
                            if peeled and ahead(j):
                                maxes(j, PAIRS - 1, 0)
                        weights_at(chunk, "G", j, i, u, (0,))
                        if has:
                            stage3(j, *before, (0,))
                        if u == 1 and more:
                            counts(j, i + 1, 1)
                        if has:
                            stage3(j, *before, (1,))
                        weights_at(chunk, "G", j, i, u, (1,))
                        if j == 0 and peeled and i == 0 and u == 1:
                            columns(w0_hi, w0_lo, D, 0, 2, "W2a", 0)
                        if u == 0 and more:
                            args(j, i + 1, 0)
                            counts(j, i + 1, 0)
                        if u == 1 and more:
                            p_low(j, i + 1)
                            if peeled and ahead(j):
                                maxes(j, PAIRS - 1, 1)
                        weights_at(chunk, "G", j, i, u, (2,))
                pairs(dve, body, None,
                      lambda: columns(w1_hi, w1_lo, HID, RAW1, AC, "W1b0", 2) if j == 1 else None)
                stage1(j, PAIRS - 1, 1)
                stage2(j, PAIRS - 1, 1)
                if j not in FINAL:
                    stage3(j, PAIRS - 1, 1, (0, 1) if j == 0 else (0,))
                    stage4(j, PAIRS - 1, 0)
                    if j:
                        stage3(j, PAIRS - 1, 1, (1,))
                    split_low(j + 1, range(EARLY))
                    stage4(j, PAIRS - 1, 1)

            dve.sem_inc(s_oh, CH * NS)
            dve.wait_ge(s_edges, 32)
            v.tensor_copy(dst_f, dst_i)
            v.tensor_copy(src_f, src_i).then_inc(s_conv, 1)
            dve.wait_ge(s_conv, 1)
            v.tensor_reduce(out=edge[0:NS, 12:13], in_=dst_f, axis=AX.X, op=ALU.min)
            v.tensor_reduce(out=edge[0:NS, 13:14], in_=dst_f, axis=AX.X, op=ALU.max).then_inc(s_prep, 1)
            dve.wait_ge(s_prep, 1)
            dve.wait_ge(s_const, 1)
            ed = lambda a, b, p=NS: edge[0:p, a:b]
            v.tensor_scalar(ed(30, 40), ed(0, NT), ed(13, 14), None, ALU.is_le)
            v.tensor_scalar(ed(40, 50), ed(0, NT), float(T - 1), ed(12, 13), ALU.add, ALU.is_ge).then_inc(s_prep, 1)
            dve.wait_ge(s_prep, 2)
            v.tensor_tensor(ed(30, 40), ed(30, 40), ed(40, 50), ALU.mult).then_inc(s_prep, 1)
            dve.wait_ge(s_prep, 3)
            v.tensor_scalar(ed(40, 50), ed(30, 40), ed(10, 11), None, ALU.mult)
            v.tensor_scalar(ed(50, 60), ed(30, 40), ed(11, 12), None, ALU.mult).then_inc(s_prep, 1)
            dve.wait_ge(s_etr, 1)
            v.tensor_copy(ecol[0:T], ps_t[0:T, 0:2 * CH * NS].rearrange("p (q c) -> p q c", q=2 * CH)).then_inc(s_ecol, 1)
            dve.wait_ge(s_ltr, 1)
            ps_lim = ps_a
            v.tensor_reduce(out=ed(14, 15, NT), in_=ps_lim[0:NT, 0:NS], axis=AX.X, op=ALU.min)
            v.tensor_reduce(out=ed(15, 16, NT), in_=ps_lim[0:NT, NS:2 * NS], axis=AX.X, op=ALU.max).then_inc(s_prep, 1)
            dve.wait_ge(s_prep, 5)
            v.tensor_scalar(ed(14, 15, NT), ed(14, 15, NT), float(NS), float(NS - 1), ALU.add, ALU.min).then_inc(s_prep, 1)
            dve.wait_ge(s_prep, 6)
            v.scalar_tensor_tensor(out=ed(15, 16, NT), in0=ed(14, 15, NT), scalar=1.0, in1=ed(15, 16, NT), op0=ALU.add, op1=ALU.max)\
                .then_inc(s_prep, 1)
            dve.wait_ge(s_prep, 7)
            v.tensor_tensor(ed(16, 17, NT), ed(15, 16, NT), ed(14, 15, NT), ALU.subtract).then_inc(s_prep, 1)
            dve.wait_ge(s_tabps, 1)
            v.tensor_copy(edge[0:1, 20:30], ps_a[0:1, 192:192 + NT])
            v.tensor_copy(edge[0:1, 30:50], ps_a[0:1, 160:180]).then_inc(s_prep, 1)
            dve.wait_ge(s_prep, 9)
            v.tensor_copy(tab[0:1, 0:2 * NT], edge[0:1, 30:50])
            v.scalar_tensor_tensor(out=tab[0:1, 2 * NT:3 * NT], in0=edge[0:1, 20:30], scalar=float(NS), in1=edge[0:1, 30:40],
                                   op0=ALU.add, op1=ALU.subtract).then_inc(s_tab, 1)
            for c in range(KD):
                chunk("W1a", c // 2, c % 2)
            v.memset(h0_hi[0:T, :, D:D + 2].bitcast(f32), 1.0)
            v.memset(h0_lo[0:T, :, D:D + 2].bitcast(f32), 0.0).then_inc(s_ones, 1)
            dve.wait_ge(s_tab, 1)

            def from_counts(t):
                dve.wait_ge(s_cev, t + 1)
                if t >= 2:
                    dve.wait_ge(s_mst[t % 2], 16 * (t // 2))
                v.tensor_scalar(mask[0:T, t % 2, :], C[t % 2][0:T, :], 0.5, NEG, ALU.is_lt, ALU.mult).then_inc(s_mk, 1)

            dve.wait_ge(s_ecol, 1)
            for t in range(NT):
                lo = dve.value_load(tab[0:1, t:t + 1], min_val=0, max_val=NS - 1)
                hi = dve.value_load(tab[0:1, NT + t:NT + t + 1], min_val=1, max_val=NS)
                sh = dve.value_load(tab[0:1, 2 * NT + t:2 * NT + t + 1], min_val=1, max_val=NS * NT)
                with dve.Fori(lo, hi, 1) as c:
                    for q in range(CH):
                        dve.wait_ge(s_used, CH * (c + sh) + q + 1)
                        v.tensor_scalar(oh_dst[q][0:T, 0:T], iota[0:T, T * t:T * (t + 1)], ecol[0:T, q, bass.ds(c, 1)], None, ALU.is_equal)
                        v.tensor_scalar(oh_src[q][0:T, :], iota[0:T, :], ecol[0:T, CH + q, bass.ds(c, 1)], None, ALU.is_equal)\
                            .then_inc(s_oh, 1)
                if t:
                    dve.wait_ge(s_cdone, t)
                v.tensor_scalar(oh_dst[CH][0:T, 0:T], iota[0:T, T * t:T * (t + 1)], selfcol[0:T, t:t + 1], None, ALU.is_equal)
                v.tensor_scalar(oh_src[CH][0:T, :], iota[0:T, :], selfcol[0:T, t:t + 1], None, ALU.is_equal).then_inc(s_self, 1)
                if t:
                    from_counts(t - 1)
            from_counts(NT - 1)

            for j in range(NATT):
                if h_phase(j):
                    if j == 2:
                        dve.wait_ge(s_agg, 2 * NT)
                        v.memset(h1_hi[0:T, :, HID:HID + 2].bitcast(f32), 1.0)
                        v.memset(h1_lo[0:T, :, HID:HID + 2].bitcast(f32), 0.0).then_inc(s_ones, 1)

                    for r in range(2):
                        if ahead(j):
                            diag(j, r)
                        low(tb(j), 0, KD, False, (r,))
                    if ahead(j):
                        diag(j, 2)
                        scaled(j)

                    def body(i):
                        for u in range(2):
                            if ahead(j) and isinstance(i, int) and i == PAIRS - 1 and u == 0:
                                pair_cols(j, 0)
                                pair_diag(j, 0)
                            nxt = () if isinstance(i, int) and i == PAIRS - 1 and u == 1 else (0, 1)
                            low(tb(j) + 2 * i + u + 1, 1 - u, KD, False, nxt[0:1])
                            last = isinstance(i, int) and i == PAIRS - 1
                            if ahead(j) and not last:
                                maxes(j, i, u)
                            weights_at(chunk, "H", j, i, u, (0,))
                            low(tb(j) + 2 * i + u + 1, 1 - u, KD, False, nxt[1:2])
                            weights_at(chunk, "H", j, i, u, (1,), True)
                            if ahead(j):
                                if last and u == 0:
                                    args(j, 0, 0)
                                if last and u == 1:
                                    args(j, 0, 1)
                                    counts(j, 0, 0)
                                    counts(j, 0, 1)
                                h_low(j, i, u)
                            else:
                                dve.wait_ge(s_hhi, hh(j) + 2 * i + u + 1)
                                a_cols(j, "H", i, u)
                                h_low(j, i, u)
                            weights_at(chunk, "H", j, i, u, (2,))
                            if not ahead(j) and last:
                                diag(j, u)

                    pairs(dve, body)
                    if not ahead(j):
                        dve.wait_ge(s_oev, ob(j) + NT)
                        diag(j, 2)
                else:
                    dve.wait_ge(s_h2ev, h2b(j - 1) + NT)
                    for k in range(3):
                        diag(j, k)
                    if j == LAST:
                        dve.wait_ge(s_tuse, 2 * NT + 2 * NT * HEADS)
                        v.memset(h0_hi[0:T, :, D:D + 2].bitcast(f32), 1.0)
                        v.memset(h0_lo[0:T, :, D:D + 2].bitcast(f32), 0.0).then_inc(s_ones, 1)
                aggregate(j)

        @block.tensor
        def _(pe):
            mm = nc.tensor.matmul

            def transposes(t, u, K, ready, r):
                n = K // 2
                if r == 0:
                    ready()
                if not (isinstance(t, int) and t == 0 and r == 0):
                    pe.wait_ge(s_tlo, 2 * t + r)
                else:
                    pe.wait_ge(s_ctev, 3 * NT)
                for k in range(n):
                    kk = n * r + k
                    ins = nc.tensor.transpose(ps_t[:, T * k:T * (k + 1)], nat[0:T, u, 128 * kk:128 * (kk + 1)], ident[0:T, 0:T])
                ins.then_inc(s_tr, 1)

            def product(o, K, u, w_hi, w_lo, parts, between={}):
                for k in range(K):
                    for a_, b_, st, sp_ in ((tr_hi, w_hi, k == 0, False), (tr_hi, w_lo, False, False), (tr_lo, w_hi, False, k == K - 1)):
                        for b, (c0, c1) in enumerate(parts):
                            ins = mm(o[:, b, 0:c1 - c0], a_[:, u, k, :], b_[:, k, c0:c1], start=st, stop=sp_)
                    if k in between:
                        between[k]()
                    if k == K - 1:
                        ins.then_inc(s_tuse, 1)

            def sum_tile(j, i, u, between):
                p, o = NT * j + 2 * i + u, og(j) + 2 * i + u
                w = hw(j) // 2
                h_hi, h_lo = (h0_hi, h0_lo) if hw(j) == D else (h1_hi, h1_lo)
                pe.wait_ge(s_plo[u], PAIRS * j + i + 1)
                pe.wait_ge(s_oev, o - 1)
                for s in range(NT):
                    if j in FINAL and u == 0 and isinstance(i, int) and i == 0:
                        pe.wait_ge(s_split if s < PAIRS else s_split2, PAIRS * (j == LAST) + s % PAIRS + 1)
                    for a_, b_, st, sp_ in ((p_hi, h_hi, s == 0, False), (p_hi, h_lo, False, False), (p_lo, h_hi, False, s == NT - 1)):
                        for b, (c0, c1) in enumerate(((0, w), (w, 2 * w + 2))):
                            ins = mm(ps_o[0:T, 2 * u + b, 0:c1 - c0], a_[0:T, u, s, :], b_[0:T, s, c0:c1], start=st, stop=sp_)
                    if s == NT - 1:
                        ins.then_inc(s_agg, 1)
                    if s in between:
                        between[s]()

            def row(j, k):
                rr = NROW * j + k
                n = ROUNDS[k][1]
                pe.wait_ge(s_diag, rr + 1)
                if rr >= 2:
                    pe.wait_ge(s_rev, rr - 1)
                if k == 0:
                    if j == 0:
                        pe.wait_ge(s_ctev, 3 * NT)
                    else:
                        pe.wait_ge(s_h2ev, h2b(j - 1) + NT if j != 2 else NT)
                mm(ps_h2[0:T, rr % 2, 0:n * T], ones[0:T, :], flatP[0:T, 500 * k:500 * k + n * T],
                   start=True, stop=True).then_inc(s_row, 1)

            def pair_row(j, i):
                n = PAIRS * j + i
                pe.wait_ge(s_pdiag, n + 1)
                if not (isinstance(i, int) and i == 0 and j == 0):
                    pe.wait_ge(s_prev, n)
                mm(ps_a[0:T, 0:2 * CP], ones[0:T, :], flatP[0:T, 0:2 * CP], start=True, stop=True).then_inc(s_prow, 1)

            def y_ready(j, i, u):
                def f():
                    if head(j) is None:
                        pe.wait_ge(s_oev, og(j) + 2 * i + u + 1)
                    else:
                        pe.wait_ge(s_y, NT * head(j) + 2 * i + u + 1)
                return f

            def next_h(j, i, u, between={}):
                t = tg(j) + 2 * i + u
                pe.wait_ge(s_tlo, 2 * t + 2)
                if isinstance(i, int) and i == 0 and u == 0:
                    pe.wait_ge(s_wlo, done("W2a" if j == 0 else "W2b%d" % head(j)))
                    if j == 0:
                        pe.wait_ge(s_hcol, 2)
                    pe.wait_ge(s_rev, NROW * (j + 1))
                n = h2b(j) + 2 * i + u
                if not (isinstance(i, int) and i == 0 and u == 0 and j == 0):
                    pe.wait_ge(s_h2ev, n)
                hi, lo = (w0_hi, w0_lo) if j == 0 else (w2_hi, w2_lo)
                product(ps_h2[0:T], ky(j), u, hi, lo, ((0, HALF), (HALF, D + 2)), between)

            pe.sem_inc(s_used, CH * NS + CH)
            pe.wait_ge(s_const, 1)
            pe.wait_ge(s_conv, 1)
            for q in range(2 * CH):
                ins = nc.tensor.transpose(ps_t[0:T, NS * q:NS * (q + 1)], (dst_f, src_f)[q // CH][:, T * (q % CH):T * (q % CH + 1)],
                                          ident[0:NS, 0:NS])
            ins.then_inc(s_etr, 1)
            pe.wait_ge(s_prep, 4)
            nc.tensor.transpose(ps_a[0:NT, 0:NS], edge[0:NS, 40:50], ident[0:NS, 0:NS])
            nc.tensor.transpose(ps_a[0:NT, NS:2 * NS], edge[0:NS, 50:60], ident[0:NS, 0:NS]).then_inc(s_ltr, 1)
            pe.wait_ge(s_prep, 8)
            mm(ps_a[0:1, 160:170], edge[0:NT, 14:15], ident[0:NT, 0:NT], start=True, stop=True)
            mm(ps_a[0:1, 170:180], edge[0:NT, 15:16], ident[0:NT, 0:NT], start=True, stop=True)
            mm(ps_a[0:1, 192:202], edge[0:NT, 16:17], edge[0:NT, 20:30], start=True, stop=True).then_inc(s_tabps, 1)
            pe.wait_ge(s_tab, 1)

            BANKS = ((0, 512), (512, 1024), (1024, N))

            def transpose_counts(t):
                pe.wait_ge(s_cev, t + 1)
                for r, (t0, n) in enumerate(ROUNDS):
                    if t:
                        pe.wait_ge(s_ctev, 3 * t + r - 2)
                    for q in range(n):
                        ins = nc.tensor.transpose(ps_ct[r][0:T, T * q:T * (q + 1)], C[t % 2][0:T, T * (t0 + q):T * (t0 + q + 1)],
                                                  ident[0:T, 0:T])
                    ins.then_inc(s_ctr, 1)

            for t in range(NT):
                lo = pe.value_load(tab[0:1, t:t + 1], min_val=0, max_val=NS - 1)
                hi = pe.value_load(tab[0:1, NT + t:NT + t + 1], min_val=1, max_val=NS)
                sh = pe.value_load(tab[0:1, 2 * NT + t:2 * NT + t + 1], min_val=1, max_val=NS * NT)
                if t:
                    pe.wait_ge(s_cev, t)
                for b, (c0, c1) in enumerate(BANKS):
                    mm(ps_o[0:T, b, 0:c1 - c0], zeros[0:T, 0:T], iota[0:T, c0:c1], start=True, stop=False)
                with pe.Fori(lo, hi, 1) as c:
                    for q in range(CH):
                        pe.wait_ge(s_oh, CH * (c + sh) + q + 1)
                        for b, (c0, c1) in enumerate(BANKS):
                            ins = mm(ps_o[0:T, b, 0:c1 - c0], oh_dst[q][0:T, 0:T], oh_src[q][0:T, c0:c1], start=False, stop=False)
                        ins.then_inc(s_used, 1)
                pe.wait_ge(s_self, t + 1)
                for b, (c0, c1) in enumerate(BANKS):
                    ins = mm(ps_o[0:T, b, 0:c1 - c0], oh_dst[CH][0:T, 0:T], oh_src[CH][0:T, c0:c1], start=False, stop=True)
                ins.then_inc(s_cdone, 1)
                if t:
                    transpose_counts(t - 1)
            transpose_counts(NT - 1)
            pe.wait_ge(s_ecol, 1)

            for j in range(NATT):
                if h_phase(j):
                    hi, lo = (w0_hi, w0_lo) if j == 0 else (w1_hi, w1_lo)
                    w = hw(j) // 2
                    parts = ((0, w), (w, 2 * w + {0: 2, 2: AC}.get(j, 0)))
                    n_nat = 0 if j == 0 else PAIRS * (1 + head(j))

                    def nat_ready(i, u):
                        return lambda: pe.wait_ge(s_nat[u], 16 * (n_nat + i + 1))

                    def h_tile(i, u):
                        t, o = tb(j) + 2 * i + u, ob(j) + 2 * i + u
                        first = isinstance(i, int) and i == 0
                        pe.wait_ge(s_tlo, 2 * t + 2)
                        if first and u == 0:
                            pe.wait_ge(s_wlo, done({0: "W1a"}.get(j, "W1b%d" % (head(j) or 0))))
                            if j == 0:
                                pe.wait_ge(s_cev, NT)
                            else:
                                pe.wait_ge(s_hcol, 4)
                        if not (j == 0 and first):
                            pe.wait_ge(s_oev, o - 1)
                        between = {}
                        if not (isinstance(i, int) and i == PAIRS - 1 and u == 1):
                            nxt = (i, 1) if u == 0 else (i + 1, 0)
                            between = {0: lambda: transposes(t + 1, 1 - u, KD, nat_ready(*nxt), 0),
                                       3: lambda: transposes(t + 1, 1 - u, KD, None, 1)}
                        if ahead(j) and isinstance(i, int) and i == PAIRS - 1 and u == 0:
                            between[2] = lambda: pair_row(j, 0)
                        if not ahead(j) and isinstance(i, int) and i == PAIRS - 1 and u == 1:
                            between[4] = lambda: row(j, 0)
                        product(ps_o[0:T, 2 * u:2 * u + 2], KD, u, hi, lo, parts, between)

                    for r in range(2):
                        transposes(tb(j), 0, KD, nat_ready(0, 0), r)
                        if ahead(j):
                            row(j, r)
                    if ahead(j):
                        row(j, 2)

                    def body(i):
                        h_tile(i, 0)
                        h_tile(i, 1)
                    if ahead(j):
                        pairs(pe, body)
                    else:
                        pairs(pe, body)
                        row(j, 1)
                        row(j, 2)
                        pair_row(j, 0)
                    pe.wait_ge(s_oev, ob(j) + NT)
                else:
                    for k in range(3):
                        row(j, k)
                    pair_row(j, 0)
                pe.wait_ge(s_ones, {0: 1, 1: 1, LAST: 3}.get(j, 2))

                def body(i):
                    peeled = isinstance(i, int)
                    more = not (peeled and i == PAIRS - 1)
                    for u, b in ((0, (i - 1, 1)), (1, (i, 0))):
                        has = j not in FINAL and not (peeled and i == 0 and u == 0)
                        between = {}
                        if has:
                            tt = tg(j) + 2 * b[0] + b[1]
                            between[4] = lambda: transposes(tt, b[1], ky(j), y_ready(j, *b), 0)
                            between[8 if j == 0 else 7] = lambda: transposes(tt, b[1], ky(j), None, 1)
                        if u == 0 and more:
                            between[5 if j in FINAL else 6] = lambda: pair_row(j, i + 1)
                        sum_tile(j, i, u, between)
                        if has and not (peeled and i == PAIRS - 1 and u == 1):
                            next_h(j, *b)
                pairs(pe, body)
                if j not in FINAL:
                    def last_tile(r):
                        return lambda: transposes(tg(j) + NT - 1, 1, ky(j), y_ready(j, PAIRS - 1, 1), r)
                    next_h(j, PAIRS - 1, 0, {1 if j == 0 else 2: last_tile(0), 3: last_tile(1)})
                    next_h(j, PAIRS - 1, 1)


_INS = ["x", "src", "dst",
        "L0_gnn_W1", "L0_gnn_att_src1", "L0_gnn_att_dst1", "L0_gnn_b1", "L0_gnn_W2", "L0_gnn_att_src2", "L0_gnn_att_dst2", "L0_gnn_b2",
        "L1_gnn_W1", "L1_gnn_a1_src", "L1_gnn_a1_dst", "L1_gnn_b1", "L1_gnn_W2", "L1_gnn_a2_src", "L1_gnn_a2_dst", "L1_gnn_b2"]


def kernel(**inputs):
    import numpy as np
    import concourse.bacc as bacc
    from concourse import mybir as mb
    from concourse.bass_utils import run_bass_kernel_spmd as run

    nc = bacc.Bacc("TRN2", target_bir_lowering=False, num_devices=1)
    arrays, args = {}, []
    for name in _INS:
        a = np.ascontiguousarray(inputs[name])
        arrays["in_" + name] = a
        args.append(nc.dram_tensor("in_" + name, a.shape, mb.dt.from_np(a.dtype), kind="ExternalInput").ap())
    args.append(nc.dram_tensor("out_0", (N, D), mb.dt.float32, kind="ExternalOutput").ap())
    gnn(nc, *args)
    r = run(nc, [arrays], core_ids=[0])
    return r.results[0]["out_0"]
```
